# Optimizing a Trainium2 kernel written in Bass

```python
import numpy as np
import jax
import jax.numpy as jnp

def _softmax(x, axis=-1):
    return jax.nn.softmax(x, axis=axis)

def _gelu(x):
    return jax.nn.gelu(x, approximate=True)

def _silu(x):
    return jax.nn.silu(x)

def _sigmoid(x):
    return jax.nn.sigmoid(x)

def _layernorm(x, axis=-1, eps=1e-05):
    m = jnp.mean(x, axis=axis, keepdims=True)
    v = jnp.var(x, axis=axis, keepdims=True)
    return (x - m) / jnp.sqrt(v + eps)

def _scatter_add(tgt, idx, src, axis=0):
    return tgt.at[idx].add(src)

def _segment_sum(src, seg, n):
    return jax.ops.segment_sum(src, seg, n)
kernel_name = 'mk_macaron_d1_jaxref_r4_6227c6'

def setup_inputs(seed: int=0):
    np.random.seed(seed)
    _w = jnp.asarray

    def _L0_attn_setup():
        import jax, jax.numpy as jnp
        import numpy as np
        LAMBDA_0 = 1.0
        EPS = 1e-06
        key = jax.random.key(seed)
        ks = jax.random.split(key, 5)
        B, T, D, H = (4, 512, 256, 128)
        x = jax.random.normal(ks[0], (B, T, D), dtype=jnp.float32)
        Wq = jax.random.normal(ks[1], (H, D), dtype=jnp.float32) * D ** (-0.5)
        Wk = jax.random.normal(ks[2], (H, D), dtype=jnp.float32) * D ** (-0.5)
        Wv = jax.random.normal(ks[3], (H, D), dtype=jnp.float32) * D ** (-0.5)
        Wo = jax.random.normal(ks[4], (D, H), dtype=jnp.float32) * H ** (-0.5)
        bq = jnp.zeros((H,), jnp.float32)
        bk = jnp.zeros((H,), jnp.float32)
        bv = jnp.zeros((H,), jnp.float32)
        bo = jnp.zeros((D,), jnp.float32)
        return {'x': x, 'Wq': Wq, 'bq': bq, 'Wk': Wk, 'bk': bk, 'Wv': Wv, 'bv': bv, 'Wo': Wo, 'bo': bo}
    _L0_attn_in = _L0_attn_setup()

    def _L0_ffn_setup():
        import jax, jax.numpy as jnp
        import numpy as np
        EMB = 256
        FF = 4 * EMB

        def _ternary(w):
            scale = jnp.maximum(jnp.mean(jnp.abs(w)), 1e-08)
            w_t = jnp.clip(jnp.round(w / scale), -1.0, 1.0)
            return w + jax.lax.stop_gradient(w_t - w)
        key = jax.random.key(seed)
        kx, k1, k2, kb1, kb2 = jax.random.split(key, 5)
        x = jax.random.normal(kx, (4, 512, EMB), dtype=jnp.float32)
        lim1 = 1.0 / np.sqrt(EMB)
        lim2 = 1.0 / np.sqrt(FF)
        W1 = jax.random.uniform(k1, (FF, EMB), jnp.float32, -lim1, lim1)
        b1 = jax.random.uniform(kb1, (FF,), jnp.float32, -lim1, lim1)
        W2 = jax.random.uniform(k2, (EMB, FF), jnp.float32, -lim2, lim2)
        b2 = jax.random.uniform(kb2, (EMB,), jnp.float32, -lim2, lim2)
        return {'x': x, 'W1': W1, 'b1': b1, 'W2': W2, 'b2': b2}
    _L0_ffn_in = _L0_ffn_setup()
    _d = {'L0_attn_x': _L0_attn_in['x'], 'L0_attn_Wq': _L0_attn_in['Wq'], 'L0_attn_bq': _L0_attn_in['bq'], 'L0_attn_Wk': _L0_attn_in['Wk'], 'L0_attn_bk': _L0_attn_in['bk'], 'L0_attn_Wv': _L0_attn_in['Wv'], 'L0_attn_bv': _L0_attn_in['bv'], 'L0_attn_Wo': _L0_attn_in['Wo'], 'L0_attn_bo': _L0_attn_in['bo'], 'L0_ffn_W1': _L0_ffn_in['W1'], 'L0_ffn_b1': _L0_ffn_in['b1'], 'L0_ffn_W2': _L0_ffn_in['W2'], 'L0_ffn_b2': _L0_ffn_in['b2']}
    _x0 = _d['L0_attn_x']
    _d['L0_attn_x'] = jax.random.normal(jax.random.fold_in(jax.random.key(seed), 1), (8, 1024, 256), dtype=_x0.dtype)
    del _x0
    return _d

def reference(L0_attn_x, L0_attn_Wq, L0_attn_bq, L0_attn_Wk, L0_attn_bk, L0_attn_Wv, L0_attn_bv, L0_attn_Wo, L0_attn_bo, L0_ffn_W1, L0_ffn_b1, L0_ffn_W2, L0_ffn_b2):

    def _L0_attn_ref(x, Wq, bq, Wk, bk, Wv, bv, Wo, bo):
        import jax, jax.numpy as jnp
        import numpy as np
        LAMBDA_0 = 1.0
        EPS = 1e-06
        B, T, D = x.shape
        H = Wq.shape[0]
        Q = jnp.einsum('btd,hd->bth', x, Wq) + bq
        K = jnp.einsum('btd,hd->bth', x, Wk) + bk
        V = jnp.einsum('btd,hd->bth', x, Wv) + bv
        A0 = jnp.broadcast_to(jnp.eye(H, dtype=jnp.float32) / LAMBDA_0, (B, H, H))
        M0 = jnp.zeros((B, H, H), jnp.float32)

        def step(carry, qkv):
            A, M = carry
            q, k, v = qkv
            s_t = jnp.sum(k * q, axis=-1, keepdims=True)
            u = k / (jnp.linalg.norm(k, axis=-1, keepdims=True) + EPS)
            Au = jnp.einsum('bij,bj->bi', A, u)
            denom = 1.0 + jnp.sum(u * Au, axis=-1, keepdims=True)
            A = A - jnp.einsum('bi,bj->bij', Au, Au) / denom[..., None]
            z = Au / denom
            alpha = s_t * z
            M = M + jnp.einsum('bi,bj->bij', v, alpha)
            o = jnp.einsum('bij,bj->bi', M, q)
            return ((A, M), o)
        qkv = (jnp.swapaxes(Q, 0, 1), jnp.swapaxes(K, 0, 1), jnp.swapaxes(V, 0, 1))
        _, O = jax.lax.scan(step, (A0, M0), qkv)
        O = jnp.swapaxes(O, 0, 1)
        return jnp.einsum('bth,dh->btd', O, Wo) + bo

    def _L0_ffn_ref(x, W1, b1, W2, b2):
        import jax, jax.numpy as jnp
        import numpy as np
        EMB = 256
        FF = 4 * EMB

        def _ternary(w):
            scale = jnp.maximum(jnp.mean(jnp.abs(w)), 1e-08)
            w_t = jnp.clip(jnp.round(w / scale), -1.0, 1.0)
            return w + jax.lax.stop_gradient(w_t - w)
        h = jnp.einsum('bsd,fd->bsf', x, _ternary(W1)) + b1
        h = jax.nn.gelu(h, approximate=False)
        out = jnp.einsum('bsf,df->bsd', h, _ternary(W2)) + b2
        return out
    x = L0_attn_x
    x = x + 0.5 * _L0_ffn_ref(_layernorm(x, axis=-1), L0_ffn_W1, L0_ffn_b1, L0_ffn_W2, L0_ffn_b2)
    x = x + _L0_attn_ref(_layernorm(x, axis=-1), L0_attn_Wq, L0_attn_bq, L0_attn_Wk, L0_attn_bk, L0_attn_Wv, L0_attn_bv, L0_attn_Wo, L0_attn_bo)
    x = x + 0.5 * _L0_ffn_ref(_layernorm(x, axis=-1), L0_ffn_W1, L0_ffn_b1, L0_ffn_W2, L0_ffn_b2)
    return x

_drawn_inputs = setup_inputs


def setup_inputs(seed=0):
    import zlib

    import numpy as np

    out = dict(_drawn_inputs(seed))
    spreads = {'L0_attn_bq': (0.0, 0.1),
     'L0_attn_bk': (0.0, 0.1),
     'L0_attn_bv': (0.0, 0.1),
     'L0_attn_bo': (0.0, 2.0)}
    factors = {'L0_ffn_b1': 8.0, 'L0_ffn_b2': 200.0}
    for name, (base, spread) in spreads.items():
        noise = np.random.default_rng([zlib.crc32(name.encode()), seed]).standard_normal(out[name].shape)
        drawn = base * np.exp(spread * noise) if base else spread * noise
        out[name] = jnp.asarray(drawn.astype(out[name].dtype))
    for name, factor in factors.items():
        out[name] = (out[name] * factor).astype(out[name].dtype)
    return out
```

```python
from contextlib import ExitStack

import concourse.bass as bass
from concourse import mybir

F32 = mybir.dt.float32
F16 = mybir.dt.float16
ALU = mybir.AluOpType
ACT = mybir.ActivationFunctionType
AX_X = mybir.AxisListType.X

P = 128
BATCH, T, D = 8, 1024, 256
H = 128
FF = 1024
DC = D // P
FC = FF // P
TOKENS = BATCH * T
BLOCK = 512
BT = BLOCK // P
NBLOCK = TOKENS // BLOCK
CHUNKS = T // P
NP = BATCH * CHUNKS
GROUP = 4
NG = NP // GROUP
LN_EPS = 1e-5
NORM_EPS = 1e-6
W = 32
NW = P // W


def wait(eng, sem, value):
    if not isinstance(value, int) or value > 0:
        eng.wait_ge(sem, value)


class Step:

    def __init__(self, pair, parity):
        self.pair, self.s, self.n = pair, parity, pair * 2 + parity

    def later(self, k):
        p = self.s + k
        return Step(self.pair + p // 2, p % 2)


def steps(eng, count, body):
    body(Step(0, 0))
    body(Step(0, 1))
    body(Step(1, 0))
    with eng.Fori(1, count // 2 - 1) as m:
        body(Step(m, 1))
        body(Step(m + 1, 0))
    body(Step(count // 2 - 1, 1))


def is_first(st):
    return isinstance(st.n, int) and st.n == 0


def is_last(st, count):
    return isinstance(st.n, int) and st.n == count - 1


def prepare(nc, ctx, a, c):
    def sb(name, shape, dt=F32):
        return ctx.enter_context(nc.sbuf_tensor(name, shape, dt))

    c.w1 = sb("w1_ternary", [P, DC, FF], F16)
    c.w2 = sb("w2_ternary", [P, FC, D], F16)
    c.b1 = sb("b1_columns", [P, FC])
    c.hb2 = sb("half_b2_rows", [P, D])
    c.ident = sb("ident", [P, P])
    c.ident16 = sb("ident16", [P, P], F16)
    c.causal = sb("causal", [P, P])
    c.minus_half = sb("minus_half", [P, BT])
    c.eps = sb("ln_eps", [P, BT])
    c.plus_half = sb("plus_half", [P, BT])

    with ExitStack() as own:
        def tmp(name, shape, dt=F32):
            return own.enter_context(nc.sbuf_tensor(name, shape, dt))

        def sem(name):
            return own.enter_context(nc.semaphore(name))

        raw = [tmp("w1_raw", [P, DC * FF]), tmp("w2_raw", [P, FC * D])]
        tern = [c.w1[:].rearrange("p c f -> p (c f)"), c.w2[:].rearrange("p c d -> p (c d)")]
        absw = tmp("abs_w", [P, 2, 2048])
        part = tmp("partial_sums", [P, 2, 32])
        colsum = tmp("column_sums", [P, 2])
        mean_w = tmp("mean_weights", [P, P])
        thr = tmp("thresholds", [P, 2, 2])
        above = tmp("above", [P, 2, 2048])
        below = tmp("below", [P, 2, 2048])
        b2_rows = tmp("b2_rows", [P, D])
        ps = own.enter_context(nc.psum_tensor("mean_psum", [P, 2], F32))
        w_in = [sem("prep_w1_in"), sem("prep_w2_in")]
        small_in = sem("prep_small_in")
        abs_done = sem("prep_abs_done")
        dve = sem("prep_dve_chain")
        sums_done = sem("prep_sums_done")
        mean_done = sem("prep_mean_done")
        pool = sem("prep_pool_chain")
        consts = sem("prep_mean_weights_done")

        with nc.Block() as block:
            @block.sync
            def _(sp):
                sp.dma_start(raw[0][:].rearrange("p (c f) -> p c f", c=DC),
                             a["W1T"].rearrange("(c p) f -> p c f", p=P)).then_inc(w_in[0], 16)
                sp.dma_start(raw[1][:].rearrange("p (c d) -> p c d", c=FC),
                             a["W2T"].rearrange("(c p) d -> p c d", p=P)).then_inc(w_in[1], 16)
                sp.dma_start(c.b1[:], a["b1"]).then_inc(small_in, 16)
                sp.dma_start(b2_rows[:], a["b2"].partition_broadcast(P)).then_inc(small_in, 16)
                sp.wait_ge(small_in, 32)

            @block.scalar
            def _(act):
                for i in range(2):
                    act.wait_ge(w_in[i], 16)
                    nc.scalar.activation(absw[:, i], raw[i][:], ACT.Abs).then_inc(abs_done, 1)
                act.wait_ge(small_in, 32)
                nc.scalar.mul(c.hb2[:], b2_rows[:], 0.5)

            @block.gpsimd
            def _(pool_):
                nc.gpsimd.memset(mean_w[:], 1.0 / (FF * D)).then_inc(consts, 1)
                nc.gpsimd.memset(c.ident[:], 0.0).then_inc(pool, 1)
                nc.gpsimd.memset(c.causal[:], 1.0).then_inc(pool, 1)
                nc.gpsimd.memset(c.minus_half[:], -0.5)
                nc.gpsimd.memset(c.eps[:], LN_EPS)
                nc.gpsimd.memset(c.plus_half[:], 0.5)
                pool_.wait_ge(pool, 2)
                nc.gpsimd.affine_select(out=c.ident[:], in_=c.ident[:], compare_op=ALU.not_equal, fill=1.0,
                                        base=0, pattern=[[1, P]], channel_multiplier=-1).then_inc(pool, 1)
                nc.gpsimd.affine_select(out=c.causal[:], in_=c.causal[:], compare_op=ALU.is_ge, fill=0.0,
                                        base=0, pattern=[[1, P]], channel_multiplier=-1)
                pool_.wait_ge(pool, 3)
                nc.gpsimd.tensor_copy(c.ident16[:], c.ident[:])

            @block.vector
            def _(v):
                n = [0]

                def link(ins):
                    n[0] += 1
                    ins.then_inc(dve, 1)
                    v.wait_ge(dve, n[0])

                for i in range(2):
                    v.wait_ge(abs_done, i + 1)
                    link(nc.vector.tensor_reduce(part[:, i], absw[:, i].rearrange("p (a b) -> p a b", b=64),
                                                 AX_X, ALU.add))
                    nc.vector.tensor_reduce(colsum[:, i:i + 1], part[:, i], AX_X, ALU.add).then_inc(sums_done, 1)
                v.wait_ge(mean_done, 1)
                link(nc.vector.tensor_scalar(thr[:, 0], ps[:], 1e-8, 0.5, ALU.max, ALU.mult))
                link(nc.vector.tensor_scalar(thr[:, 1], thr[:, 0], -1.0, None, ALU.mult))
                for i in range(2):
                    nc.vector.tensor_scalar(above[:, i], raw[i][:], thr[:, 0, i:i + 1], None, ALU.is_gt)
                    link(nc.vector.tensor_scalar(below[:, i], raw[i][:], thr[:, 1, i:i + 1], None, ALU.is_lt))
                for i in range(2):
                    nc.vector.tensor_tensor(tern[i], above[:, i], below[:, i], ALU.subtract)

            @block.tensor
            def _(pe):
                pe.wait_ge(consts, 1)
                pe.wait_ge(sums_done, 2)
                nc.tensor.matmul(ps[:], mean_w[:], colsum[:], start=True, stop=True).then_inc(mean_done, 1)


def feed_forward(nc, name, src, dst, c):
    x_v = src.rearrange("(n p t) d -> n p t d", p=P, t=BT)
    o_v = dst.rearrange("(n p t) d -> n p t d", p=P, t=BT)
    with ExitStack() as ctx:
        def sb(what, shape, dt=F32):
            return ctx.enter_context(nc.sbuf_tensor(f"{name}_{what}", shape, dt))

        def psum(what, shape, dt=F32):
            return ctx.enter_context(nc.psum_tensor(f"{name}_{what}", shape, dt))

        def sem(what):
            return ctx.enter_context(nc.semaphore(f"{name}_{what}"))

        x = [sb(f"x{s}", [P, BT, D]) for s in range(2)]
        bn = sb("bn", [P, BT, 6])
        gate = sb("gate", [P, 1])
        mv = sb("mean_var", [P, BT, 2])
        ve = sb("var_eps", [P, BT])
        rstd = sb("rstd", [P, BT])
        xn = sb("xn", [P, BT, D])
        xh = sb("xn_high", [P, BT, D], F16)
        xl = sb("xn_rest", [P, BT, D], F16)
        xTh = [sb(f"xT_high{s}", [P, DC, BLOCK], F16) for s in range(2)]
        xTl = [sb(f"xT_rest{s}", [P, DC, BLOCK], F16) for s in range(2)]
        hh = [sb(f"h_high{s}", [P, FC, BLOCK], F16) for s in range(2)]
        hl = [sb(f"h_rest{s}", [P, FC, BLOCK], F16) for s in range(2)]
        xb = [sb(f"x_plus_bias{s}", [P, BT, D]) for s in range(2)]
        xo = [sb(f"x_out{s}", [P, BT, D]) for s in range(2)]
        ps_t = [psum(f"ps_t{i}", [P, DC, BLOCK], F16) for i in range(2)]
        ps_h = [psum(f"ps_h{i}", [P, BLOCK]) for i in range(4)]
        ps_y = [psum(f"ps_y{i}", [P, D]) for i in range(2)]

        x_in = [sem(f"x_in{s}") for s in range(2)]
        bn_done = sem("bn_done")
        stats_done = sem("stats_done")
        ve_done = sem("ve_done")
        rstd_done = sem("rstd_done")
        xn_done = sem("xn_done")
        xh_done = sem("xh_done")
        xl_done = sem("xl_done")
        xb_done = sem("xb_done")
        tr_done = sem("tr_done")
        xT_done = sem("xT_done")
        h_done = sem("h_done")
        g_done = sem("g_done")
        hl_done = sem("hl_done")
        y_done = sem("y_done")
        xo_done = sem("xo_done")
        stored = [sem(f"stored{s}") for s in range(2)]

        with nc.Block() as block:
            @block.sync
            def _(sp):
                def load(st):
                    if not (isinstance(st.n, int) and st.n < 2):
                        wait(sp, xn_done, st.n - 1)
                        wait(sp, xb_done, st.n - 1)
                    sp.dma_start(x[st.s][:], x_v[st.n]).then_inc(x_in[st.s], 16)

                def store(st):
                    wait(sp, xo_done, BT * (st.n + 1))
                    sp.dma_start(o_v[st.n], xo[st.s][:]).then_inc(stored[st.s], 16)

                def step(st):
                    if not is_last(st, NBLOCK):
                        load(st.later(1))
                    if not is_first(st):
                        store(st.later(-1))

                load(Step(0, 0))
                steps(sp, NBLOCK, step)
                store(Step(NBLOCK // 2 - 1, 1))
                for s in range(2):
                    sp.wait_ge(stored[s], 16 * NBLOCK // 2)

            @block.vector
            def _(v):
                def stats(st):
                    v.wait_ge(x_in[st.s], 16 * (st.pair + 1))
                    for t in range(BT):
                        i = nc.vector.bn_stats(bn[:, t], x[st.s][:, t])
                    i.then_inc(bn_done, 1)
                    v.wait_ge(bn_done, st.n + 1)
                    wait(v, rstd_done, st.n)
                    nc.vector.memset(gate[:], 0.0)
                    for t in range(BT):
                        i = nc.vector.bn_aggr(mv[:, t], bn[:, t])
                    i.then_inc(stats_done, 1)

                def normalise(st):
                    v.wait_ge(rstd_done, st.n + 1)
                    wait(v, xh_done, st.n)
                    wait(v, xl_done, st.n)
                    for t in range(BT):
                        i = nc.vector.tensor_scalar(xn[:, t], x[st.s][:, t], mv[:, t, 0:1], rstd[:, t:t + 1],
                                                    ALU.subtract, ALU.mult)
                    i.then_inc(xn_done, 1)

                def rest(st, f):
                    v.wait_ge(g_done, FC * st.n + f + 1)
                    if f == 0:
                        wait(v, y_done, BT * (st.n - 1)) if not is_first(st) else None
                    nc.vector.tensor_tensor(hl[st.s][:, f], ps_h[f % 4][:], hh[st.s][:, f],
                                            ALU.subtract).then_inc(hl_done, 1)

                def copy_xT(st):
                    v.wait_ge(tr_done, st.n + 1)
                    wait(v, h_done, FC * (st.n - 1)) if not is_first(st) else None
                    nc.vector.tensor_copy(xTh[st.s][:], ps_t[0][:]).then_inc(xT_done, 1)
                    nc.vector.tensor_copy(xTl[st.s][:], ps_t[1][:]).then_inc(xT_done, 1)

                def finish(st, t):
                    v.wait_ge(y_done, BT * st.n + t + 1)
                    if t == 0:
                        v.wait_ge(xb_done, st.n + 1)
                        wait(v, stored[st.s], st.pair * 16)
                    nc.vector.scalar_tensor_tensor(out=xo[st.s][:, t], in0=ps_y[t % 2][:], scalar=0.5,
                                                   in1=xb[st.s][:, t], op0=ALU.mult, op1=ALU.add
                                                   ).then_inc(xo_done, 1)

                def step(st):
                    first, last, prev = is_first(st), is_last(st, NBLOCK), st.later(-1)
                    if not last:
                        stats(st.later(1))
                    rest(st, 0)
                    rest(st, 1)
                    if not last:
                        normalise(st.later(1))
                    rest(st, 2)
                    if not first:
                        finish(prev, 0)
                    rest(st, 3)
                    if not first:
                        finish(prev, 1)
                    rest(st, 4)
                    rest(st, 5)
                    if not first:
                        finish(prev, 2)
                    if not last:
                        copy_xT(st.later(1))
                    rest(st, 6)
                    if not first:
                        finish(prev, 3)
                    rest(st, 7)

                stats(Step(0, 0))
                normalise(Step(0, 0))
                copy_xT(Step(0, 0))
                steps(v, NBLOCK, step)
                for t in range(BT):
                    finish(Step((NBLOCK - 1) // 2, (NBLOCK - 1) % 2), t)

            @block.gpsimd
            def _(pool):
                def rsqrt(st):
                    pool.wait_ge(stats_done, st.n + 1)
                    nc.gpsimd.tensor_tensor(ve[:], mv[:, :, 1], c.eps[:], ALU.add).then_inc(ve_done, 1)
                    pool.wait_ge(ve_done, st.n + 1)
                    wait(pool, xn_done, st.n)
                    nc.gpsimd.tensor_tensor(rstd[:], ve[:], c.minus_half[:], ALU.pow).then_inc(rstd_done, 1)

                def split(st):
                    pool.wait_ge(xh_done, st.n + 1)
                    wait(pool, tr_done, st.n)
                    nc.gpsimd.tensor_tensor(xl[:], xn[:], xh[:], ALU.subtract).then_inc(xl_done, 1)

                def add_bias(st):
                    pool.wait_ge(x_in[st.s], 16 * (st.pair + 1))
                    wait(pool, xo_done, BT * (st.n - 1)) if not is_first(st) else None
                    nc.gpsimd.tensor_tensor(xb[st.s][:], x[st.s][:],
                                            c.hb2[:].unsqueeze(1).to_broadcast([P, BT, D]),
                                            ALU.add).then_inc(xb_done, 1)

                def step(st):
                    if not is_last(st, NBLOCK):
                        rsqrt(st.later(1))
                    add_bias(st)
                    if not is_last(st, NBLOCK):
                        split(st.later(1))

                rsqrt(Step(0, 0))
                split(Step(0, 0))
                steps(pool, NBLOCK, step)

            @block.scalar
            def _(act):
                def high(st):
                    act.wait_ge(xn_done, st.n + 1)
                    wait(act, tr_done, st.n)
                    nc.scalar.activation(xh[:], xn[:], ACT.Copy).then_inc(xh_done, 1)

                def gelu(st, f):
                    act.wait_ge(h_done, FC * st.n + f + 1)
                    if f == 0:
                        wait(act, y_done, BT * (st.n - 1)) if not is_first(st) else None
                    nc.scalar.activation(hh[st.s][:, f], ps_h[f % 4][:], ACT.Gelu, bias=c.b1[:, f:f + 1])
                    nc.scalar.activation(ps_h[f % 4][:], ps_h[f % 4][:], ACT.Gelu,
                                         bias=c.b1[:, f:f + 1]).then_inc(g_done, 1)

                def step(st):
                    for f in range(FC):
                        gelu(st, f)
                        if f == 2 and not is_last(st, NBLOCK):
                            high(st.later(1))

                high(Step(0, 0))
                steps(act, NBLOCK, step)

            @block.tensor
            def _(pe):
                def turn(st):
                    pe.wait_ge(xh_done, st.n + 1)
                    pe.wait_ge(xl_done, st.n + 1)
                    wait(pe, xT_done, 2 * st.n)
                    for i, part in enumerate((xh, xl)):
                        for d in range(DC):
                            for t in range(BT):
                                ins = nc.tensor.transpose(ps_t[i][:, d, t * P:(t + 1) * P],
                                                          part[:, t, d * P:(d + 1) * P], c.ident16[:])
                    ins.then_inc(tr_done, 1)

                def first_product(st, f):
                    if f == 0:
                        pe.wait_ge(xT_done, 2 * (st.n + 1))
                    if not (is_first(st) and f < 4):
                        pe.wait_ge(hl_done, FC * st.n + f - 3)
                    k = 0
                    for d in range(DC):
                        for part in (xTh, xTl):
                            ins = nc.tensor.matmul(ps_h[f % 4][:], c.w1[:, d, f * P:(f + 1) * P], part[st.s][:, d],
                                                   start=(k == 0), stop=(k == 2 * DC - 1))
                            k += 1
                    ins.then_inc(h_done, 1)

                def second_product(st, t):
                    if t == 0:
                        pe.wait_ge(hl_done, FC * (st.n + 1))
                    if not (is_first(st) and t < 2):
                        pe.wait_ge(xo_done, BT * st.n + t - 1)
                    k = 0
                    for f in range(FC):
                        for part in (hh, hl):
                            ins = nc.tensor.matmul(ps_y[t % 2][:], part[st.s][:, f, t * P:(t + 1) * P], c.w2[:, f],
                                                   start=(k == 0), stop=(k == 2 * FC - 1))
                            k += 1
                    ins.then_inc(y_done, 1)

                def step(st):
                    first, last, prev = is_first(st), is_last(st, NBLOCK), st.later(-1)
                    for f in range(FC):
                        first_product(st, f)
                        if not first and f in (2, 3, 5, 6):
                            second_product(prev, (2, 3, 5, 6).index(f))
                        if f == 5 and not last:
                            turn(st.later(1))

                turn(Step(0, 0))
                steps(pe, NBLOCK, step)
                for t in range(BT):
                    second_product(Step((NBLOCK - 1) // 2, (NBLOCK - 1) % 2), t)


def project(nc, x1, m, c, a):
    HC = CHUNKS // 2
    NSTEP = 2 * BATCH
    x_v = x1.rearrange("(n c t) d -> n t c d", c=HC, t=P)
    qT_v, uT_v, vs_v = (y.rearrange("(c b) i j -> b i c j", b=BATCH) for y in (m.qT, m.uT, m.vs))
    with ExitStack() as ctx:
        def sb(what, shape, dt=F32):
            return ctx.enter_context(nc.sbuf_tensor(f"proj_{what}", shape, dt))

        def psum(what, shape, dt=F32):
            return ctx.enter_context(nc.psum_tensor(f"proj_{what}", shape, dt))

        def sem(what):
            return ctx.enter_context(nc.semaphore(f"proj_{what}"))

        w = sb("wqkv", [P, DC, 3 * H])
        bias = sb("bqkv", [P, 3 * H])
        x = [sb(f"x{s}", [P, HC, D]) for s in range(2)]
        bn = sb("bn", [P, HC, 6])
        gate = sb("gate", [P, 1])
        mv = sb("mean_var", [P, HC, 2])
        ve = sb("var_eps", [P, HC])
        rstd = sb("rstd", [P, HC])
        xn = sb("xn", [P, HC, D])
        aT = sb("aT", [P, HC, DC, P])
        qkv = [sb(f"qkv{s}", [P, HC, 3 * H]) for s in range(2)]
        junk = sb("junk", [P, HC, H])
        junk_v = sb("junk_v", [P, HC, H])
        ksq = sb("k_squared", [P, HC])
        kq = sb("k_dot_q", [P, HC])
        norm = sb("k_norm", [P, HC])
        norm_eps = sb("k_norm_eps", [P, HC])
        rnorm = sb("k_norm_inverse", [P, HC])
        u = [sb(f"u{s}", [P, HC, H]) for s in range(2)]
        vs = [sb(f"v_scaled{s}", [P, HC, H]) for s in range(2)]
        qT = [sb(f"qT{s}", [P, HC, P]) for s in range(2)]
        uT = [sb(f"uT{s}", [P, HC, P]) for s in range(2)]
        ps_a = psum("ps_a", [P, HC, DC, P])
        ps_q = [psum(f"ps_q{i}", [P, 512]) for i in range(2)]
        ps_x = [psum(f"ps_x{i}", [P, HC, P]) for i in range(2)]
        ps_p = psum("ps_p", [P, HC, P])

        w_in = sem("w_in")
        x_in = [sem(f"x_in{s}") for s in range(2)]
        kk_start = sem("kk_start")
        bn_done = sem("bn_done")
        stats_done = sem("stats_done")
        ve_done = sem("ve_done")
        rstd_done = sem("rstd_done")
        xn_done = sem("xn_done")
        ta_done = sem("ta_done")
        aT_done = sem("aT_done")
        q_done = sem("q_done")
        qkv_done = sem("qkv_done")
        ksq_done = sem("ksq_done")
        kq_done = sem("kq_done")
        norm_done = sem("norm_done")
        norm_eps_done = sem("norm_eps_done")
        rnorm_done = sem("rnorm_done")
        u_done = sem("u_done")
        vs_done = sem("vs_done")
        tx_done = sem("tx_done")
        qT_done = sem("qT_done")
        uT_done = sem("uT_done")
        p_done = sem("p_done")
        kk_done = sem("kk_done")
        stored = [sem(f"stored{s}") for s in range(2)]

        with nc.Block() as block:
            @block.sync
            def _(sp):
                def load(st):
                    if not (isinstance(st.n, int) and st.n < 2):
                        wait(sp, xn_done, st.n - 1)
                    sp.dma_start(x[st.s][:], x_v[st.n]).then_inc(x_in[st.s], 16)

                def store(st):
                    lo, hi = HC * st.s, HC * st.s + HC
                    sp.wait_ge(vs_done, st.n + 1)
                    sp.dma_start(vs_v[st.pair, :, lo:hi], vs[st.s][:]).then_inc(stored[st.s], 16)
                    sp.wait_ge(qT_done, st.n + 1)
                    sp.dma_start(qT_v[st.pair, :, lo:hi], qT[st.s][:]).then_inc(stored[st.s], 16)
                    sp.wait_ge(uT_done, st.n + 1)
                    sp.dma_start(uT_v[st.pair, :, lo:hi], uT[st.s][:]).then_inc(stored[st.s], 16)

                def step(st):
                    if not is_last(st, NSTEP):
                        load(st.later(1))
                    if not is_first(st):
                        store(st.later(-1))

                sp.dma_start(w[:], a["WqkvT"].rearrange("(c p) n -> p c n", p=P)).then_inc(w_in, 16)
                sp.dma_start(bias[:], a["bqkv"].partition_broadcast(P)).then_inc(w_in, 16)
                load(Step(0, 0))
                steps(sp, NSTEP, step)
                store(Step(NSTEP // 2 - 1, 1))
                for s in range(2):
                    sp.wait_ge(stored[s], 48 * NSTEP // 2)

            @block.vector
            def _(v):
                def stats(st):
                    v.wait_ge(x_in[st.s], 16 * (st.pair + 1))
                    for t in range(HC):
                        i = nc.vector.bn_stats(bn[:, t], x[st.s][:, t])
                    i.then_inc(bn_done, 1)
                    v.wait_ge(bn_done, st.n + 1)
                    wait(v, rstd_done, st.n)
                    nc.vector.memset(gate[:], 0.0)
                    for t in range(HC):
                        i = nc.vector.bn_aggr(mv[:, t], bn[:, t])
                    i.then_inc(stats_done, 1)

                def normalise(st):
                    v.wait_ge(rstd_done, st.n + 1)
                    wait(v, ta_done, st.n)
                    for t in range(HC):
                        i = nc.vector.tensor_scalar(xn[:, t], x[st.s][:, t], mv[:, t, 0:1], rstd[:, t:t + 1],
                                                    ALU.subtract, ALU.mult)
                    i.then_inc(xn_done, 1)

                def add_bias(st):
                    if not is_first(st):
                        wait(v, tx_done, st.n - 1)
                        wait(v, vs_done, st.n - 1)
                        wait(v, u_done, st.n - 1)
                    for j in range(HC):
                        v.wait_ge(q_done, HC * st.n + j + 1)
                        nc.vector.tensor_tensor(qkv[st.s][:, j], ps_q[j % 2][:, :3 * H], bias[:],
                                                ALU.add).then_inc(qkv_done, 1)
                    v.wait_ge(qkv_done, HC * (st.n + 1))
                    wait(v, vs_done, st.n)
                    for j in range(HC):
                        i = nc.vector.tensor_tensor_reduce(junk_v[:, j], qkv[st.s][:, j, 0:H], qkv[st.s][:, j, H:2 * H],
                                                           1.0, 0.0, ALU.mult, ALU.add, kq[:, j:j + 1])
                    i.then_inc(kq_done, 1)

                def invert_norm(st):
                    v.wait_ge(norm_done, st.n + 1)
                    wait(v, u_done, st.n)
                    nc.vector.tensor_scalar(norm_eps[:], norm[:], NORM_EPS, None, ALU.add).then_inc(norm_eps_done, 1)
                    v.wait_ge(norm_eps_done, st.n + 1)
                    nc.vector.reciprocal(rnorm[:], norm_eps[:]).then_inc(rnorm_done, 1)

                def copy_qT(st):
                    v.wait_ge(tx_done, st.n + 1)
                    wait(v, stored[st.s], 48 * st.pair)
                    nc.vector.tensor_copy(qT[st.s][:], ps_x[0][:]).then_inc(qT_done, 1)

                def prefix(st):
                    v.wait_ge(p_done, st.n + 1)
                    for j in range(HC):
                        chunk = HC * st.s + j
                        if chunk == CHUNKS - 1:
                            nc.vector.memset(gate[:], 0.0).then_inc(kk_done, 1)
                            break
                        wait(v, kk_done, HC * st.n + j)
                        nc.vector.tensor_tensor(m.KK[:, bass.ds(st.pair + (chunk + 1) * BATCH, 1), :],
                                                ps_p[:, j:j + 1], m.KK[:, bass.ds(st.pair + chunk * BATCH, 1), :],
                                                ALU.add).then_inc(kk_done, 1)

                def step(st):
                    if not is_last(st, NSTEP):
                        stats(st.later(1))
                        normalise(st.later(1))
                    copy_qT(st)
                    prefix(st)
                    if not is_last(st, NSTEP):
                        add_bias(st.later(1))
                        invert_norm(st.later(1))

                for b in range(BATCH):
                    i = nc.vector.tensor_copy(m.KK[:, b], c.ident[:])
                i.then_inc(kk_start, 1)
                v.wait_ge(kk_start, 1)
                stats(Step(0, 0))
                normalise(Step(0, 0))
                v.wait_ge(w_in, 32)
                add_bias(Step(0, 0))
                invert_norm(Step(0, 0))
                steps(v, NSTEP, step)

            @block.gpsimd
            def _(pool):
                def rsqrt(st):
                    pool.wait_ge(stats_done, st.n + 1)
                    nc.gpsimd.tensor_tensor(ve[:], mv[:, :, 1], c.eps[:], ALU.add).then_inc(ve_done, 1)
                    pool.wait_ge(ve_done, st.n + 1)
                    wait(pool, xn_done, st.n)
                    nc.gpsimd.tensor_tensor(rstd[:], ve[:], c.minus_half[:], ALU.pow).then_inc(rstd_done, 1)

                def root(st):
                    pool.wait_ge(ksq_done, st.n + 1)
                    wait(pool, norm_eps_done, st.n)
                    nc.gpsimd.tensor_tensor(norm[:], ksq[:], c.plus_half[:], ALU.pow).then_inc(norm_done, 1)

                def scale_v(st):
                    pool.wait_ge(kq_done, st.n + 1)
                    wait(pool, stored[st.s], 48 * st.pair)
                    nc.gpsimd.tensor_tensor(vs[st.s][:], qkv[st.s][:, :, 2 * H:],
                                            kq[:].unsqueeze(2).to_broadcast([P, HC, H]),
                                            ALU.mult).then_inc(vs_done, 1)

                def step(st):
                    if not is_last(st, NSTEP):
                        rsqrt(st.later(1))
                        root(st.later(1))
                        scale_v(st.later(1))

                rsqrt(Step(0, 0))
                nc.gpsimd.memset(m.Tn[:], 0.0)
                nc.gpsimd.memset(m.Tt[:], 0.0)
                root(Step(0, 0))
                scale_v(Step(0, 0))
                steps(pool, NSTEP, step)

            @block.scalar
            def _(act):
                def copy_aT(st):
                    act.wait_ge(ta_done, st.n + 1)
                    wait(act, q_done, HC * st.n)
                    for i in range(2):
                        nc.scalar.activation(aT[:, 2 * i:2 * i + 2], ps_a[:, 2 * i:2 * i + 2],
                                             ACT.Copy).then_inc(aT_done, 1)

                def square(st):
                    wait(act, norm_done, st.n)
                    for j in range(HC):
                        act.wait_ge(qkv_done, HC * st.n + j + 1)
                        i = nc.scalar.activation(junk[:, j], qkv[st.s][:, j, H:2 * H], ACT.Square,
                                                 accum_out=ksq[:, j:j + 1])
                    i.then_inc(ksq_done, 1)

                def scale_u(st):
                    act.wait_ge(rnorm_done, st.n + 1)
                    if not is_first(st):
                        wait(act, p_done, st.n - 1)
                    for j in range(HC):
                        i = nc.scalar.activation(u[st.s][:, j], qkv[st.s][:, j, H:2 * H], ACT.Copy,
                                                 scale=rnorm[:, j:j + 1])
                    i.then_inc(u_done, 1)

                def copy_uT(st):
                    act.wait_ge(tx_done, st.n + 1)
                    wait(act, stored[st.s], 48 * st.pair)
                    nc.scalar.activation(uT[st.s][:], ps_x[1][:], ACT.Copy).then_inc(uT_done, 1)

                def step(st):
                    copy_uT(st)
                    if not is_last(st, NSTEP):
                        nxt = st.later(1)
                        copy_aT(nxt)
                        square(nxt)
                        scale_u(nxt)

                copy_aT(Step(0, 0))
                square(Step(0, 0))
                scale_u(Step(0, 0))
                steps(act, NSTEP, step)

            @block.tensor
            def _(pe):
                def turn_a(st):
                    pe.wait_ge(xn_done, st.n + 1)
                    wait(pe, aT_done, 2 * st.n)
                    for j in range(HC):
                        for d in range(DC):
                            i = nc.tensor.transpose(ps_a[:, j, d], xn[:, j, d * P:(d + 1) * P], c.ident[:])
                    i.then_inc(ta_done, 1)

                def products(st):
                    pe.wait_ge(aT_done, 2 * (st.n + 1))
                    for j in range(HC):
                        if not (is_first(st) and j < 2):
                            pe.wait_ge(qkv_done, HC * st.n + j - 1)
                        for d in range(DC):
                            i = nc.tensor.matmul(ps_q[j % 2][:, :3 * H], aT[:, j, d], w[:, d],
                                                 start=(d == 0), stop=(d == DC - 1))
                        i.then_inc(q_done, 1)

                def turn_qu(st):
                    pe.wait_ge(u_done, st.n + 1)
                    wait(pe, qT_done, st.n)
                    wait(pe, uT_done, st.n)
                    for j in range(HC):
                        nc.tensor.transpose(ps_x[0][:, j], qkv[st.s][:, j, 0:H], c.ident[:])
                        i = nc.tensor.transpose(ps_x[1][:, j], u[st.s][:, j], c.ident[:])
                    i.then_inc(tx_done, 1)

                def squares(st):
                    wait(pe, kk_done, HC * st.n)
                    for j in range(HC):
                        i = nc.tensor.matmul(ps_p[:, j], u[st.s][:, j], u[st.s][:, j], start=True, stop=True)
                    i.then_inc(p_done, 1)

                def step(st):
                    if not is_last(st, NSTEP):
                        turn_a(st.later(1))
                    turn_qu(st)
                    squares(st)
                    if not is_last(st, NSTEP):
                        products(st.later(1))

                turn_a(Step(0, 0))
                pe.wait_ge(w_in, 32)
                products(Step(0, 0))
                steps(pe, NSTEP, step)


LEAF, SCHUR, JOIN = "leaf", "schur", "join"
PLAN = [(LEAF, 0, 32), (SCHUR, 0, 32), (LEAF, 32, 32), (JOIN, 0, 32), (SCHUR, 0, 64),
        (LEAF, 64, 32), (SCHUR, 64, 32), (LEAF, 96, 32), (JOIN, 64, 32), (JOIN, 0, 64)]


def groups_of(w):
    n = 512 // w
    return n, NP // n


def done_before(kind, index):
    return sum(1 if kind == LEAF else groups_of(w)[1] for k, _, w in PLAN[:index] if k == kind)


def factorise(nc, name, m, c):
    with ExitStack() as ctx:
        def sb(what, shape, dt=F32):
            return ctx.enter_context(nc.sbuf_tensor(f"{name}_{what}", shape, dt))

        def psum(what, shape, dt=F32):
            return ctx.enter_context(nc.psum_tensor(f"{name}_{what}", shape, dt))

        def sem(what):
            return ctx.enter_context(nc.semaphore(f"{name}_{what}"))

        KK, Tn, Tt, dinv, ndinv = m.KK, m.Tn, m.Tt, m.dinv, m.ndinv
        lane_ident = sb("lane_ident", [NP, W, W])
        prod = sb("rank_one", [NP, W, W])
        mult = sb("multipliers", [NP, W])
        dl = sb("lane_dinv", [NP, W])
        Tl = sb("lane_T", [NP, W, W])
        Y = [sb(f"Y{i}", [P, 512]) for i in range(2)]
        V = [sb(f"V{i}", [P, 512]) for i in range(2)]
        Yd = {32: sb("Yd32", [P, NP, 32]), 64: sb("Yd64", [64, NP, 64])}
        ps_lane = psum("ps_lane", [P, 4, 512])
        M = ps_lane[0:NP].rearrange("p a (b x) -> p (a b) x", x=2 * W)
        ps = [psum(f"ps{i}", [P, 512]) for i in range(4)]

        init_done = sem("init_done")
        leaf_in = sem("leaf_in")
        leaf_T = sem("leaf_T")
        chain = sem("lane_chain")
        leaf_done = sem("leaf_done")
        out_done = sem("out_done")
        out_dve = sem("out_dve")
        out_act = sem("out_act")
        y_done = sem("y_done")
        y_copied = sem("y_copied")
        yd_done = sem("yd_done")
        s_done = sem("s_done")
        kk_done = sem("kk_done")
        v_done = sem("v_done")
        v_copied = sem("v_copied")
        j_done = sem("j_done")
        tn_done = sem("tn_done")
        tt_done = sem("tt_done")

        def span(o, w):
            return slice(o, o + w)

        with nc.Block() as block:
            @block.gpsimd
            def _(pool):
                nc.gpsimd.memset(lane_ident[:], 0.0).then_inc(init_done, 1)
                pool.wait_ge(init_done, 1)
                nc.gpsimd.affine_select(out=lane_ident[:], in_=lane_ident[:], compare_op=ALU.not_equal, fill=1.0,
                                        base=0, pattern=[[1, W], [-1, W]], channel_multiplier=0
                                        ).then_inc(init_done, 1)

            @block.vector
            def _(v):
                links = [0]

                def link(ins):
                    links[0] += 1
                    ins.then_inc(chain, 1)
                    v.wait_ge(chain, links[0])

                def leaf(index, o):
                    r = done_before(LEAF, index)
                    v.wait_ge(leaf_in, r + 1)
                    v.wait_ge(leaf_T, r + 1)
                    if r:
                        v.wait_ge(out_done, 9 * r)
                    for j in range(W):
                        n = W - 1 - j
                        link(nc.vector.reciprocal(dl[:, j:j + 1], M[:, j, j:j + 1]))
                        if not n:
                            break
                        link(nc.vector.tensor_scalar(mult[:, :n], M[:, j + 1:, j], dl[:, j:j + 1], -1.0,
                                                     ALU.mult, ALU.mult))
                        window = slice(j + 1, W + j)
                        nc.vector.tensor_copy(M[:, j + 1:, W + j], mult[:, :n])
                        link(nc.vector.tensor_tensor(prod[:, :n, :W - 1],
                                                     mult[:, :n].unsqueeze(2).to_broadcast([NP, n, W - 1]),
                                                     M[:, j:j + 1, window].to_broadcast([NP, n, W - 1]), ALU.mult))
                        link(nc.vector.tensor_tensor(M[:, j + 1:, window], M[:, j + 1:, window],
                                                     prod[:, :n, :W - 1], ALU.add))
                    nc.vector.tensor_copy(Tl[:], M[:, :, W:]).then_inc(leaf_done, 1)
                    v.wait_ge(out_done, 9 * r + 1)
                    nc.vector.tensor_copy(dinv[span(o, W)], ps[0][0:W, 0:NP])
                    nc.vector.tensor_scalar(ndinv[span(o, W)], ps[0][0:W, 0:NP], -1.0, None,
                                            ALU.mult).then_inc(out_dve, 1)
                    for q in range(4):
                        v.wait_ge(out_done, 9 * r + 3 + 2 * q)
                        at = o + 8 * q
                        nc.vector.tensor_copy(Tn[span(o, W), :, at:at + 8],
                                              ps[(2 + 2 * q) % 4][0:W].rearrange("i (j p) -> i p j", j=8)
                                              ).then_inc(out_dve, 1)

                def schur(index, o, w):
                    n, count = groups_of(w)
                    base = done_before(SCHUR, index)
                    b1, b2 = span(o, w), span(o + w, w)

                    def scale(g):
                        pr = slice(g * n, g * n + n)
                        v.wait_ge(y_copied, base + g + 1)
                        nc.vector.tensor_tensor(Yd[w][b1, pr], ps[g % 2][b1].rearrange("i (p j) -> i p j", p=n),
                                                ndinv[b1, pr].unsqueeze(2).to_broadcast([w, n, w]),
                                                ALU.mult).then_inc(yd_done, 1)

                    def update(g):
                        pr = slice(g * n, g * n + n)
                        v.wait_ge(s_done, base + g + 1)
                        nc.vector.tensor_tensor(KK[b2, pr, b2], ps[2 + g % 2][b2].rearrange("i (p j) -> i p j", p=n),
                                                KK[b2, pr, b2], ALU.add).then_inc(kk_done, 1)

                    v.wait_ge(chain, links[0])
                    v.wait_ge(out_dve, 5 * done_before(LEAF, index))
                    scale(0)
                    for g in range(count):
                        if g + 1 < count:
                            scale(g + 1)
                        update(g)

                def join(index, o, w):
                    n, count = groups_of(w)
                    base = done_before(JOIN, index)
                    b1, b2 = span(o, w), span(o + w, w)
                    for g in range(count):
                        pr = slice(g * n, g * n + n)
                        v.wait_ge(j_done, base + g + 1)
                        nc.vector.tensor_copy(Tn[b2, pr, b1], ps[2 + g % 2][b2].rearrange("i (p j) -> i p j", p=n)
                                              ).then_inc(tn_done, 1)

                for index, (kind, o, w) in enumerate(PLAN):
                    if kind == LEAF:
                        leaf(index, o)
                    elif kind == SCHUR:
                        schur(index, o, w)
                    else:
                        join(index, o, w)

            @block.scalar
            def _(act):
                def leaf(index, o):
                    r = done_before(LEAF, index)
                    if r == 0:
                        act.wait_ge(init_done, 2)
                    else:
                        act.wait_ge(leaf_done, r)
                    act.wait_ge(leaf_in, r + 1)
                    nc.scalar.activation(M[:, :, W:], lane_ident[:], ACT.Copy).then_inc(leaf_T, 1)
                    for q in range(4):
                        act.wait_ge(out_done, 9 * r + 2 + 2 * q)
                        at = o + 8 * q
                        nc.scalar.activation(Tt[span(o, W), :, at:at + 8],
                                             ps[(1 + 2 * q) % 4][0:W].rearrange("j (i p) -> j p i", i=8),
                                             ACT.Copy).then_inc(out_act, 1)

                def schur(index, o, w):
                    n, count = groups_of(w)
                    base = done_before(SCHUR, index)
                    b1 = span(o, w)
                    for g in range(count):
                        act.wait_ge(y_done, base + g + 1)
                        if base + g > 1:
                            act.wait_ge(s_done, base + g - 1)
                        nc.scalar.activation(Y[g % 2][b1], ps[g % 2][b1], ACT.Copy).then_inc(y_copied, 1)

                def join(index, o, w):
                    n, count = groups_of(w)
                    base = done_before(JOIN, index)
                    b1, b2 = span(o, w), span(o + w, w)

                    def copy_v(g):
                        act.wait_ge(v_done, base + g + 1)
                        if base + g > 1:
                            act.wait_ge(j_done, base + g - 1)
                        nc.scalar.activation(V[g % 2][b2], ps[g % 2][b2], ACT.Copy).then_inc(v_copied, 1)

                    copy_v(0)
                    for g in range(count):
                        if g + 1 < count:
                            copy_v(g + 1)
                        pr = slice(g * n, g * n + n)
                        act.wait_ge(j_done, base + g + 1)
                        nc.scalar.activation(Tt[b1, pr, b2], ps_lane[b1, g % 2].rearrange("i (p j) -> i p j", p=n),
                                             ACT.Copy).then_inc(tt_done, 1)

                for index, (kind, o, w) in enumerate(PLAN):
                    if kind == LEAF:
                        leaf(index, o)
                    elif kind == SCHUR:
                        schur(index, o, w)
                    else:
                        join(index, o, w)

            @block.tensor
            def _(pe):
                def all_copied(index):
                    r, sc, jn = (done_before(k, index) for k in (LEAF, SCHUR, JOIN))
                    wait(pe, out_dve, 5 * r)
                    wait(pe, out_act, 4 * r)
                    wait(pe, kk_done, sc)
                    wait(pe, tn_done, jn)
                    wait(pe, tt_done, jn)

                def leaf(index, o):
                    r = done_before(LEAF, index)
                    all_copied(index)
                    b = span(o, W)
                    for j in range(W):
                        i = nc.tensor.transpose(M[:, j, 0:W], KK[b, :, o + j], c.ident[b, b])
                    i.then_inc(leaf_in, 1)
                    pe.wait_ge(leaf_done, r + 1)
                    nc.tensor.transpose(ps[0][0:W, 0:NP], dl[:], c.ident[0:NP, 0:NP]).then_inc(out_done, 1)
                    for q in range(4):
                        for side in range(2):
                            bank = 1 + 2 * q + side
                            if bank == 4:
                                pe.wait_ge(out_dve, 5 * r + 1)
                            elif bank > 4 and side == 0:
                                pe.wait_ge(out_act, 4 * r + q - 1)
                            elif bank > 4:
                                pe.wait_ge(out_dve, 5 * r + q)
                            for k in range(8):
                                src = Tl[:, 8 * q + k, :] if side == 0 else Tl[:, :, 8 * q + k]
                                i = nc.tensor.transpose(ps[bank % 4][0:W, k * NP:(k + 1) * NP], src,
                                                        c.ident[0:NP, 0:NP])
                            i.then_inc(out_done, 1)

                def schur(index, o, w):
                    n, count = groups_of(w)
                    base = done_before(SCHUR, index)
                    b1, b2 = span(o, w), span(o + w, w)
                    all_copied(index)

                    def reduce_right(g):
                        if g > 1:
                            pe.wait_ge(y_copied, base + g - 1)
                            pe.wait_ge(yd_done, base + g - 1)
                        for k in range(n):
                            p = g * n + k
                            i = nc.tensor.matmul(ps[g % 2][b1, k * w:(k + 1) * w], Tt[b1, p, b1], KK[b1, p, b2],
                                                 start=True, stop=True)
                        i.then_inc(y_done, 1)

                    reduce_right(0)
                    for g in range(count):
                        if g + 1 < count:
                            reduce_right(g + 1)
                        pe.wait_ge(y_copied, base + g + 1)
                        pe.wait_ge(yd_done, base + g + 1)
                        if g > 1:
                            pe.wait_ge(kk_done, base + g - 1)
                        for k in range(n):
                            i = nc.tensor.matmul(ps[2 + g % 2][b2, k * w:(k + 1) * w],
                                                 Y[g % 2][b1, k * w:(k + 1) * w], Yd[w][b1, g * n + k],
                                                 start=True, stop=True)
                        i.then_inc(s_done, 1)

                def join(index, o, w):
                    n, count = groups_of(w)
                    base = done_before(JOIN, index)
                    b1, b2 = span(o, w), span(o + w, w)
                    all_copied(index)

                    def first(g):
                        if g > 1:
                            pe.wait_ge(v_copied, base + g - 1)
                        for k in range(n):
                            p = g * n + k
                            i = nc.tensor.matmul(ps[g % 2][b2, k * w:(k + 1) * w], Yd[w][b1, p], Tn[b1, p, b1],
                                                 start=True, stop=True)
                        i.then_inc(v_done, 1)

                    first(0)
                    for g in range(count):
                        if g + 1 < count:
                            first(g + 1)
                        pe.wait_ge(v_copied, base + g + 1)
                        if g > 1:
                            pe.wait_ge(tn_done, base + g - 1)
                            pe.wait_ge(tt_done, base + g - 1)
                        for k in range(n):
                            nc.tensor.matmul(ps[2 + g % 2][b2, k * w:(k + 1) * w], Tt[b2, g * n + k, b2],
                                             V[g % 2][b2, k * w:(k + 1) * w], start=True, stop=True)
                        for k in range(n):
                            i = nc.tensor.matmul(ps_lane[b1, g % 2, k * w:(k + 1) * w],
                                                 V[g % 2][b2, k * w:(k + 1) * w], Tt[b2, g * n + k, b2],
                                                 start=True, stop=True)
                        i.then_inc(j_done, 1)

                for index, (kind, o, w) in enumerate(PLAN):
                    if kind == LEAF:
                        leaf(index, o)
                    elif kind == SCHUR:
                        schur(index, o, w)
                    else:
                        join(index, o, w)


def gram(nc, m, c):
    uT_v, UA_v = (y.rearrange("(g k) i j -> g i k j", k=GROUP) for y in (m.uT, m.UA))
    with ExitStack() as ctx:
        def sb(what, shape, dt=F32):
            return ctx.enter_context(nc.sbuf_tensor(f"gram_{what}", shape, dt))

        def psum(what):
            return [ctx.enter_context(nc.psum_tensor(f"gram_{what}{i}", [P, GROUP, P], F32)) for i in range(2)]

        def sem(what):
            return ctx.enter_context(nc.semaphore(f"gram_{what}"))

        group = [P, GROUP, P]
        uTa, uTb, Td, A, WW, UA = ([sb(f"{x}{s}", group) for s in range(2)]
                                   for x in ("uT_for_w", "uT_for_g", "Td", "A", "W", "UA"))
        ps_a, ps_w, ps_g, ps_u = (psum(x) for x in ("ps_a", "ps_w", "ps_g", "ps_u"))
        ua_in = [sem(f"uT_for_w_in{s}") for s in range(2)]
        ub_in = [sem(f"uT_for_g_in{s}") for s in range(2)]
        td_done, a_done, A_done, w_done, W_done, g_done, kk_done, u_done, UA_done = (
            sem(x) for x in ("td_done", "a_product", "A_done", "w_product", "W_done", "g_product", "kk_done",
                             "u_turned", "UA_done"))
        stored = [sem(f"stored{s}") for s in range(2)]

        with nc.Block() as block:
            @block.sync
            def _(sp):
                def load_a(st):
                    if not (isinstance(st.n, int) and st.n < 2):
                        wait(sp, w_done, st.n - 1)
                    sp.dma_start(uTa[st.s][:], uT_v[st.n]).then_inc(ua_in[st.s], 16)

                def load_b(st):
                    if not (isinstance(st.n, int) and st.n < 2):
                        wait(sp, g_done, st.n - 1)
                    sp.dma_start(uTb[st.s][:], uT_v[st.n]).then_inc(ub_in[st.s], 16)

                def store(st):
                    sp.wait_ge(UA_done, st.n + 1)
                    sp.dma_start(UA_v[st.n], UA[st.s][:]).then_inc(stored[st.s], 16)

                def step(st):
                    if not is_last(st, NG):
                        load_a(st.later(1))
                        load_b(st.later(1))
                    if not is_first(st):
                        store(st.later(-1))

                load_a(Step(0, 0))
                load_b(Step(0, 0))
                steps(sp, NG, step)
                store(Step(NG // 2 - 1, 1))
                for s in range(2):
                    sp.wait_ge(stored[s], 16 * NG // 2)

            @block.vector
            def _(v):
                def scale(st):
                    if not is_first(st):
                        wait(v, a_done, st.n - 1)
                    nc.vector.tensor_tensor(Td[st.s][:], m.Tn[:, bass.ds(st.n * GROUP, GROUP), :],
                                            m.dinv[:, bass.ds(st.n * GROUP, GROUP)].unsqueeze(2).to_broadcast(group),
                                            ALU.mult).then_inc(td_done, 1)

                def copy_w(st):
                    v.wait_ge(w_done, st.n + 1)
                    if not is_first(st):
                        wait(v, g_done, st.n - 1)
                        wait(v, u_done, st.n - 1)
                    nc.vector.tensor_copy(WW[st.s][:], ps_w[st.s][:]).then_inc(W_done, 1)

                def add_identity(st):
                    v.wait_ge(g_done, st.n + 1)
                    nc.vector.tensor_tensor(m.KK[:, bass.ds(st.n * GROUP, GROUP), :], ps_g[st.s][:],
                                            c.ident[:].unsqueeze(1).to_broadcast(group),
                                            ALU.add).then_inc(kk_done, 1)

                def step(st):
                    if not is_last(st, NG):
                        scale(st.later(1))
                    copy_w(st)
                    if not is_first(st):
                        add_identity(st.later(-1))

                scale(Step(0, 0))
                steps(v, NG, step)
                add_identity(Step(NG // 2 - 1, 1))

            @block.scalar
            def _(act):
                def copy_a(st):
                    act.wait_ge(a_done, st.n + 1)
                    if not is_first(st):
                        wait(act, w_done, st.n - 1)
                    nc.scalar.activation(A[st.s][:], ps_a[st.s][:], ACT.Copy).then_inc(A_done, 1)

                def copy_ua(st):
                    act.wait_ge(u_done, st.n + 1)
                    wait(act, stored[st.s], 16 * st.pair)
                    nc.scalar.activation(UA[st.s][:], ps_u[st.s][:], ACT.Copy).then_inc(UA_done, 1)

                def step(st):
                    if not is_last(st, NG):
                        copy_a(st.later(1))
                    if not is_first(st):
                        copy_ua(st.later(-1))

                copy_a(Step(0, 0))
                steps(act, NG, step)
                copy_ua(Step(NG // 2 - 1, 1))

            @block.tensor
            def _(pe):
                def inverse(st):
                    pe.wait_ge(td_done, st.n + 1)
                    if not is_first(st):
                        wait(pe, A_done, st.n - 1)
                    for k in range(GROUP):
                        i = nc.tensor.matmul(ps_a[st.s][:, k], Td[st.s][:, k], m.Tn[:, bass.ds(st.n * GROUP + k, 1), :],
                                             start=True, stop=True)
                    i.then_inc(a_done, 1)

                def times_u(st):
                    pe.wait_ge(ua_in[st.s], 16 * (st.pair + 1))
                    pe.wait_ge(A_done, st.n + 1)
                    if not is_first(st):
                        wait(pe, W_done, st.n - 1)
                    for k in range(GROUP):
                        i = nc.tensor.matmul(ps_w[st.s][:, k], A[st.s][:, k], uTa[st.s][:, k], start=True, stop=True)
                    i.then_inc(w_done, 1)

                def products(st):
                    pe.wait_ge(ub_in[st.s], 16 * (st.pair + 1))
                    pe.wait_ge(W_done, st.n + 1)
                    if not is_first(st):
                        wait(pe, kk_done, st.n - 1)
                        wait(pe, UA_done, st.n - 1)
                    for k in range(GROUP):
                        i = nc.tensor.matmul(ps_g[st.s][:, k], uTb[st.s][:, k], WW[st.s][:, k], start=True, stop=True)
                    i.then_inc(g_done, 1)
                    for k in range(GROUP):
                        i = nc.tensor.transpose(ps_u[st.s][:, k], WW[st.s][:, k], c.ident[:])
                    i.then_inc(u_done, 1)

                def step(st):
                    if not is_last(st, NG):
                        inverse(st.later(1))
                    times_u(st)
                    if not is_first(st):
                        products(st.later(-1))

                inverse(Step(0, 0))
                steps(pe, NG, step)
                products(Step(NG // 2 - 1, 1))


def outputs(nc, x1, x2, m, c, a):
    x_v, o_v = (y.rearrange("(b c t) d -> c t b d", b=BATCH, t=P) for y in (x1, x2))
    UA_v, qT_v, vs_v = (y.rearrange("(g k) i j -> g i k j", k=GROUP) for y in (m.UA, m.qT, m.vs))
    with ExitStack() as ctx:
        def sb(what, shape, dt=F32):
            return ctx.enter_context(nc.sbuf_tensor(f"out_{what}", shape, dt))

        def psum(what, shape):
            return ctx.enter_context(nc.psum_tensor(f"out_{what}", shape, F32))

        def sem(what):
            return ctx.enter_context(nc.semaphore(f"out_{what}"))

        group = [P, GROUP, P]
        wide = [P, GROUP, D]
        UA, qT, v0, vd, zT, zn, sc, oT, M = ([sb(f"{x}{s}", group) for s in range(2)]
                                             for x in ("UA", "qT", "v", "v_over_d", "zT", "z", "scores", "oT", "M"))
        x, xb, xo = ([sb(f"{y}{s}", wide) for s in range(2)] for y in ("x", "x_plus_bias", "x_out"))
        dcol = [sb(f"dcol{s}", [P, GROUP]) for s in range(2)]
        wo = sb("wo", [P, D])
        bo = sb("bo", [P, D])
        ps_z, ps_s, ps_n, ps_o, ps_m = (psum(y, group) for y in ("ps_z", "ps_s", "ps_n", "ps_o", "ps_m"))
        ps_r = psum("ps_r", wide)
        w_in = sem("w_in")
        UA_in, q_in, v_in, x_in, stored = ([sem(f"{y}{s}") for s in range(2)]
                                           for y in ("UA_in", "q_in", "v_in", "x_in", "stored"))
        (M_zero, dcol_done, vd_done, xb_done, z_done, zT_done, s_done, sc_done, n_done, zn_done, o_done, oT_done,
         m_done, M_done, r_done, xo_done) = (
            sem(y) for y in ("M_zero", "dcol_done", "vd_done", "xb_done", "z_product", "zT_done", "s_product",
                             "sc_done", "z_turned", "zn_done", "o_product", "oT_done", "m_product", "M_done",
                             "r_product", "xo_done"))

        with nc.Block() as block:
            @block.sync
            def _(sp):
                def load(st, tiles, src, landed, used):
                    if not (isinstance(st.n, int) and st.n < 2):
                        wait(sp, used, st.n - 1)
                    sp.dma_start(tiles[st.s][:], src).then_inc(landed[st.s], 16)

                def load_ua(st):
                    load(st, UA, UA_v[st.n], UA_in, z_done)

                def load_rest(st):
                    load(st, v0, vs_v[st.n], v_in, vd_done)
                    load(st, qT, qT_v[st.n], q_in, o_done)
                    load(st, x, x_v[st.pair, :, GROUP * st.s:GROUP * st.s + GROUP], x_in, xb_done)

                def step(st):
                    if not is_last(st, NG):
                        load_ua(st.later(1))
                        load_rest(st.later(1))

                sp.dma_start(wo[:], a["WoT"]).then_inc(w_in, 16)
                sp.dma_start(bo[:], a["bo"].partition_broadcast(P)).then_inc(w_in, 16)
                load_ua(Step(0, 0))
                load_rest(Step(0, 0))
                steps(sp, NG, step)

            @block.gpsimd
            def _(pool):
                def scale_v(st):
                    pool.wait_ge(v_in[st.s], 16 * (st.pair + 1))
                    pool.wait_ge(dcol_done, st.n + 1)
                    if not is_first(st):
                        wait(pool, m_done, st.n - 1)
                    nc.gpsimd.tensor_tensor(vd[st.s][:], v0[st.s][:], dcol[st.s][:].unsqueeze(2).to_broadcast(group),
                                            ALU.mult).then_inc(vd_done, 1)

                def add_bias(st):
                    pool.wait_ge(x_in[st.s], 16 * (st.pair + 1))
                    if not is_first(st):
                        wait(pool, xo_done, st.n - 1)
                    nc.gpsimd.tensor_tensor(xb[st.s][:], x[st.s][:], bo[:].unsqueeze(1).to_broadcast(wide),
                                            ALU.add).then_inc(xb_done, 1)

                def step(st):
                    if not is_last(st, NG):
                        scale_v(st.later(1))
                    add_bias(st)

                pool.wait_ge(w_in, 32)
                scale_v(Step(0, 0))
                steps(pool, NG, step)

            @block.vector
            def _(v):
                def pick_d(st):
                    if not is_first(st):
                        wait(v, vd_done, st.n - 1)
                    nc.vector.tensor_copy(dcol[st.s][:], m.dinv[:, bass.ds(st.n * GROUP, GROUP)]
                                          ).then_inc(dcol_done, 1)

                def mask(st):
                    v.wait_ge(s_done, st.n + 1)
                    if not is_first(st):
                        wait(v, o_done, st.n - 1)
                    nc.vector.tensor_tensor(sc[st.s][:], ps_s[:], c.causal[:].unsqueeze(1).to_broadcast(group),
                                            ALU.mult).then_inc(sc_done, 1)

                def update(st):
                    v.wait_ge(m_done, st.n + 1)
                    nc.vector.tensor_tensor(M[st.s][:], ps_m[:], M[st.s][:], ALU.add).then_inc(M_done, 1)

                def residual(st):
                    v.wait_ge(r_done, st.n + 1)
                    v.wait_ge(xb_done, st.n + 1)
                    wait(v, stored[st.s], 16 * st.pair)
                    nc.vector.tensor_tensor(xo[st.s][:], ps_r[:], xb[st.s][:], ALU.add).then_inc(xo_done, 1)

                def step(st):
                    if not is_last(st, NG):
                        pick_d(st.later(1))
                    mask(st)
                    if not is_first(st):
                        residual(st.later(-1))
                    update(st)

                for s in range(2):
                    nc.vector.memset(M[s][:], 0.0).then_inc(M_zero, 1)
                v.wait_ge(M_zero, 2)
                pick_d(Step(0, 0))
                steps(v, NG, step)
                residual(Step(NG // 2 - 1, 1))

            @block.scalar
            def _(act):
                def copy(st, dst, src, made, used, done):
                    act.wait_ge(made, st.n + 1)
                    if not is_first(st):
                        wait(act, used, st.n - 1)
                    nc.scalar.activation(dst[st.s][:], src[:], ACT.Copy).then_inc(done, 1)

                def store(st):
                    act.wait_ge(xo_done, st.n + 1)
                    act.dma_start(o_v[st.pair, :, GROUP * st.s:GROUP * st.s + GROUP], xo[st.s][:]
                                  ).then_inc(stored[st.s], 16)

                def step(st):
                    if not is_last(st, NG):
                        copy(st.later(1), zT, ps_z, z_done, n_done, zT_done)
                    copy(st, zn, ps_n, n_done, m_done, zn_done)
                    if not is_first(st):
                        store(st.later(-1))
                    copy(st, oT, ps_o, o_done, r_done, oT_done)

                copy(Step(0, 0), zT, ps_z, z_done, n_done, zT_done)
                steps(act, NG, step)
                store(Step(NG // 2 - 1, 1))
                for s in range(2):
                    act.wait_ge(stored[s], 16 * NG // 2)

            @block.tensor
            def _(pe):
                def z_product(st):
                    pe.wait_ge(UA_in[st.s], 16 * (st.pair + 1))
                    wait(pe, zT_done, st.n)
                    for k in range(GROUP):
                        i = nc.tensor.matmul(ps_z[:, k], UA[st.s][:, k], m.Tt[:, bass.ds(st.n * GROUP + k, 1), :],
                                             start=True, stop=True)
                    i.then_inc(z_done, 1)

                def scores(st):
                    pe.wait_ge(zT_done, st.n + 1)
                    pe.wait_ge(q_in[st.s], 16 * (st.pair + 1))
                    wait(pe, sc_done, st.n)
                    for k in range(GROUP):
                        i = nc.tensor.matmul(ps_s[:, k], zT[st.s][:, k], qT[st.s][:, k], start=True, stop=True)
                    i.then_inc(s_done, 1)
                    wait(pe, zn_done, st.n)
                    for k in range(GROUP):
                        i = nc.tensor.transpose(ps_n[:, k], zT[st.s][:, k], c.ident[:])
                    i.then_inc(n_done, 1)

                def attend(st):
                    pe.wait_ge(sc_done, st.n + 1)
                    pe.wait_ge(vd_done, st.n + 1)
                    wait(pe, oT_done, st.n)
                    if is_first(st):
                        pe.wait_ge(M_zero, 2)
                    else:
                        wait(pe, M_done, st.n - 1)
                    for k in range(GROUP):
                        nc.tensor.matmul(ps_o[:, k], vd[st.s][:, k], sc[st.s][:, k], start=True, stop=False)
                        i = nc.tensor.matmul(ps_o[:, k], M[st.s][:, k], qT[st.s][:, k], start=False, stop=True)
                    i.then_inc(o_done, 1)
                    pe.wait_ge(zn_done, st.n + 1)
                    wait(pe, M_done, st.n)
                    for k in range(GROUP):
                        i = nc.tensor.matmul(ps_m[:, k], zn[st.s][:, k], vd[st.s][:, k], start=True, stop=True)
                    i.then_inc(m_done, 1)

                def project_out(st):
                    pe.wait_ge(oT_done, st.n + 1)
                    wait(pe, xo_done, st.n)
                    for k in range(GROUP):
                        i = nc.tensor.matmul(ps_r[:, k], oT[st.s][:, k], wo[:], start=True, stop=True)
                    i.then_inc(r_done, 1)

                def step(st):
                    if not is_last(st, NG):
                        z_product(st.later(1))
                    scores(st)
                    if not is_first(st):
                        project_out(st.later(-1))
                    attend(st)

                pe.wait_ge(w_in, 32)
                z_product(Step(0, 0))
                steps(pe, NG, step)
                project_out(Step(NG // 2 - 1, 1))


class Names:
    pass


def macaron(nc, a, out):
    def dram(name, shape):
        return nc.dram_tensor(name, shape, F32, kind="Internal").ap()

    x1, x2 = dram("x1_scratch", (TOKENS, D)), dram("x2_scratch", (TOKENS, D))
    m = Names()
    m.qT, m.uT, m.vs, m.UA = (dram(f"{n}_scratch", (NP, P, P)) for n in ("qT", "uT", "vs", "UA"))
    with ExitStack() as ctx:
        c = Names()
        prepare(nc, ctx, a, c)
        feed_forward(nc, "ffn1", a["x"], x1, c)
        with ExitStack() as own:
            m.KK, m.Tn, m.Tt = (own.enter_context(nc.sbuf_tensor(n, [P, NP, P], F32)) for n in ("KK", "Tn", "Tt"))
            m.dinv, m.ndinv = (own.enter_context(nc.sbuf_tensor(n, [P, NP], F32)) for n in ("dinv", "minus_dinv"))
            project(nc, x1, m, c, a)
            factorise(nc, "inv", m, c)
            gram(nc, m, c)
            factorise(nc, "ldl", m, c)
            outputs(nc, x1, x2, m, c, a)
        feed_forward(nc, "ffn2", x2, out, c)


def kernel(**inputs):
    import numpy as np
    import concourse.bacc as bacc
    from concourse import mybir as _mybir
    from concourse.bass_utils import run_bass_kernel_spmd

    g = {k.replace("L0_", ""): np.asarray(v) for k, v in inputs.items()}
    laid = {
        "x": g["attn_x"].reshape(TOKENS, D),
        "W1T": g["ffn_W1"].T,
        "W2T": g["ffn_W2"].T,
        "b1": g["ffn_b1"].reshape(FC, P).T,
        "b2": g["ffn_b2"],
        "WqkvT": np.concatenate([g["attn_Wq"].T, g["attn_Wk"].T, g["attn_Wv"].T], axis=1),
        "bqkv": np.concatenate([g["attn_bq"], g["attn_bk"], g["attn_bv"]]),
        "WoT": g["attn_Wo"].T,
        "bo": g["attn_bo"],
    }
    nc = bacc.Bacc("TRN2", target_bir_lowering=False, num_devices=1)
    arrays, aps = {}, {}
    for k, v in laid.items():
        arrays[f"in_{k}"] = np.ascontiguousarray(v)
        aps[k] = nc.dram_tensor(f"in_{k}", v.shape, _mybir.dt.from_np(v.dtype), kind="ExternalInput").ap()
    out = nc.dram_tensor("out_x", (TOKENS, D), F32, kind="ExternalOutput").ap()
    macaron(nc, aps, out)
    r = run_bass_kernel_spmd(nc, [arrays], core_ids=[0])
    return r.results[0]["out_x"].reshape(BATCH, T, D)
```

```python
from contextlib import ExitStack

import concourse.bass as bass
from concourse import mybir

F32 = mybir.dt.float32
F16 = mybir.dt.float16
ALU = mybir.AluOpType
ACT = mybir.ActivationFunctionType
AX_X = mybir.AxisListType.X

P = 128
BATCH, T, D = 8, 1024, 256
H = 128
FF = 1024
DC = D // P
FC = FF // P
TOKENS = BATCH * T
BLOCK = 512
BT = BLOCK // P
NBLOCK = TOKENS // BLOCK
CHUNKS = T // P
NP = BATCH * CHUNKS
GROUP = 4
NG = NP // GROUP
LN_EPS = 1e-5
NORM_EPS = 1e-6
W = 32
NW = P // W


def wait(eng, sem, value):
    if not isinstance(value, int) or value > 0:
        eng.wait_ge(sem, value)


class Step:

    def __init__(self, pair, parity):
        self.pair, self.s, self.n = pair, parity, pair * 2 + parity

    def later(self, k):
        p = self.s + k
        return Step(self.pair + p // 2, p % 2)


def steps(eng, count, body, head=3, tail=1):
    for n in range(head):
        body(Step(n // 2, n % 2))
    with eng.Fori(head // 2, (count - tail) // 2) as m:
        body(Step(m, 1))
        body(Step(m + 1, 0))
    for n in range(count - tail, count):
        body(Step(n // 2, n % 2))


def is_first(st):
    return isinstance(st.n, int) and st.n == 0


def is_last(st, count):
    return isinstance(st.n, int) and st.n == count - 1


def prepare(nc, ctx, a, c):
    def sb(name, shape, dt=F32):
        return ctx.enter_context(nc.sbuf_tensor(name, shape, dt))

    c.w1 = sb("w1_ternary", [P, DC, FF], F16)
    c.w2 = sb("w2_ternary", [P, FC, D], F16)
    c.b1 = sb("b1_columns", [P, FC])
    c.hb2 = sb("half_b2_rows", [P, D])
    c.ident = sb("ident", [P, P])
    c.ident16 = sb("ident16", [P, P], F16)
    c.causal = sb("causal", [P, P])
    c.minus_half = sb("minus_half", [P, BT])
    c.eps = sb("ln_eps", [P, BT])
    c.plus_half = sb("plus_half", [P, BT])

    with ExitStack() as own:
        def tmp(name, shape, dt=F32):
            return own.enter_context(nc.sbuf_tensor(name, shape, dt))

        def sem(name):
            return own.enter_context(nc.semaphore(name))

        raw = [tmp("w1_raw", [P, DC * FF]), tmp("w2_raw", [P, FC * D])]
        tern = [c.w1[:].rearrange("p c f -> p (c f)"), c.w2[:].rearrange("p c d -> p (c d)")]
        absw = tmp("abs_w", [P, 2, 2048])
        part = tmp("partial_sums", [P, 2, 32])
        colsum = tmp("column_sums", [P, 2])
        mean_w = tmp("mean_weights", [P, P])
        thr = tmp("thresholds", [P, 2, 2])
        above = tmp("above", [P, 2, 2048])
        below = tmp("below", [P, 2, 2048])
        b2_rows = tmp("b2_rows", [P, D])
        ps = own.enter_context(nc.psum_tensor("mean_psum", [P, 2], F32))
        w_in = [sem("prep_w1_in"), sem("prep_w2_in")]
        small_in = sem("prep_small_in")
        abs_done = sem("prep_abs_done")
        dve = sem("prep_dve_chain")
        sums_done = sem("prep_sums_done")
        mean_done = sem("prep_mean_done")
        pool = sem("prep_pool_chain")
        consts = sem("prep_mean_weights_done")

        with nc.Block() as block:
            @block.sync
            def _(sp):
                sp.dma_start(raw[0][:].rearrange("p (c f) -> p c f", c=DC),
                             a["W1T"].rearrange("(c p) f -> p c f", p=P)).then_inc(w_in[0], 16)
                sp.dma_start(raw[1][:].rearrange("p (c d) -> p c d", c=FC),
                             a["W2T"].rearrange("(c p) d -> p c d", p=P)).then_inc(w_in[1], 16)
                sp.dma_start(c.b1[:], a["b1"]).then_inc(small_in, 16)
                sp.dma_start(b2_rows[:], a["b2"].partition_broadcast(P)).then_inc(small_in, 16)
                sp.wait_ge(small_in, 32)

            @block.scalar
            def _(act):
                for i in range(2):
                    act.wait_ge(w_in[i], 16)
                    nc.scalar.activation(absw[:, i], raw[i][:], ACT.Abs).then_inc(abs_done, 1)
                act.wait_ge(small_in, 32)
                nc.scalar.mul(c.hb2[:], b2_rows[:], 0.5)

            @block.gpsimd
            def _(pool_):
                nc.gpsimd.memset(mean_w[:], 1.0 / (FF * D)).then_inc(consts, 1)
                nc.gpsimd.memset(c.ident[:], 0.0).then_inc(pool, 1)
                nc.gpsimd.memset(c.causal[:], 1.0).then_inc(pool, 1)
                nc.gpsimd.memset(c.minus_half[:], -0.5)
                nc.gpsimd.memset(c.eps[:], LN_EPS)
                nc.gpsimd.memset(c.plus_half[:], 0.5)
                pool_.wait_ge(pool, 2)
                nc.gpsimd.affine_select(out=c.ident[:], in_=c.ident[:], compare_op=ALU.not_equal, fill=1.0,
                                        base=0, pattern=[[1, P]], channel_multiplier=-1).then_inc(pool, 1)
                nc.gpsimd.affine_select(out=c.causal[:], in_=c.causal[:], compare_op=ALU.is_ge, fill=0.0,
                                        base=0, pattern=[[1, P]], channel_multiplier=-1)
                pool_.wait_ge(pool, 3)
                nc.gpsimd.tensor_copy(c.ident16[:], c.ident[:])

            @block.vector
            def _(v):
                n = [0]

                def link(ins):
                    n[0] += 1
                    ins.then_inc(dve, 1)
                    v.wait_ge(dve, n[0])

                for i in range(2):
                    v.wait_ge(abs_done, i + 1)
                    link(nc.vector.tensor_reduce(part[:, i], absw[:, i].rearrange("p (a b) -> p a b", b=64),
                                                 AX_X, ALU.add))
                    nc.vector.tensor_reduce(colsum[:, i:i + 1], part[:, i], AX_X, ALU.add).then_inc(sums_done, 1)
                v.wait_ge(mean_done, 1)
                link(nc.vector.tensor_scalar(thr[:, 0], ps[:], 1e-8, 0.5, ALU.max, ALU.mult))
                link(nc.vector.tensor_scalar(thr[:, 1], thr[:, 0], -1.0, None, ALU.mult))
                for i in range(2):
                    nc.vector.tensor_scalar(above[:, i], raw[i][:], thr[:, 0, i:i + 1], None, ALU.is_gt)
                    link(nc.vector.tensor_scalar(below[:, i], raw[i][:], thr[:, 1, i:i + 1], None, ALU.is_lt))
                for i in range(2):
                    nc.vector.tensor_tensor(tern[i], above[:, i], below[:, i], ALU.subtract)

            @block.tensor
            def _(pe):
                pe.wait_ge(consts, 1)
                pe.wait_ge(sums_done, 2)
                nc.tensor.matmul(ps[:], mean_w[:], colsum[:], start=True, stop=True).then_inc(mean_done, 1)


def feed_forward(nc, name, src, dst, c):
    x_v = src.rearrange("(n p t) d -> n p t d", p=P, t=BT)
    o_v = dst.rearrange("(n p t) d -> n p t d", p=P, t=BT)
    with ExitStack() as ctx:
        def sb(what, shape, dt=F32):
            return ctx.enter_context(nc.sbuf_tensor(f"{name}_{what}", shape, dt))

        def psum(what, shape, dt=F32):
            return ctx.enter_context(nc.psum_tensor(f"{name}_{what}", shape, dt))

        def sem(what):
            return ctx.enter_context(nc.semaphore(f"{name}_{what}"))

        x = [sb(f"x{s}", [P, BT, D]) for s in range(2)]
        bn = sb("bn", [P, BT, 6])
        gate = sb("gate", [P, 1])
        mv = sb("mean_var", [P, BT, 2])
        ve = sb("var_eps", [P, BT])
        rstd = sb("rstd", [P, BT])
        xn = sb("xn", [P, BT, D])
        xh = sb("xn_high", [P, BT, D], F16)
        xl = sb("xn_rest", [P, BT, D], F16)
        xTh = [sb(f"xT_high{s}", [P, DC, BLOCK], F16) for s in range(2)]
        xTl = [sb(f"xT_rest{s}", [P, DC, BLOCK], F16) for s in range(2)]
        hh = [sb(f"h_high{s}", [P, FC, BLOCK], F16) for s in range(2)]
        hl = [sb(f"h_rest{s}", [P, FC, BLOCK], F16) for s in range(2)]
        xb = [sb(f"x_plus_bias{s}", [P, BT, D]) for s in range(2)]
        xo = [sb(f"x_out{s}", [P, BT, D]) for s in range(2)]
        ps_t = [psum(f"ps_t{i}", [P, DC, BLOCK], F16) for i in range(2)]
        ps_h = [psum(f"ps_h{i}", [P, BLOCK]) for i in range(4)]
        ps_y = [psum(f"ps_y{i}", [P, D]) for i in range(2)]

        x_in = [sem(f"x_in{s}") for s in range(2)]
        bn_done = sem("bn_done")
        stats_done = sem("stats_done")
        ve_done = sem("ve_done")
        rstd_done = sem("rstd_done")
        xn_done = sem("xn_done")
        xh_done = sem("xh_done")
        xl_done = sem("xl_done")
        xb_done = sem("xb_done")
        tr_done = sem("tr_done")
        xT_done = sem("xT_done")
        h_done = sem("h_done")
        g_done = sem("g_done")
        hl_done = sem("hl_done")
        y_done = sem("y_done")
        xo_done = sem("xo_done")
        stored = [sem(f"stored{s}") for s in range(2)]

        def two_ahead(st):
            return not isinstance(st.n, int) or st.n + 2 < NBLOCK

        def run(eng, step):
            steps(eng, NBLOCK, step, tail=3)

        with nc.Block() as block:
            @block.sync
            def _(sp):
                def load(st):
                    if not (isinstance(st.n, int) and st.n < 2):
                        wait(sp, xn_done, st.n - 1)
                        wait(sp, xb_done, st.n - 1)
                    sp.dma_start(x[st.s][:], x_v[st.n]).then_inc(x_in[st.s], 16)

                def step(st):
                    if two_ahead(st):
                        load(st.later(2))

                load(Step(0, 0))
                load(Step(0, 1))
                run(sp, step)

            @block.vector
            def _(v):
                def stats(st):
                    v.wait_ge(x_in[st.s], 16 * (st.pair + 1))
                    for t in range(BT):
                        i = nc.vector.bn_stats(bn[:, t], x[st.s][:, t])
                    i.then_inc(bn_done, 1)
                    v.wait_ge(bn_done, st.n + 1)
                    wait(v, rstd_done, st.n)
                    nc.vector.memset(gate[:], 0.0)
                    for t in range(BT):
                        i = nc.vector.bn_aggr(mv[:, t], bn[:, t])
                    i.then_inc(stats_done, 1)

                def normalise(st):
                    v.wait_ge(rstd_done, st.n + 1)
                    wait(v, xh_done, st.n)
                    wait(v, xl_done, st.n)
                    for t in range(BT):
                        i = nc.vector.tensor_scalar(xn[:, t], x[st.s][:, t], mv[:, t, 0:1], rstd[:, t:t + 1],
                                                    ALU.subtract, ALU.mult)
                    i.then_inc(xn_done, 1)

                def rest(st, f):
                    v.wait_ge(g_done, FC * st.n + f + 1)
                    if f == 0:
                        wait(v, y_done, BT * (st.n - 1)) if not is_first(st) else None
                    nc.vector.tensor_tensor(hl[st.s][:, f], ps_h[f % 4][:], hh[st.s][:, f],
                                            ALU.subtract).then_inc(hl_done, 1)

                def copy_xT(st):
                    v.wait_ge(tr_done, st.n + 1)
                    wait(v, h_done, FC * (st.n - 1)) if not is_first(st) else None
                    nc.vector.tensor_copy(xTh[st.s][:], ps_t[0][:]).then_inc(xT_done, 1)
                    nc.vector.tensor_copy(xTl[st.s][:], ps_t[1][:]).then_inc(xT_done, 1)

                def finish(st, t):
                    v.wait_ge(y_done, BT * st.n + t + 1)
                    if t == 0:
                        v.wait_ge(xb_done, st.n + 1)
                        wait(v, stored[st.s], st.pair * 16)
                    nc.vector.scalar_tensor_tensor(out=xo[st.s][:, t], in0=ps_y[t % 2][:], scalar=0.5,
                                                   in1=xb[st.s][:, t], op0=ALU.mult, op1=ALU.add
                                                   ).then_inc(xo_done, 1)

                def step(st):
                    first, last, prev = is_first(st), is_last(st, NBLOCK), st.later(-1)
                    if not last:
                        normalise(st.later(1))
                    for f in range(FC):
                        rest(st, f)
                        if not first and f in (2, 4, 6):
                            finish(prev, (f - 2) // 2)
                        if f == 5 and not last:
                            copy_xT(st.later(1))
                        if f == 6 and two_ahead(st):
                            stats(st.later(2))
                    if not first:
                        finish(prev, BT - 1)

                stats(Step(0, 0))
                normalise(Step(0, 0))
                stats(Step(0, 1))
                copy_xT(Step(0, 0))
                run(v, step)
                for t in range(BT):
                    finish(Step((NBLOCK - 1) // 2, (NBLOCK - 1) % 2), t)

            @block.gpsimd
            def _(pool):
                def rsqrt(st):
                    pool.wait_ge(stats_done, st.n + 1)
                    nc.gpsimd.tensor_tensor(ve[:], mv[:, :, 1], c.eps[:], ALU.add).then_inc(ve_done, 1)
                    pool.wait_ge(ve_done, st.n + 1)
                    wait(pool, xn_done, st.n)
                    nc.gpsimd.tensor_tensor(rstd[:], ve[:], c.minus_half[:], ALU.pow).then_inc(rstd_done, 1)

                def split(st):
                    pool.wait_ge(xh_done, st.n + 1)
                    wait(pool, tr_done, st.n)
                    nc.gpsimd.tensor_tensor(xl[:], xn[:], xh[:], ALU.subtract).then_inc(xl_done, 1)

                def add_bias(st):
                    pool.wait_ge(x_in[st.s], 16 * (st.pair + 1))
                    wait(pool, xo_done, BT * (st.n - 1)) if not is_first(st) else None
                    nc.gpsimd.tensor_tensor(xb[st.s][:], x[st.s][:],
                                            c.hb2[:].unsqueeze(1).to_broadcast([P, BT, D]),
                                            ALU.add).then_inc(xb_done, 1)

                def step(st):
                    if not is_last(st, NBLOCK):
                        split(st.later(1))
                    add_bias(st)
                    if two_ahead(st):
                        rsqrt(st.later(2))

                rsqrt(Step(0, 0))
                split(Step(0, 0))
                rsqrt(Step(0, 1))
                run(pool, step)

            @block.scalar
            def _(act):
                def high(st):
                    act.wait_ge(xn_done, st.n + 1)
                    wait(act, tr_done, st.n)
                    nc.scalar.activation(xh[:], xn[:], ACT.Copy).then_inc(xh_done, 1)

                def gelu(st, f):
                    act.wait_ge(h_done, FC * st.n + f + 1)
                    if f == 0:
                        wait(act, y_done, BT * (st.n - 1)) if not is_first(st) else None
                    nc.scalar.activation(hh[st.s][:, f], ps_h[f % 4][:], ACT.Gelu, bias=c.b1[:, f:f + 1])
                    nc.scalar.activation(ps_h[f % 4][:], ps_h[f % 4][:], ACT.Gelu,
                                         bias=c.b1[:, f:f + 1]).then_inc(g_done, 1)

                def store(st):
                    wait(act, xo_done, BT * (st.n + 1))
                    act.dma_start(o_v[st.n], xo[st.s][:]).then_inc(stored[st.s], 16)

                def step(st):
                    late = st.later(-2)
                    for f in range(FC):
                        gelu(st, f)
                        if f == 2 and not (isinstance(st.n, int) and st.n < 2):
                            store(late)
                        if f == 0 and not is_last(st, NBLOCK):
                            high(st.later(1))

                high(Step(0, 0))
                run(act, step)
                store(Step(NBLOCK // 2 - 1, 0))
                store(Step(NBLOCK // 2 - 1, 1))
                for s in range(2):
                    act.wait_ge(stored[s], 16 * NBLOCK // 2)

            @block.tensor
            def _(pe):
                def turn(st):
                    pe.wait_ge(xh_done, st.n + 1)
                    pe.wait_ge(xl_done, st.n + 1)
                    wait(pe, xT_done, 2 * st.n)
                    for i, part in enumerate((xh, xl)):
                        for d in range(DC):
                            for t in range(BT):
                                ins = nc.tensor.transpose(ps_t[i][:, d, t * P:(t + 1) * P],
                                                          part[:, t, d * P:(d + 1) * P], c.ident16[:])
                    ins.then_inc(tr_done, 1)

                def first_product(st, f):
                    if f == 0:
                        pe.wait_ge(xT_done, 2 * (st.n + 1))
                    if not (is_first(st) and f < 4):
                        pe.wait_ge(hl_done, FC * st.n + f - 3)
                    k = 0
                    for d in range(DC):
                        for part in (xTh, xTl):
                            ins = nc.tensor.matmul(ps_h[f % 4][:], c.w1[:, d, f * P:(f + 1) * P], part[st.s][:, d],
                                                   start=(k == 0), stop=(k == 2 * DC - 1))
                            k += 1
                    ins.then_inc(h_done, 1)

                def second_product(st, t, half):
                    if t == 0 and half == 0:
                        pe.wait_ge(hl_done, FC * (st.n + 1))
                    if half == 0 and not (is_first(st) and t < 2):
                        pe.wait_ge(xo_done, BT * st.n + t - 1)
                    for f in range(half * FC // 2, (half + 1) * FC // 2):
                        for part in (hh, hl):
                            ins = nc.tensor.matmul(ps_y[t % 2][:], part[st.s][:, f, t * P:(t + 1) * P], c.w2[:, f],
                                                   start=(f == 0 and part is hh), stop=(f == FC - 1 and part is hl))
                    if half:
                        ins.then_inc(y_done, 1)

                def step(st):
                    first, last, prev = is_first(st), is_last(st, NBLOCK), st.later(-1)
                    for f in range(FC):
                        first_product(st, f)
                        if not first and f > 0:
                            second_product(prev, (f - 1) // 2, (f - 1) % 2)
                        if f == 5 and not last:
                            turn(st.later(1))
                    if not first:
                        second_product(prev, BT - 1, 1)

                turn(Step(0, 0))
                run(pe, step)
                for t in range(BT):
                    for half in range(2):
                        second_product(Step((NBLOCK - 1) // 2, (NBLOCK - 1) % 2), t, half)


def project(nc, x1, m, c, a):
    HC = CHUNKS // 2
    NSTEP = 2 * BATCH
    x_v = x1.rearrange("(n c t) d -> n t c d", c=HC, t=P)
    qT_v, uT_v, vs_v = (y.rearrange("(c b) i j -> b i c j", b=BATCH) for y in (m.qT, m.uT, m.vs))
    with ExitStack() as ctx:
        def sb(what, shape, dt=F32):
            return ctx.enter_context(nc.sbuf_tensor(f"proj_{what}", shape, dt))

        def psum(what, shape, dt=F32):
            return ctx.enter_context(nc.psum_tensor(f"proj_{what}", shape, dt))

        def sem(what):
            return ctx.enter_context(nc.semaphore(f"proj_{what}"))

        w = sb("wqkv", [P, DC, 3 * H])
        bias = sb("bqkv", [P, 3 * H])
        x = [sb(f"x{s}", [P, HC, D]) for s in range(2)]
        bn = sb("bn", [P, HC, 6])
        gate = sb("gate", [P, 1])
        mv = sb("mean_var", [P, HC, 2])
        ve = sb("var_eps", [P, HC])
        rstd = sb("rstd", [P, HC])
        xn = sb("xn", [P, HC, D])
        aT = sb("aT", [P, HC, DC, P])
        qkv = [sb(f"qkv{s}", [P, HC, 3 * H]) for s in range(2)]
        junk = sb("junk", [P, HC, H])
        junk_v = sb("junk_v", [P, HC, H])
        ksq = sb("k_squared", [P, HC])
        kq = sb("k_dot_q", [P, HC])
        norm = sb("k_norm", [P, HC])
        norm_eps = sb("k_norm_eps", [P, HC])
        rnorm = sb("k_norm_inverse", [P, HC])
        u = [sb(f"u{s}", [P, HC, H]) for s in range(2)]
        vs = [sb(f"v_scaled{s}", [P, HC, H]) for s in range(2)]
        qT = [sb(f"qT{s}", [P, HC, P]) for s in range(2)]
        uT = [sb(f"uT{s}", [P, HC, P]) for s in range(2)]
        ps_a = psum("ps_a", [P, HC, DC, P])
        ps_q = [psum(f"ps_q{i}", [P, 512]) for i in range(2)]
        ps_x = [psum(f"ps_x{i}", [P, HC, P]) for i in range(2)]
        ps_p = psum("ps_p", [P, HC, P])

        w_in = sem("w_in")
        x_in = [sem(f"x_in{s}") for s in range(2)]
        kk_start = sem("kk_start")
        bn_done = sem("bn_done")
        stats_done = sem("stats_done")
        ve_done = sem("ve_done")
        rstd_done = sem("rstd_done")
        xn_done = sem("xn_done")
        ta_done = sem("ta_done")
        aT_done = sem("aT_done")
        q_done = sem("q_done")
        qkv_done = sem("qkv_done")
        ksq_done = sem("ksq_done")
        kq_done = sem("kq_done")
        norm_done = sem("norm_done")
        norm_eps_done = sem("norm_eps_done")
        rnorm_done = sem("rnorm_done")
        u_done = sem("u_done")
        vs_done = sem("vs_done")
        tx_done = sem("tx_done")
        qT_done = sem("qT_done")
        uT_done = sem("uT_done")
        p_done = sem("p_done")
        kk_done = sem("kk_done")
        stored = [sem(f"stored{s}") for s in range(2)]

        def stage(st, lag, what):
            at = st.later(lag)
            if not isinstance(at.n, int) or 0 <= at.n < NSTEP:
                what(at)

        def run(eng, step):
            steps(eng, NSTEP + 2, step, head=5, tail=3)

        with nc.Block() as block:
            @block.sync
            def _(sp):
                def load(st):
                    if not (isinstance(st.n, int) and st.n < 2):
                        wait(sp, xn_done, st.n - 1)
                    sp.dma_start(x[st.s][:], x_v[st.n]).then_inc(x_in[st.s], 16)

                def store(st):
                    lo, hi = HC * st.s, HC * st.s + HC
                    sp.wait_ge(vs_done, st.n + 1)
                    sp.dma_start(vs_v[st.pair, :, lo:hi], vs[st.s][:]).then_inc(stored[st.s], 16)
                    sp.wait_ge(qT_done, st.n + 1)
                    sp.dma_start(qT_v[st.pair, :, lo:hi], qT[st.s][:]).then_inc(stored[st.s], 16)
                    sp.wait_ge(uT_done, st.n + 1)
                    sp.dma_start(uT_v[st.pair, :, lo:hi], uT[st.s][:]).then_inc(stored[st.s], 16)

                def step(st):
                    stage(st, 1, load)
                    stage(st, -2, store)

                sp.dma_start(w[:], a["WqkvT"].rearrange("(c p) n -> p c n", p=P)).then_inc(w_in, 16)
                sp.dma_start(bias[:], a["bqkv"].partition_broadcast(P)).then_inc(w_in, 16)
                load(Step(0, 0))
                run(sp, step)
                for s in range(2):
                    sp.wait_ge(stored[s], 48 * NSTEP // 2)

            @block.vector
            def _(v):
                def stats(st):
                    v.wait_ge(x_in[st.s], 16 * (st.pair + 1))
                    for t in range(HC):
                        i = nc.vector.bn_stats(bn[:, t], x[st.s][:, t])
                    i.then_inc(bn_done, 1)
                    v.wait_ge(bn_done, st.n + 1)
                    wait(v, rstd_done, st.n)
                    nc.vector.memset(gate[:], 0.0)
                    for t in range(HC):
                        i = nc.vector.bn_aggr(mv[:, t], bn[:, t])
                    i.then_inc(stats_done, 1)

                def normalise(st):
                    v.wait_ge(rstd_done, st.n + 1)
                    wait(v, ta_done, st.n)
                    for t in range(HC):
                        i = nc.vector.tensor_scalar(xn[:, t], x[st.s][:, t], mv[:, t, 0:1], rstd[:, t:t + 1],
                                                    ALU.subtract, ALU.mult)
                    i.then_inc(xn_done, 1)

                def add_bias(st, half):
                    if not half and not is_first(st):
                        wait(v, tx_done, st.n - 1)
                        wait(v, vs_done, st.n - 1)
                        wait(v, u_done, st.n - 1)
                    for j in range(2 * half, 2 * half + 2):
                        v.wait_ge(q_done, HC * st.n + j + 1)
                        nc.vector.tensor_tensor(qkv[st.s][:, j], ps_q[j % 2][:, :3 * H], bias[:],
                                                ALU.add).then_inc(qkv_done, 1)

                def k_dot_q(st):
                    v.wait_ge(qkv_done, HC * (st.n + 1))
                    wait(v, vs_done, st.n)
                    for j in range(HC):
                        i = nc.vector.tensor_tensor_reduce(junk_v[:, j], qkv[st.s][:, j, 0:H],
                                                           qkv[st.s][:, j, H:2 * H],
                                                           1.0, 0.0, ALU.mult, ALU.add, kq[:, j:j + 1])
                    i.then_inc(kq_done, 1)

                def invert_norm(st):
                    v.wait_ge(norm_done, st.n + 1)
                    wait(v, u_done, st.n)
                    nc.vector.tensor_scalar(norm_eps[:], norm[:], NORM_EPS, None, ALU.add).then_inc(norm_eps_done, 1)
                    v.wait_ge(norm_eps_done, st.n + 1)
                    nc.vector.reciprocal(rnorm[:], norm_eps[:]).then_inc(rnorm_done, 1)

                def prefix(st):
                    v.wait_ge(p_done, st.n + 1)
                    for j in range(HC):
                        chunk = HC * st.s + j
                        if chunk == CHUNKS - 1:
                            nc.vector.memset(gate[:], 0.0).then_inc(kk_done, 1)
                            break
                        wait(v, kk_done, HC * st.n + j)
                        nc.vector.tensor_tensor(m.KK[:, bass.ds(st.pair + (chunk + 1) * BATCH, 1), :],
                                                ps_p[:, j:j + 1], m.KK[:, bass.ds(st.pair + chunk * BATCH, 1), :],
                                                ALU.add).then_inc(kk_done, 1)

                def step(st):
                    stage(st, 0, stats)
                    stage(st, -1, lambda x: add_bias(x, 0))
                    stage(st, 0, normalise)
                    stage(st, -1, lambda x: add_bias(x, 1))
                    stage(st, -1, k_dot_q)
                    stage(st, -2, prefix)
                    stage(st, -1, invert_norm)

                for b in range(BATCH):
                    i = nc.vector.tensor_copy(m.KK[:, b], c.ident[:])
                i.then_inc(kk_start, 1)
                v.wait_ge(kk_start, 1)
                v.wait_ge(w_in, 32)
                run(v, step)

            @block.gpsimd
            def _(pool):
                def rsqrt(st):
                    pool.wait_ge(stats_done, st.n + 1)
                    nc.gpsimd.tensor_tensor(ve[:], mv[:, :, 1], c.eps[:], ALU.add).then_inc(ve_done, 1)
                    pool.wait_ge(ve_done, st.n + 1)
                    wait(pool, xn_done, st.n)
                    nc.gpsimd.tensor_tensor(rstd[:], ve[:], c.minus_half[:], ALU.pow).then_inc(rstd_done, 1)

                def root(st):
                    pool.wait_ge(ksq_done, st.n + 1)
                    wait(pool, norm_eps_done, st.n)
                    nc.gpsimd.tensor_tensor(norm[:], ksq[:], c.plus_half[:], ALU.pow).then_inc(norm_done, 1)

                def scale_v(st):
                    pool.wait_ge(kq_done, st.n + 1)
                    wait(pool, stored[st.s], 48 * st.pair)
                    nc.gpsimd.tensor_tensor(vs[st.s][:], qkv[st.s][:, :, 2 * H:],
                                            kq[:].unsqueeze(2).to_broadcast([P, HC, H]),
                                            ALU.mult).then_inc(vs_done, 1)

                def step(st):
                    stage(st, 0, rsqrt)
                    stage(st, -1, root)
                    stage(st, -1, scale_v)

                nc.gpsimd.memset(m.Tn[:], 0.0)
                nc.gpsimd.memset(m.Tt[:], 0.0)
                run(pool, step)

            @block.scalar
            def _(act):
                def copy_aT(st):
                    act.wait_ge(ta_done, st.n + 1)
                    wait(act, q_done, HC * st.n)
                    for i in range(2):
                        nc.scalar.activation(aT[:, 2 * i:2 * i + 2], ps_a[:, 2 * i:2 * i + 2],
                                             ACT.Copy).then_inc(aT_done, 1)

                def square(st):
                    wait(act, norm_done, st.n)
                    for j in range(HC):
                        act.wait_ge(qkv_done, HC * st.n + j + 1)
                        i = nc.scalar.activation(junk[:, j], qkv[st.s][:, j, H:2 * H], ACT.Square,
                                                 accum_out=ksq[:, j:j + 1])
                    i.then_inc(ksq_done, 1)

                def scale_u(st):
                    act.wait_ge(rnorm_done, st.n + 1)
                    if not is_first(st):
                        wait(act, p_done, st.n - 1)
                    for j in range(HC):
                        i = nc.scalar.activation(u[st.s][:, j], qkv[st.s][:, j, H:2 * H], ACT.Copy,
                                                 scale=rnorm[:, j:j + 1])
                    i.then_inc(u_done, 1)

                def copy_qu(st):
                    act.wait_ge(tx_done, st.n + 1)
                    wait(act, stored[st.s], 48 * st.pair)
                    nc.scalar.activation(qT[st.s][:], ps_x[0][:], ACT.Copy).then_inc(qT_done, 1)
                    nc.scalar.activation(uT[st.s][:], ps_x[1][:], ACT.Copy).then_inc(uT_done, 1)

                def step(st):
                    stage(st, -1, square)
                    stage(st, 0, copy_aT)
                    stage(st, -2, copy_qu)
                    stage(st, -1, scale_u)

                run(act, step)

            @block.tensor
            def _(pe):
                def turn_a(st):
                    pe.wait_ge(xn_done, st.n + 1)
                    wait(pe, aT_done, 2 * st.n)
                    for j in range(HC):
                        for d in range(DC):
                            i = nc.tensor.transpose(ps_a[:, j, d], xn[:, j, d * P:(d + 1) * P], c.ident[:])
                    i.then_inc(ta_done, 1)

                def products(st):
                    pe.wait_ge(aT_done, 2 * (st.n + 1))
                    for j in range(HC):
                        if not (is_first(st) and j < 2):
                            pe.wait_ge(qkv_done, HC * st.n + j - 1)
                        for d in range(DC):
                            i = nc.tensor.matmul(ps_q[j % 2][:, :3 * H], aT[:, j, d], w[:, d],
                                                 start=(d == 0), stop=(d == DC - 1))
                        i.then_inc(q_done, 1)

                def turn_qu(st):
                    pe.wait_ge(u_done, st.n + 1)
                    wait(pe, qT_done, st.n)
                    wait(pe, uT_done, st.n)
                    for j in range(HC):
                        nc.tensor.transpose(ps_x[0][:, j], qkv[st.s][:, j, 0:H], c.ident[:])
                        i = nc.tensor.transpose(ps_x[1][:, j], u[st.s][:, j], c.ident[:])
                    i.then_inc(tx_done, 1)

                def squares(st):
                    wait(pe, kk_done, HC * st.n)
                    for j in range(HC):
                        i = nc.tensor.matmul(ps_p[:, j], u[st.s][:, j], u[st.s][:, j], start=True, stop=True)
                    i.then_inc(p_done, 1)

                def step(st):
                    stage(st, -1, products)
                    stage(st, 0, turn_a)
                    stage(st, -2, turn_qu)
                    stage(st, -2, squares)

                pe.wait_ge(w_in, 32)
                run(pe, step)


LEAF, SCHUR, JOIN = "leaf", "schur", "join"
PLAN = [(LEAF, 0, 32), (SCHUR, 0, 32), (LEAF, 32, 32), (JOIN, 0, 32), (SCHUR, 0, 64),
        (LEAF, 64, 32), (SCHUR, 64, 32), (LEAF, 96, 32), (JOIN, 64, 32), (JOIN, 0, 64)]


def groups_of(w):
    n = 512 // w
    return n, NP // n


def done_before(kind, index):
    return sum(1 if kind == LEAF else groups_of(w)[1] for k, _, w in PLAN[:index] if k == kind)


def factorise(nc, name, m, c):
    with ExitStack() as ctx:
        def sb(what, shape, dt=F32):
            return ctx.enter_context(nc.sbuf_tensor(f"{name}_{what}", shape, dt))

        def psum(what, shape, dt=F32):
            return ctx.enter_context(nc.psum_tensor(f"{name}_{what}", shape, dt))

        def sem(what):
            return ctx.enter_context(nc.semaphore(f"{name}_{what}"))

        KK, Tn, Tt, dinv, ndinv = m.KK, m.Tn, m.Tt, m.dinv, m.ndinv
        RW = W // 2
        lane_ident = sb("lane_ident", [P, RW, W])
        R = sb("lane_rows", [P, W, 2 * W])
        prod = sb("rank_one", [P, RW, W + 1])
        mult = [sb(f"multipliers{i}", [P, W]) for i in range(2)]
        dl = sb("lane_dinv", [P, W])
        Y = [sb(f"Y{i}", [P, 512]) for i in range(2)]
        V = [sb(f"V{i}", [P, 512]) for i in range(2)]
        Yd = {32: sb("Yd32", [P, NP, 32]), 64: sb("Yd64", [64, NP, 64])}
        ps_lane = psum("ps_lane", [P, 2, 512])
        M = ps_lane[:].rearrange("p a (b x) -> p (a b) x", x=2 * W)
        ps = [psum(f"ps{i}", [P, 512]) for i in range(4)]

        init_done = sem("init_done")
        leaf_odd = sem("leaf_odd")
        leaf_in = sem("leaf_in")
        leaf_T = sem("leaf_T")
        chain = sem("lane_chain")
        leaf_done = sem("leaf_done")
        out_done = sem("out_done")
        out_dve = sem("out_dve")
        out_act = sem("out_act")
        y_done = sem("y_done")
        y_copied = sem("y_copied")
        yd_done = sem("yd_done")
        s_done = sem("s_done")
        kk_done = sem("kk_done")
        v_done = sem("v_done")
        v_copied = sem("v_copied")
        j_done = sem("j_done")
        tn_done = sem("tn_done")
        tt_done = sem("tt_done")

        def span(o, w):
            return slice(o, o + w)

        with nc.Block() as block:
            @block.gpsimd
            def _(pool):
                nc.gpsimd.memset(lane_ident[:], 0.0).then_inc(init_done, 1)
                pool.wait_ge(init_done, 1)
                for h in range(2):
                    half = lane_ident[h * NP:(h + 1) * NP]
                    nc.gpsimd.affine_select(out=half, in_=half, compare_op=ALU.not_equal, fill=1.0, base=h,
                                            pattern=[[2, RW], [-1, W]], channel_multiplier=0).then_inc(init_done, 1)

            @block.vector
            def _(v):
                links = [0]

                def note(ins):
                    links[0] += 1
                    ins.then_inc(chain, 1)
                    return links[0]

                def link(ins):
                    v.wait_ge(chain, note(ins))

                def multipliers(j):
                    for h in range(2):
                        lanes = slice(h * NP, (h + 1) * NP)
                        i = nc.vector.tensor_scalar(mult[j % 2][lanes, j + 1 - h:W - h], R[lanes, j, j + 1:W],
                                                    dl[lanes, j:j + 1], -1.0, ALU.mult, ALU.mult)
                    note(i)

                def leaf(index, o):
                    r = done_before(LEAF, index)
                    v.wait_ge(leaf_in, r + 1)
                    v.wait_ge(leaf_T, r + 1)
                    if r:
                        v.wait_ge(out_done, 9 * r)
                    for h in range(2):
                        i = nc.vector.tensor_copy(R[h * NP:(h + 1) * NP, 0], M[0:NP, 0])
                    link(i)
                    link(nc.vector.reciprocal(dl[:, 0:1], R[:, 0, 0:1]))
                    multipliers(0)
                    for j in range(W - 1):
                        v.wait_ge(chain, links[0])
                        own = ((j + 1) % 2) * NP
                        for h in range(2):
                            lanes = slice(h * NP, (h + 1) * NP)
                            i = nc.vector.scalar_tensor_tensor(
                                out=R[lanes, j + 1, j + 1:], in0=R[lanes, j, j + 1:],
                                scalar=mult[j % 2][lanes, j + 1 - h:j + 2 - h],
                                in1=M[own:own + NP, (j + 1) // 2, j + 1:], op0=ALU.mult, op1=ALU.add)
                        row = note(i)
                        r0 = (j + 2) // 2
                        n = RW - r0
                        window = slice(j + 1, W + j + 1)
                        shape = [P, n, W]
                        if n:
                            i = nc.vector.tensor_tensor(prod[:, :n, :W],
                                                        mult[j % 2][:, 2 * r0::2].unsqueeze(2).to_broadcast(shape),
                                                        R[:, j:j + 1, window].to_broadcast(shape), ALU.mult)
                            product = note(i)
                        v.wait_ge(chain, row)
                        i = nc.vector.reciprocal(dl[:, j + 1:j + 2], R[:, j + 1, j + 1:j + 2])
                        inverse = note(i)
                        if n:
                            v.wait_ge(chain, product)
                            note(nc.vector.tensor_tensor(M[:, r0:, window], M[:, r0:, window], prod[:, :n, :W], ALU.add))
                        v.wait_ge(chain, inverse)
                        if j < W - 2:
                            multipliers(j + 1)
                    nc.vector.memset(R[:, 0, 0:1], 0.0).then_inc(leaf_done, 1)
                    v.wait_ge(out_done, 9 * r + 1)
                    nc.vector.tensor_copy(dinv[span(o, W)], ps[0][0:W, 0:NP])
                    nc.vector.tensor_scalar(ndinv[span(o, W)], ps[0][0:W, 0:NP], -1.0, None,
                                            ALU.mult).then_inc(out_dve, 1)
                    for q in range(4):
                        v.wait_ge(out_done, 9 * r + 3 + 2 * q)
                        at = o + 8 * q
                        nc.vector.tensor_copy(Tn[span(o, W), :, at:at + 8],
                                              ps[(2 + 2 * q) % 4][0:W].rearrange("i (j p) -> i p j", j=8)
                                              ).then_inc(out_dve, 1)

                def schur(index, o, w):
                    n, count = groups_of(w)
                    base = done_before(SCHUR, index)
                    b1, b2 = span(o, w), span(o + w, w)

                    def scale(g):
                        pr = slice(g * n, g * n + n)
                        v.wait_ge(y_copied, base + g + 1)
                        nc.vector.tensor_tensor(Yd[w][b1, pr], ps[g % 2][b1].rearrange("i (p j) -> i p j", p=n),
                                                ndinv[b1, pr].unsqueeze(2).to_broadcast([w, n, w]),
                                                ALU.mult).then_inc(yd_done, 1)

                    def update(g):
                        pr = slice(g * n, g * n + n)
                        v.wait_ge(s_done, base + g + 1)
                        nc.vector.tensor_tensor(KK[b2, pr, b2], ps[2 + g % 2][b2].rearrange("i (p j) -> i p j", p=n),
                                                KK[b2, pr, b2], ALU.add).then_inc(kk_done, 1)

                    v.wait_ge(chain, links[0])
                    v.wait_ge(out_dve, 5 * done_before(LEAF, index))
                    scale(0)
                    for g in range(count):
                        if g + 1 < count:
                            scale(g + 1)
                        update(g)

                def join(index, o, w):
                    n, count = groups_of(w)
                    base = done_before(JOIN, index)
                    b1, b2 = span(o, w), span(o + w, w)
                    for g in range(count):
                        pr = slice(g * n, g * n + n)
                        v.wait_ge(j_done, base + g + 1)
                        nc.vector.tensor_copy(Tn[b2, pr, b1], ps[2 + g % 2][b2].rearrange("i (p j) -> i p j", p=n)
                                              ).then_inc(tn_done, 1)

                for index, (kind, o, w) in enumerate(PLAN):
                    if kind == LEAF:
                        leaf(index, o)
                    elif kind == SCHUR:
                        schur(index, o, w)
                    else:
                        join(index, o, w)

            @block.scalar
            def _(act):
                def leaf(index, o):
                    r = done_before(LEAF, index)
                    if r == 0:
                        act.wait_ge(init_done, 3)
                    else:
                        act.wait_ge(leaf_done, r)
                    act.wait_ge(leaf_odd, r + 1)
                    nc.scalar.activation(M[NP:, :, 0:W], ps[3][0:NP].rearrange("p (r x) -> p r x", x=W), ACT.Copy)
                    act.wait_ge(leaf_in, r + 1)
                    nc.scalar.activation(M[:, :, W:], lane_ident[:], ACT.Copy).then_inc(leaf_T, 1)
                    for q in range(4):
                        act.wait_ge(out_done, 9 * r + 2 + 2 * q)
                        at = o + 8 * q
                        nc.scalar.activation(Tt[span(o, W), :, at:at + 8],
                                             ps[(1 + 2 * q) % 4][0:W].rearrange("j (i p) -> j p i", i=8),
                                             ACT.Copy).then_inc(out_act, 1)

                def schur(index, o, w):
                    n, count = groups_of(w)
                    base = done_before(SCHUR, index)
                    b1 = span(o, w)
                    for g in range(count):
                        act.wait_ge(y_done, base + g + 1)
                        if base + g > 1:
                            act.wait_ge(s_done, base + g - 1)
                        nc.scalar.activation(Y[g % 2][b1], ps[g % 2][b1], ACT.Copy).then_inc(y_copied, 1)

                def join(index, o, w):
                    n, count = groups_of(w)
                    base = done_before(JOIN, index)
                    b1, b2 = span(o, w), span(o + w, w)

                    def copy_v(g):
                        act.wait_ge(v_done, base + g + 1)
                        if base + g > 1:
                            act.wait_ge(j_done, base + g - 1)
                        nc.scalar.activation(V[g % 2][b2], ps[g % 2][b2], ACT.Copy).then_inc(v_copied, 1)

                    copy_v(0)
                    for g in range(count):
                        if g + 1 < count:
                            copy_v(g + 1)
                        pr = slice(g * n, g * n + n)
                        act.wait_ge(j_done, base + g + 1)
                        nc.scalar.activation(Tt[b1, pr, b2], ps_lane[b1, g % 2].rearrange("i (p j) -> i p j", p=n),
                                             ACT.Copy).then_inc(tt_done, 1)

                for index, (kind, o, w) in enumerate(PLAN):
                    if kind == LEAF:
                        leaf(index, o)
                    elif kind == SCHUR:
                        schur(index, o, w)
                    else:
                        join(index, o, w)

            @block.tensor
            def _(pe):
                def all_copied(index):
                    r, sc, jn = (done_before(k, index) for k in (LEAF, SCHUR, JOIN))
                    wait(pe, out_dve, 5 * r)
                    wait(pe, out_act, 4 * r)
                    wait(pe, kk_done, sc)
                    wait(pe, tn_done, jn)
                    wait(pe, tt_done, jn)

                def leaf(index, o):
                    r = done_before(LEAF, index)
                    all_copied(index)
                    b = span(o, W)
                    for h in (1, 0):
                        for j in range(RW):
                            to = ps[3][0:NP, j * W:(j + 1) * W] if h else M[0:NP, j, 0:W]
                            i = nc.tensor.transpose(to, KK[b, :, o + 2 * j + h], c.ident[b, b])
                        i.then_inc(leaf_odd if h else leaf_in, 1)
                    pe.wait_ge(leaf_done, r + 1)
                    nc.tensor.transpose(ps[0][0:W, 0:NP], dl[0:NP], c.ident[0:NP, 0:NP]).then_inc(out_done, 1)
                    for q in range(4):
                        for side in range(2):
                            bank = 1 + 2 * q + side
                            if bank == 4:
                                pe.wait_ge(out_dve, 5 * r + 1)
                            elif bank > 4 and side == 0:
                                pe.wait_ge(out_act, 4 * r + q - 1)
                            elif bank > 4:
                                pe.wait_ge(out_dve, 5 * r + q)
                            for k in range(8):
                                src = R[0:NP, 8 * q + k, W:] if side == 0 else R[0:NP, :, W + 8 * q + k]
                                i = nc.tensor.transpose(ps[bank % 4][0:W, k * NP:(k + 1) * NP], src,
                                                        c.ident[0:NP, 0:NP])
                            i.then_inc(out_done, 1)

                def schur(index, o, w):
                    n, count = groups_of(w)
                    base = done_before(SCHUR, index)
                    b1, b2 = span(o, w), span(o + w, w)
                    all_copied(index)

                    def reduce_right(g):
                        if g > 1:
                            pe.wait_ge(y_copied, base + g - 1)
                            pe.wait_ge(yd_done, base + g - 1)
                        for k in range(n):
                            p = g * n + k
                            i = nc.tensor.matmul(ps[g % 2][b1, k * w:(k + 1) * w], Tt[b1, p, b1], KK[b1, p, b2],
                                                 start=True, stop=True)
                        i.then_inc(y_done, 1)

                    reduce_right(0)
                    for g in range(count):
                        if g + 1 < count:
                            reduce_right(g + 1)
                        pe.wait_ge(y_copied, base + g + 1)
                        pe.wait_ge(yd_done, base + g + 1)
                        if g > 1:
                            pe.wait_ge(kk_done, base + g - 1)
                        for k in range(n):
                            i = nc.tensor.matmul(ps[2 + g % 2][b2, k * w:(k + 1) * w],
                                                 Y[g % 2][b1, k * w:(k + 1) * w], Yd[w][b1, g * n + k],
                                                 start=True, stop=True)
                        i.then_inc(s_done, 1)

                def join(index, o, w):
                    n, count = groups_of(w)
                    base = done_before(JOIN, index)
                    b1, b2 = span(o, w), span(o + w, w)
                    all_copied(index)

                    def first(g):
                        if g > 1:
                            pe.wait_ge(v_copied, base + g - 1)
                        for k in range(n):
                            p = g * n + k
                            i = nc.tensor.matmul(ps[g % 2][b2, k * w:(k + 1) * w], Yd[w][b1, p], Tn[b1, p, b1],
                                                 start=True, stop=True)
                        i.then_inc(v_done, 1)

                    first(0)
                    for g in range(count):
                        if g + 1 < count:
                            first(g + 1)
                        pe.wait_ge(v_copied, base + g + 1)
                        if g > 1:
                            pe.wait_ge(tn_done, base + g - 1)
                            pe.wait_ge(tt_done, base + g - 1)
                        for k in range(n):
                            nc.tensor.matmul(ps[2 + g % 2][b2, k * w:(k + 1) * w], Tt[b2, g * n + k, b2],
                                             V[g % 2][b2, k * w:(k + 1) * w], start=True, stop=True)
                        for k in range(n):
                            i = nc.tensor.matmul(ps_lane[b1, g % 2, k * w:(k + 1) * w],
                                                 V[g % 2][b2, k * w:(k + 1) * w], Tt[b2, g * n + k, b2],
                                                 start=True, stop=True)
                        i.then_inc(j_done, 1)

                for index, (kind, o, w) in enumerate(PLAN):
                    if kind == LEAF:
                        leaf(index, o)
                    elif kind == SCHUR:
                        schur(index, o, w)
                    else:
                        join(index, o, w)


def gram(nc, m, c):
    uT_v, UA_v = (y.rearrange("(g k) i j -> g i k j", k=GROUP) for y in (m.uT, m.UA))
    with ExitStack() as ctx:
        def sb(what, shape, dt=F32):
            return ctx.enter_context(nc.sbuf_tensor(f"gram_{what}", shape, dt))

        def psum(what):
            return [ctx.enter_context(nc.psum_tensor(f"gram_{what}{i}", [P, GROUP, P], F32)) for i in range(2)]

        def sem(what):
            return ctx.enter_context(nc.semaphore(f"gram_{what}"))

        group = [P, GROUP, P]
        uTa, uTb, Td, A, WW, UA = ([sb(f"{x}{s}", group) for s in range(2)]
                                   for x in ("uT_for_w", "uT_for_g", "Td", "A", "W", "UA"))
        ps_a, ps_w, ps_g, ps_u = (psum(x) for x in ("ps_a", "ps_w", "ps_g", "ps_u"))
        ua_in = [sem(f"uT_for_w_in{s}") for s in range(2)]
        ub_in = [sem(f"uT_for_g_in{s}") for s in range(2)]
        td_done, a_done, A_done, w_done, W_done, g_done, kk_done, u_done, UA_done = (
            sem(x) for x in ("td_done", "a_product", "A_done", "w_product", "W_done", "g_product", "kk_done",
                             "u_turned", "UA_done"))
        stored = [sem(f"stored{s}") for s in range(2)]

        with nc.Block() as block:
            @block.sync
            def _(sp):
                def load_a(st):
                    if not (isinstance(st.n, int) and st.n < 2):
                        wait(sp, w_done, st.n - 1)
                    sp.dma_start(uTa[st.s][:], uT_v[st.n]).then_inc(ua_in[st.s], 16)

                def load_b(st):
                    if not (isinstance(st.n, int) and st.n < 2):
                        wait(sp, g_done, st.n - 1)
                    sp.dma_start(uTb[st.s][:], uT_v[st.n]).then_inc(ub_in[st.s], 16)

                def store(st):
                    sp.wait_ge(UA_done, st.n + 1)
                    sp.dma_start(UA_v[st.n], UA[st.s][:]).then_inc(stored[st.s], 16)

                def step(st):
                    if not is_last(st, NG):
                        load_a(st.later(1))
                        load_b(st.later(1))
                    if not is_first(st):
                        store(st.later(-1))

                load_a(Step(0, 0))
                load_b(Step(0, 0))
                steps(sp, NG, step)
                store(Step(NG // 2 - 1, 1))
                for s in range(2):
                    sp.wait_ge(stored[s], 16 * NG // 2)

            @block.vector
            def _(v):
                def scale(st):
                    if not is_first(st):
                        wait(v, a_done, st.n - 1)
                    nc.vector.tensor_tensor(Td[st.s][:], m.Tn[:, bass.ds(st.n * GROUP, GROUP), :],
                                            m.dinv[:, bass.ds(st.n * GROUP, GROUP)].unsqueeze(2).to_broadcast(group),
                                            ALU.mult).then_inc(td_done, 1)

                def copy_w(st):
                    v.wait_ge(w_done, st.n + 1)
                    if not is_first(st):
                        wait(v, g_done, st.n - 1)
                        wait(v, u_done, st.n - 1)
                    nc.vector.tensor_copy(WW[st.s][:], ps_w[st.s][:]).then_inc(W_done, 1)

                def add_identity(st):
                    v.wait_ge(g_done, st.n + 1)
                    nc.vector.tensor_tensor(m.KK[:, bass.ds(st.n * GROUP, GROUP), :], ps_g[st.s][:],
                                            c.ident[:].unsqueeze(1).to_broadcast(group),
                                            ALU.add).then_inc(kk_done, 1)

                def step(st):
                    if not is_last(st, NG):
                        scale(st.later(1))
                    copy_w(st)
                    if not is_first(st):
                        add_identity(st.later(-1))

                scale(Step(0, 0))
                steps(v, NG, step)
                add_identity(Step(NG // 2 - 1, 1))

            @block.scalar
            def _(act):
                def copy_a(st):
                    act.wait_ge(a_done, st.n + 1)
                    if not is_first(st):
                        wait(act, w_done, st.n - 1)
                    nc.scalar.activation(A[st.s][:], ps_a[st.s][:], ACT.Copy).then_inc(A_done, 1)

                def copy_ua(st):
                    act.wait_ge(u_done, st.n + 1)
                    wait(act, stored[st.s], 16 * st.pair)
                    nc.scalar.activation(UA[st.s][:], ps_u[st.s][:], ACT.Copy).then_inc(UA_done, 1)

                def step(st):
                    if not is_last(st, NG):
                        copy_a(st.later(1))
                    if not is_first(st):
                        copy_ua(st.later(-1))

                copy_a(Step(0, 0))
                steps(act, NG, step)
                copy_ua(Step(NG // 2 - 1, 1))

            @block.tensor
            def _(pe):
                def inverse(st):
                    pe.wait_ge(td_done, st.n + 1)
                    if not is_first(st):
                        wait(pe, A_done, st.n - 1)
                    for k in range(GROUP):
                        i = nc.tensor.matmul(ps_a[st.s][:, k], Td[st.s][:, k], m.Tn[:, bass.ds(st.n * GROUP + k, 1), :],
                                             start=True, stop=True)
                    i.then_inc(a_done, 1)

                def times_u(st):
                    pe.wait_ge(ua_in[st.s], 16 * (st.pair + 1))
                    pe.wait_ge(A_done, st.n + 1)
                    if not is_first(st):
                        wait(pe, W_done, st.n - 1)
                    for k in range(GROUP):
                        i = nc.tensor.matmul(ps_w[st.s][:, k], A[st.s][:, k], uTa[st.s][:, k], start=True, stop=True)
                    i.then_inc(w_done, 1)

                def products(st):
                    pe.wait_ge(ub_in[st.s], 16 * (st.pair + 1))
                    pe.wait_ge(W_done, st.n + 1)
                    if not is_first(st):
                        wait(pe, kk_done, st.n - 1)
                        wait(pe, UA_done, st.n - 1)
                    for k in range(GROUP):
                        i = nc.tensor.matmul(ps_g[st.s][:, k], uTb[st.s][:, k], WW[st.s][:, k], start=True, stop=True)
                    i.then_inc(g_done, 1)
                    for k in range(GROUP):
                        i = nc.tensor.transpose(ps_u[st.s][:, k], WW[st.s][:, k], c.ident[:])
                    i.then_inc(u_done, 1)

                def step(st):
                    if not is_last(st, NG):
                        inverse(st.later(1))
                    times_u(st)
                    if not is_first(st):
                        products(st.later(-1))

                inverse(Step(0, 0))
                steps(pe, NG, step)
                products(Step(NG // 2 - 1, 1))


def outputs(nc, x1, x2, m, c, a):
    x_v, o_v = (y.rearrange("(b c t) d -> c t b d", b=BATCH, t=P) for y in (x1, x2))
    UA_v, qT_v, vs_v = (y.rearrange("(g k) i j -> g i k j", k=GROUP) for y in (m.UA, m.qT, m.vs))
    with ExitStack() as ctx:
        def sb(what, shape, dt=F32):
            return ctx.enter_context(nc.sbuf_tensor(f"out_{what}", shape, dt))

        def psum(what, shape):
            return ctx.enter_context(nc.psum_tensor(f"out_{what}", shape, F32))

        def sem(what):
            return ctx.enter_context(nc.semaphore(f"out_{what}"))

        group = [P, GROUP, P]
        wide = [P, GROUP, D]
        UA, qT, v0, vd, zT, zn, sc, oT, M = ([sb(f"{x}{s}", group) for s in range(2)]
                                             for x in ("UA", "qT", "v", "v_over_d", "zT", "z", "scores", "oT", "M"))
        x, xb, xo = ([sb(f"{y}{s}", wide) for s in range(2)] for y in ("x", "x_plus_bias", "x_out"))
        dcol = [sb(f"dcol{s}", [P, GROUP]) for s in range(2)]
        wo = sb("wo", [P, D])
        bo = sb("bo", [P, D])
        ps_z, ps_s, ps_n, ps_o, ps_m = (psum(y, group) for y in ("ps_z", "ps_s", "ps_n", "ps_o", "ps_m"))
        ps_r = psum("ps_r", wide)
        w_in = sem("w_in")
        UA_in, q_in, v_in, x_in, stored = ([sem(f"{y}{s}") for s in range(2)]
                                           for y in ("UA_in", "q_in", "v_in", "x_in", "stored"))
        (M_zero, dcol_done, vd_done, xb_done, z_done, zT_done, s_done, sc_done, n_done, zn_done, o_done, oT_done,
         m_done, M_done, r_done, xo_done) = (
            sem(y) for y in ("M_zero", "dcol_done", "vd_done", "xb_done", "z_product", "zT_done", "s_product",
                             "sc_done", "z_turned", "zn_done", "o_product", "oT_done", "m_product", "M_done",
                             "r_product", "xo_done"))

        with nc.Block() as block:
            @block.sync
            def _(sp):
                def load(st, tiles, src, landed, used):
                    if not (isinstance(st.n, int) and st.n < 2):
                        wait(sp, used, st.n - 1)
                    sp.dma_start(tiles[st.s][:], src).then_inc(landed[st.s], 16)

                def load_ua(st):
                    load(st, UA, UA_v[st.n], UA_in, z_done)

                def load_rest(st):
                    load(st, v0, vs_v[st.n], v_in, vd_done)
                    load(st, qT, qT_v[st.n], q_in, o_done)
                    load(st, x, x_v[st.pair, :, GROUP * st.s:GROUP * st.s + GROUP], x_in, xb_done)

                def step(st):
                    if not is_last(st, NG):
                        load_ua(st.later(1))
                        load_rest(st.later(1))

                sp.dma_start(wo[:], a["WoT"]).then_inc(w_in, 16)
                sp.dma_start(bo[:], a["bo"].partition_broadcast(P)).then_inc(w_in, 16)
                load_ua(Step(0, 0))
                load_rest(Step(0, 0))
                steps(sp, NG, step)

            @block.gpsimd
            def _(pool):
                def scale_v(st):
                    pool.wait_ge(v_in[st.s], 16 * (st.pair + 1))
                    pool.wait_ge(dcol_done, st.n + 1)
                    if not is_first(st):
                        wait(pool, m_done, st.n - 1)
                    nc.gpsimd.tensor_tensor(vd[st.s][:], v0[st.s][:], dcol[st.s][:].unsqueeze(2).to_broadcast(group),
                                            ALU.mult).then_inc(vd_done, 1)

                def add_bias(st):
                    pool.wait_ge(x_in[st.s], 16 * (st.pair + 1))
                    if not is_first(st):
                        wait(pool, xo_done, st.n - 1)
                    nc.gpsimd.tensor_tensor(xb[st.s][:], x[st.s][:], bo[:].unsqueeze(1).to_broadcast(wide),
                                            ALU.add).then_inc(xb_done, 1)

                def step(st):
                    if not is_last(st, NG):
                        scale_v(st.later(1))
                    add_bias(st)

                pool.wait_ge(w_in, 32)
                scale_v(Step(0, 0))
                steps(pool, NG, step)

            @block.vector
            def _(v):
                def pick_d(st):
                    if not is_first(st):
                        wait(v, vd_done, st.n - 1)
                    nc.vector.tensor_copy(dcol[st.s][:], m.dinv[:, bass.ds(st.n * GROUP, GROUP)]
                                          ).then_inc(dcol_done, 1)

                def mask(st):
                    v.wait_ge(s_done, st.n + 1)
                    if not is_first(st):
                        wait(v, o_done, st.n - 1)
                    nc.vector.tensor_tensor(sc[st.s][:], ps_s[:], c.causal[:].unsqueeze(1).to_broadcast(group),
                                            ALU.mult).then_inc(sc_done, 1)

                def update(st):
                    v.wait_ge(m_done, st.n + 1)
                    nc.vector.tensor_tensor(M[st.s][:], ps_m[:], M[st.s][:], ALU.add).then_inc(M_done, 1)

                def residual(st):
                    v.wait_ge(r_done, st.n + 1)
                    v.wait_ge(xb_done, st.n + 1)
                    wait(v, stored[st.s], 16 * st.pair)
                    nc.vector.tensor_tensor(xo[st.s][:], ps_r[:], xb[st.s][:], ALU.add).then_inc(xo_done, 1)

                def step(st):
                    if not is_last(st, NG):
                        pick_d(st.later(1))
                    mask(st)
                    if not is_first(st):
                        residual(st.later(-1))
                    update(st)

                for s in range(2):
                    nc.vector.memset(M[s][:], 0.0).then_inc(M_zero, 1)
                v.wait_ge(M_zero, 2)
                pick_d(Step(0, 0))
                steps(v, NG, step)
                residual(Step(NG // 2 - 1, 1))

            @block.scalar
            def _(act):
                def copy(st, dst, src, made, used, done):
                    act.wait_ge(made, st.n + 1)
                    if not is_first(st):
                        wait(act, used, st.n - 1)
                    nc.scalar.activation(dst[st.s][:], src[:], ACT.Copy).then_inc(done, 1)

                def store(st):
                    act.wait_ge(xo_done, st.n + 1)
                    act.dma_start(o_v[st.pair, :, GROUP * st.s:GROUP * st.s + GROUP], xo[st.s][:]
                                  ).then_inc(stored[st.s], 16)

                def step(st):
                    if not is_last(st, NG):
                        copy(st.later(1), zT, ps_z, z_done, n_done, zT_done)
                    copy(st, zn, ps_n, n_done, m_done, zn_done)
                    if not is_first(st):
                        store(st.later(-1))
                    copy(st, oT, ps_o, o_done, r_done, oT_done)

                copy(Step(0, 0), zT, ps_z, z_done, n_done, zT_done)
                steps(act, NG, step)
                store(Step(NG // 2 - 1, 1))
                for s in range(2):
                    act.wait_ge(stored[s], 16 * NG // 2)

            @block.tensor
            def _(pe):
                def z_product(st):
                    pe.wait_ge(UA_in[st.s], 16 * (st.pair + 1))
                    wait(pe, zT_done, st.n)
                    for k in range(GROUP):
                        i = nc.tensor.matmul(ps_z[:, k], UA[st.s][:, k], m.Tt[:, bass.ds(st.n * GROUP + k, 1), :],
                                             start=True, stop=True)
                    i.then_inc(z_done, 1)

                def scores(st):
                    pe.wait_ge(zT_done, st.n + 1)
                    pe.wait_ge(q_in[st.s], 16 * (st.pair + 1))
                    wait(pe, sc_done, st.n)
                    for k in range(GROUP):
                        i = nc.tensor.matmul(ps_s[:, k], zT[st.s][:, k], qT[st.s][:, k], start=True, stop=True)
                    i.then_inc(s_done, 1)
                    wait(pe, zn_done, st.n)
                    for k in range(GROUP):
                        i = nc.tensor.transpose(ps_n[:, k], zT[st.s][:, k], c.ident[:])
                    i.then_inc(n_done, 1)

                def attend(st):
                    pe.wait_ge(sc_done, st.n + 1)
                    pe.wait_ge(vd_done, st.n + 1)
                    wait(pe, oT_done, st.n)
                    if is_first(st):
                        pe.wait_ge(M_zero, 2)
                    else:
                        wait(pe, M_done, st.n - 1)
                    for k in range(GROUP):
                        nc.tensor.matmul(ps_o[:, k], vd[st.s][:, k], sc[st.s][:, k], start=True, stop=False)
                        i = nc.tensor.matmul(ps_o[:, k], M[st.s][:, k], qT[st.s][:, k], start=False, stop=True)
                    i.then_inc(o_done, 1)
                    pe.wait_ge(zn_done, st.n + 1)
                    wait(pe, M_done, st.n)
                    for k in range(GROUP):
                        i = nc.tensor.matmul(ps_m[:, k], zn[st.s][:, k], vd[st.s][:, k], start=True, stop=True)
                    i.then_inc(m_done, 1)

                def project_out(st):
                    pe.wait_ge(oT_done, st.n + 1)
                    wait(pe, xo_done, st.n)
                    for k in range(GROUP):
                        i = nc.tensor.matmul(ps_r[:, k], oT[st.s][:, k], wo[:], start=True, stop=True)
                    i.then_inc(r_done, 1)

                def step(st):
                    if not is_last(st, NG):
                        z_product(st.later(1))
                    scores(st)
                    if not is_first(st):
                        project_out(st.later(-1))
                    attend(st)

                pe.wait_ge(w_in, 32)
                z_product(Step(0, 0))
                steps(pe, NG, step)
                project_out(Step(NG // 2 - 1, 1))


class Names:
    pass


def macaron(nc, a, out):
    def dram(name, shape):
        return nc.dram_tensor(name, shape, F32, kind="Internal").ap()

    x1, x2 = dram("x1_scratch", (TOKENS, D)), dram("x2_scratch", (TOKENS, D))
    m = Names()
    m.qT, m.uT, m.vs, m.UA = (dram(f"{n}_scratch", (NP, P, P)) for n in ("qT", "uT", "vs", "UA"))
    with ExitStack() as ctx:
        c = Names()
        prepare(nc, ctx, a, c)
        feed_forward(nc, "ffn1", a["x"], x1, c)
        with ExitStack() as own:
            m.KK, m.Tn, m.Tt = (own.enter_context(nc.sbuf_tensor(n, [P, NP, P], F32)) for n in ("KK", "Tn", "Tt"))
            m.dinv, m.ndinv = (own.enter_context(nc.sbuf_tensor(n, [P, NP], F32)) for n in ("dinv", "minus_dinv"))
            project(nc, x1, m, c, a)
            factorise(nc, "inv", m, c)
            gram(nc, m, c)
            factorise(nc, "ldl", m, c)
            outputs(nc, x1, x2, m, c, a)
        feed_forward(nc, "ffn2", x2, out, c)


def kernel(**inputs):
    import numpy as np
    import concourse.bacc as bacc
    from concourse import mybir as _mybir
    from concourse.bass_utils import run_bass_kernel_spmd

    g = {k.replace("L0_", ""): np.asarray(v) for k, v in inputs.items()}
    laid = {
        "x": g["attn_x"].reshape(TOKENS, D),
        "W1T": g["ffn_W1"].T,
        "W2T": g["ffn_W2"].T,
        "b1": g["ffn_b1"].reshape(FC, P).T,
        "b2": g["ffn_b2"],
        "WqkvT": np.concatenate([g["attn_Wq"].T, g["attn_Wk"].T, g["attn_Wv"].T], axis=1),
        "bqkv": np.concatenate([g["attn_bq"], g["attn_bk"], g["attn_bv"]]),
        "WoT": g["attn_Wo"].T,
        "bo": g["attn_bo"],
    }
    nc = bacc.Bacc("TRN2", target_bir_lowering=False, num_devices=1)
    arrays, aps = {}, {}
    for k, v in laid.items():
        arrays[f"in_{k}"] = np.ascontiguousarray(v)
        aps[k] = nc.dram_tensor(f"in_{k}", v.shape, _mybir.dt.from_np(v.dtype), kind="ExternalInput").ap()
    out = nc.dram_tensor("out_x", (TOKENS, D), F32, kind="ExternalOutput").ap()
    macaron(nc, aps, out)
    r = run_bass_kernel_spmd(nc, [arrays], core_ids=[0])
    return r.results[0]["out_x"].reshape(BATCH, T, D)
```

```python
from contextlib import ExitStack

import concourse.bass as bass
from concourse import mybir

F32 = mybir.dt.float32
F16 = mybir.dt.float16
ALU = mybir.AluOpType
ACT = mybir.ActivationFunctionType
AX_X = mybir.AxisListType.X

P = 128
BATCH, T, D = 8, 1024, 256
H = 128
FF = 1024
DC = D // P
FC = FF // P
TOKENS = BATCH * T
BLOCK = 512
BT = BLOCK // P
NBLOCK = TOKENS // BLOCK
CHUNKS = T // P
NP = BATCH * CHUNKS
GROUP = 4
NG = NP // GROUP
HC = CHUNKS // 2
NSTEP = 2 * BATCH
LN_EPS = 1e-5
NORM_EPS = 1e-6
W = 32
RW = W // 2
NW = P // W


def wait(eng, sem, value):
    if not isinstance(value, int) or value > 0:
        eng.wait_ge(sem, value)


class Step:

    def __init__(self, pair, parity):
        self.pair, self.s, self.n = pair, parity, pair * 2 + parity

    def later(self, k):
        p = self.s + k
        return Step(self.pair + p // 2, p % 2)


def steps(eng, count, body, head=3, tail=1):
    for n in range(head):
        body(Step(n // 2, n % 2))
    with eng.Fori(head // 2, (count - tail) // 2) as m:
        body(Step(m, 1))
        body(Step(m + 1, 0))
    for n in range(count - tail, count):
        body(Step(n // 2, n % 2))


def is_first(st):
    return isinstance(st.n, int) and st.n == 0


def is_last(st, count):
    return isinstance(st.n, int) and st.n == count - 1


def constants(nc, ctx, c):
    def sb(name, shape, dt=F32):
        return ctx.enter_context(nc.sbuf_tensor(name, shape, dt))

    c.w1 = sb("w1_ternary", [P, DC, FF], F16)
    c.w2 = sb("w2_ternary", [P, FC, D], F16)
    c.b1 = sb("b1_columns", [P, FC])
    c.hb2 = sb("half_b2_rows", [P, D])
    c.ident = sb("ident", [P, P])
    c.ident16 = sb("ident16", [P, P], F16)
    c.causal = sb("causal", [P, P])
    c.minus_half = sb("minus_half", [P, BT])
    c.eps = sb("ln_eps", [P, BT])
    c.plus_half = sb("plus_half", [P, BT])
    c.R = [sb(f"lane_rows{i}", [P, W, 2 * W]) for i in range(2)]
    c.lane_ident = sb("lane_ident", [P, RW, W])


class Preparation:

    def __init__(self, nc, ctx, a, c, ps):
        def tmp(name, shape, dt=F32):
            return ctx.enter_context(nc.sbuf_tensor(name, shape, dt))

        def sem(name):
            return ctx.enter_context(nc.semaphore(name))

        self.nc, self.a, self.c = nc, a, c
        self.raw = [tmp("w1_raw", [P, DC * FF]), tmp("w2_raw", [P, FC * D])]
        self.tern = [c.w1[:].rearrange("p c f -> p (c f)"), c.w2[:].rearrange("p c d -> p (c d)")]
        self.absw = tmp("abs_w", [P, 2, 2048])
        self.part = tmp("partial_sums", [P, 2, 32])
        self.colsum = tmp("column_sums", [P, 2])
        self.mean_w = tmp("mean_weights", [P, P])
        self.thr = tmp("thresholds", [P, 2, 2])
        self.below = tmp("below", [P, 2, 2048])
        self.b2_rows = tmp("b2_rows", [P, D])
        self.ps = ps
        self.w_in = [sem("prep_w1_in"), sem("prep_w2_in")]
        self.small_in = sem("prep_small_in")
        self.abs_done = sem("prep_abs_done")
        self.dve = sem("prep_dve_chain")
        self.links = 0
        self.sums_done = sem("prep_sums_done")
        self.mean_done = sem("prep_mean_done")
        self.pool = sem("prep_pool_chain")
        self.consts_done = sem("prep_constants_done")
        self.hb2_done = sem("prep_half_b2_done")
        self.ready = [sem("prep_w1_ready"), sem("prep_w2_ready")]

    def load(self, sp, i):
        view = self.a["W2T" if i else "W1T"].rearrange("(c p) f -> p c f", p=P)
        sp.dma_start(self.raw[i][:].rearrange("p (c f) -> p c f", c=FC if i else DC), view
                     ).then_inc(self.w_in[i], 16)

    def load_small(self, sp):
        sp.dma_start(self.c.b1[:], self.a["b1"]).then_inc(self.small_in, 16)
        sp.dma_start(self.b2_rows[:], self.a["b2"].partition_broadcast(P)).then_inc(self.small_in, 16)

    def absolute(self, act):
        nc = self.nc
        for i in range(2):
            act.wait_ge(self.w_in[i], 16)
            for half in (slice(0, 1024), slice(1024, 2048)):
                nc.scalar.activation(self.absw[:, i, half], self.raw[i][:, half], ACT.Abs).then_inc(self.abs_done, 1)
        act.wait_ge(self.small_in, 32)
        nc.scalar.mul(self.c.hb2[:], self.b2_rows[:], 0.5).then_inc(self.hb2_done, 1)

    def link(self, v, ins):
        self.links += 1
        ins.then_inc(self.dve, 1)
        v.wait_ge(self.dve, self.links)

    def sums(self, v, i):
        nc = self.nc
        for h in range(2):
            v.wait_ge(self.abs_done, 2 * i + h + 1)
            ins = nc.vector.tensor_reduce(
                self.part[:, i, 16 * h:16 * h + 16],
                self.absw[:, i, 1024 * h:1024 * h + 1024].rearrange("p (a b) -> p a b", b=64), AX_X, ALU.add)
        self.link(v, ins)
        nc.vector.tensor_reduce(self.colsum[:, i:i + 1], self.part[:, i], AX_X, ALU.add).then_inc(self.sums_done, 1)

    def mean(self, pe, i):
        pe.wait_ge(self.consts_done, 1)
        pe.wait_ge(self.sums_done, i + 1)
        self.nc.tensor.matmul(self.ps[i], self.mean_w[:], self.colsum[:, i:i + 1], start=True, stop=True
                              ).then_inc(self.mean_done, 1)

    def threshold(self, v, i):
        nc, thr = self.nc, self.thr
        v.wait_ge(self.mean_done, i + 1)
        self.link(v, nc.vector.tensor_scalar(thr[:, 0, i:i + 1], self.ps[i], 1e-8, 0.5, ALU.max, ALU.mult))
        self.link(v, nc.vector.tensor_scalar(thr[:, 1, i:i + 1], thr[:, 0, i:i + 1], -1.0, None, ALU.mult))

    def compare(self, v, i):
        self.link(v, self.nc.vector.tensor_scalar(self.below[:, i], self.raw[i][:], self.thr[:, 1, i:i + 1], None,
                                                  ALU.is_lt))

    def ternary(self, v, i):
        nc, thr = self.nc, self.thr
        nc.vector.scalar_tensor_tensor(out=self.tern[i], in0=self.raw[i][:], scalar=thr[:, 0, i:i + 1],
                                       in1=self.below[:, i], op0=ALU.is_gt, op1=ALU.subtract
                                       ).then_inc(self.ready[i], 1)

    def constants(self, pool):
        nc, c = self.nc, self.c
        nc.gpsimd.memset(c.minus_half[:], -0.5)
        nc.gpsimd.memset(c.eps[:], LN_EPS)
        nc.gpsimd.memset(c.plus_half[:], 0.5)
        nc.gpsimd.memset(self.mean_w[:], 1.0 / (FF * D))
        nc.gpsimd.memset(c.ident[:], 0.0)
        nc.gpsimd.memset(c.causal[:], 1.0).then_inc(self.pool, 1)
        pool.wait_ge(self.pool, 1)
        nc.gpsimd.affine_select(out=c.ident[:], in_=c.ident[:], compare_op=ALU.not_equal, fill=1.0,
                                base=0, pattern=[[1, P]], channel_multiplier=-1)
        nc.gpsimd.affine_select(out=c.causal[:], in_=c.causal[:], compare_op=ALU.is_ge, fill=0.0,
                                base=0, pattern=[[1, P]], channel_multiplier=-1).then_inc(self.pool, 1)
        pool.wait_ge(self.pool, 2)
        nc.gpsimd.tensor_copy(c.ident16[:], c.ident[:]).then_inc(self.consts_done, 1)
        pool.wait_ge(self.consts_done, 1)

    def leaf_constants(self, pool):
        nc, c = self.nc, self.c
        nc.gpsimd.memset(c.lane_ident[:], 0.0)
        for i in range(2):
            nc.gpsimd.memset(c.R[i][:], 0.0).then_inc(self.pool, 1)
        pool.wait_ge(self.pool, 4)
        for h in range(2):
            half = c.lane_ident[h * NP:(h + 1) * NP]
            nc.gpsimd.affine_select(out=half, in_=half, compare_op=ALU.not_equal, fill=1.0, base=h,
                                    pattern=[[2, RW], [-1, W]], channel_multiplier=0).then_inc(self.pool, 1)
        pool.wait_ge(self.pool, 6)


def feed_forward(nc, name, src, dst, c, a=None):
    x_v = src.rearrange("(n p t) d -> n p t d", p=P, t=BT)
    o_v = dst.rearrange("(n p t) d -> n p t d", p=P, t=BT)
    with ExitStack() as ctx:
        def sb(what, shape, dt=F32):
            return ctx.enter_context(nc.sbuf_tensor(f"{name}_{what}", shape, dt))

        def psum(what, shape, dt=F32):
            return ctx.enter_context(nc.psum_tensor(f"{name}_{what}", shape, dt))

        def sem(what):
            return ctx.enter_context(nc.semaphore(f"{name}_{what}"))

        x = [sb(f"x{s}", [P, BT, D]) for s in range(2)]
        bn = sb("bn", [P, BT, 6])
        gate = sb("gate", [P, 1])
        mv = sb("mean_var", [P, BT, 2])
        ve = sb("var_eps", [P, BT])
        rstd = sb("rstd", [P, BT])
        xn = sb("xn", [P, BT, D])
        xh = sb("xn_high", [P, BT, D], F16)
        xl = sb("xn_rest", [P, BT, D], F16)
        xTh = [sb(f"xT_high{s}", [P, DC, BLOCK], F16) for s in range(2)]
        xTl = [sb(f"xT_rest{s}", [P, DC, BLOCK], F16) for s in range(2)]
        hh = [sb(f"h_high{s}", [P, FC, BLOCK], F16) for s in range(2)]
        hl = [sb(f"h_rest{s}", [P, FC, BLOCK], F16) for s in range(2)]
        xb = [sb(f"x_plus_bias{s}", [P, BT, D]) for s in range(2)]
        xo = [sb(f"x_out{s}", [P, BT, D]) for s in range(2)]
        ps_t = [psum(f"ps_t{i}", [P, DC, BLOCK], F16) for i in range(2)]
        ps_h = [psum(f"ps_h{i}", [P, BLOCK]) for i in range(4)]
        ps_y = [psum(f"ps_y{i}", [P, D]) for i in range(2)]

        x_in = [sem(f"x_in{s}") for s in range(2)]
        bn_done = sem("bn_done")
        stats_done = sem("stats_done")
        ve_done = sem("ve_done")
        rstd_done = sem("rstd_done")
        xn_done = sem("xn_done")
        xh_done = sem("xh_done")
        xl_done = sem("xl_done")
        xb_done = sem("xb_done")
        tr_done = sem("tr_done")
        xT_done = sem("xT_done")
        h_done = sem("h_done")
        g_done = sem("g_done")
        hl_done = sem("hl_done")
        y_done = sem("y_done")
        xo_done = sem("xo_done")
        stored = [sem(f"stored{s}") for s in range(2)]
        prep = Preparation(nc, ctx, a, c, [y[:, 0:1] for y in ps_y]) if a is not None else None

        def two_ahead(st):
            return not isinstance(st.n, int) or st.n + 2 < NBLOCK

        def run(eng, step):
            steps(eng, NBLOCK, step, tail=3)

        with nc.Block() as block:
            @block.sync
            def _(sp):
                def load(st):
                    if not (isinstance(st.n, int) and st.n < 2):
                        wait(sp, xn_done, st.n - 1)
                        wait(sp, xb_done, st.n - 1)
                    sp.dma_start(x[st.s][:], x_v[st.n]).then_inc(x_in[st.s], 16)

                def step(st):
                    if two_ahead(st):
                        load(st.later(2))

                load(Step(0, 0))
                if prep:
                    prep.load(sp, 0)
                    prep.load(sp, 1)
                    prep.load_small(sp)
                load(Step(0, 1))
                run(sp, step)

            @block.vector
            def _(v):
                def stats(st):
                    v.wait_ge(x_in[st.s], 16 * (st.pair + 1))
                    for t in range(BT):
                        i = nc.vector.bn_stats(bn[:, t], x[st.s][:, t])
                    i.then_inc(bn_done, 1)
                    v.wait_ge(bn_done, st.n + 1)
                    wait(v, rstd_done, st.n)
                    nc.vector.memset(gate[:], 0.0)
                    for t in range(BT):
                        i = nc.vector.bn_aggr(mv[:, t], bn[:, t])
                    i.then_inc(stats_done, 1)

                def normalise(st):
                    v.wait_ge(rstd_done, st.n + 1)
                    wait(v, xh_done, st.n)
                    wait(v, xl_done, st.n)
                    for t in range(BT):
                        i = nc.vector.tensor_scalar(xn[:, t], x[st.s][:, t], mv[:, t, 0:1], rstd[:, t:t + 1],
                                                    ALU.subtract, ALU.mult)
                    i.then_inc(xn_done, 1)

                def rest(st, f):
                    v.wait_ge(g_done, FC * st.n + f + 1)
                    if f == 0:
                        wait(v, y_done, BT * (st.n - 1)) if not is_first(st) else None
                    nc.vector.tensor_tensor(hl[st.s][:, f], ps_h[f % 4][:], hh[st.s][:, f],
                                            ALU.subtract).then_inc(hl_done, 1)

                def copy_xT(st):
                    v.wait_ge(tr_done, st.n + 1)
                    wait(v, h_done, FC * (st.n - 1)) if not is_first(st) else None
                    nc.vector.tensor_copy(xTh[st.s][:], ps_t[0][:]).then_inc(xT_done, 1)
                    nc.vector.tensor_copy(xTl[st.s][:], ps_t[1][:]).then_inc(xT_done, 1)

                def finish(st, t):
                    v.wait_ge(y_done, BT * st.n + t + 1)
                    if t == 0:
                        v.wait_ge(xb_done, st.n + 1)
                        wait(v, stored[st.s], st.pair * 16)
                    nc.vector.scalar_tensor_tensor(out=xo[st.s][:, t], in0=ps_y[t % 2][:], scalar=0.5,
                                                   in1=xb[st.s][:, t], op0=ALU.mult, op1=ALU.add
                                                   ).then_inc(xo_done, 1)

                def step(st):
                    first, last, prev = is_first(st), is_last(st, NBLOCK), st.later(-1)
                    if not last:
                        normalise(st.later(1))
                    for f in range(FC):
                        rest(st, f)
                        if not first and f in (2, 4, 6):
                            finish(prev, (f - 2) // 2)
                        if first and prep:
                            if f == 1:
                                prep.threshold(v, 1)
                            elif f == 4:
                                prep.compare(v, 1)
                            elif f == 6:
                                prep.ternary(v, 1)
                        if f == 5 and not last:
                            copy_xT(st.later(1))
                        if f == 6 and two_ahead(st):
                            stats(st.later(2))
                    if not first:
                        finish(prev, BT - 1)

                stats(Step(0, 0))
                if prep:
                    prep.sums(v, 0)
                normalise(Step(0, 0))
                if prep:
                    prep.threshold(v, 0)
                    prep.compare(v, 0)
                    prep.ternary(v, 0)
                    prep.sums(v, 1)
                copy_xT(Step(0, 0))
                stats(Step(0, 1))
                run(v, step)
                for t in range(BT):
                    finish(Step((NBLOCK - 1) // 2, (NBLOCK - 1) % 2), t)

            @block.gpsimd
            def _(pool):
                def rsqrt(st):
                    pool.wait_ge(stats_done, st.n + 1)
                    nc.gpsimd.tensor_tensor(ve[:], mv[:, :, 1], c.eps[:], ALU.add).then_inc(ve_done, 1)
                    pool.wait_ge(ve_done, st.n + 1)
                    wait(pool, xn_done, st.n)
                    nc.gpsimd.tensor_tensor(rstd[:], ve[:], c.minus_half[:], ALU.pow).then_inc(rstd_done, 1)

                def split(st):
                    pool.wait_ge(xh_done, st.n + 1)
                    wait(pool, tr_done, st.n)
                    nc.gpsimd.tensor_tensor(xl[:], xn[:], xh[:], ALU.subtract).then_inc(xl_done, 1)

                def add_bias(st):
                    pool.wait_ge(x_in[st.s], 16 * (st.pair + 1))
                    wait(pool, xo_done, BT * (st.n - 1)) if not is_first(st) else None
                    nc.gpsimd.tensor_tensor(xb[st.s][:], x[st.s][:],
                                            c.hb2[:].unsqueeze(1).to_broadcast([P, BT, D]),
                                            ALU.add).then_inc(xb_done, 1)

                def step(st):
                    if not is_last(st, NBLOCK):
                        split(st.later(1))
                    add_bias(st)
                    if two_ahead(st):
                        rsqrt(st.later(2))

                if prep:
                    prep.constants(pool)
                rsqrt(Step(0, 0))
                split(Step(0, 0))
                if prep:
                    pool.wait_ge(xl_done, 1)
                    prep.leaf_constants(pool)
                    pool.wait_ge(prep.hb2_done, 1)
                rsqrt(Step(0, 1))
                run(pool, step)

            @block.scalar
            def _(act):
                def high(st):
                    act.wait_ge(xn_done, st.n + 1)
                    wait(act, tr_done, st.n)
                    nc.scalar.activation(xh[:], xn[:], ACT.Copy).then_inc(xh_done, 1)

                def gelu(st, f):
                    act.wait_ge(h_done, FC * st.n + f + 1)
                    if f == 0:
                        wait(act, y_done, BT * (st.n - 1)) if not is_first(st) else None
                    nc.scalar.activation(hh[st.s][:, f], ps_h[f % 4][:], ACT.Gelu, bias=c.b1[:, f:f + 1])
                    nc.scalar.activation(ps_h[f % 4][:], ps_h[f % 4][:], ACT.Gelu,
                                         bias=c.b1[:, f:f + 1]).then_inc(g_done, 1)

                def store(st):
                    wait(act, xo_done, BT * (st.n + 1))
                    act.dma_start(o_v[st.n], xo[st.s][:]).then_inc(stored[st.s], 16)

                def step(st):
                    late = st.later(-2)
                    for f in range(FC):
                        gelu(st, f)
                        if f == 2 and not (isinstance(st.n, int) and st.n < 2):
                            store(late)
                        if f == 0 and not is_last(st, NBLOCK):
                            high(st.later(1))

                if prep:
                    prep.absolute(act)
                high(Step(0, 0))
                run(act, step)
                store(Step(NBLOCK // 2 - 1, 0))
                store(Step(NBLOCK // 2 - 1, 1))
                for s in range(2):
                    act.wait_ge(stored[s], 16 * NBLOCK // 2)

            @block.tensor
            def _(pe):
                def turn(st):
                    pe.wait_ge(xh_done, st.n + 1)
                    pe.wait_ge(xl_done, st.n + 1)
                    wait(pe, xT_done, 2 * st.n)
                    for i, part in enumerate((xh, xl)):
                        for d in range(DC):
                            for t in range(BT):
                                ins = nc.tensor.transpose(ps_t[i][:, d, t * P:(t + 1) * P],
                                                          part[:, t, d * P:(d + 1) * P], c.ident16[:])
                    ins.then_inc(tr_done, 1)

                def first_product(st, f):
                    if f == 0:
                        pe.wait_ge(xT_done, 2 * (st.n + 1))
                    if not (is_first(st) and f < 4):
                        pe.wait_ge(hl_done, FC * st.n + f - 3)
                    k = 0
                    for d in range(DC):
                        for part in (xTh, xTl):
                            ins = nc.tensor.matmul(ps_h[f % 4][:], c.w1[:, d, f * P:(f + 1) * P], part[st.s][:, d],
                                                   start=(k == 0), stop=(k == 2 * DC - 1))
                            k += 1
                    ins.then_inc(h_done, 1)

                def second_product(st, t, half):
                    if t == 0 and half == 0:
                        pe.wait_ge(hl_done, FC * (st.n + 1))
                        if prep and is_first(st):
                            pe.wait_ge(prep.ready[1], 1)
                    if half == 0 and not (is_first(st) and t < 2):
                        pe.wait_ge(xo_done, BT * st.n + t - 1)
                    for f in range(half * FC // 2, (half + 1) * FC // 2):
                        for part in (hh, hl):
                            ins = nc.tensor.matmul(ps_y[t % 2][:], part[st.s][:, f, t * P:(t + 1) * P], c.w2[:, f],
                                                   start=(f == 0 and part is hh), stop=(f == FC - 1 and part is hl))
                    if half:
                        ins.then_inc(y_done, 1)

                def step(st):
                    first, last, prev = is_first(st), is_last(st, NBLOCK), st.later(-1)
                    for f in range(FC):
                        first_product(st, f)
                        if not first and f > 0:
                            second_product(prev, (f - 1) // 2, (f - 1) % 2)
                        if f == 5 and not last:
                            turn(st.later(1))
                    if not first:
                        second_product(prev, BT - 1, 1)

                if prep:
                    prep.mean(pe, 0)
                turn(Step(0, 0))
                if prep:
                    prep.mean(pe, 1)
                    pe.wait_ge(prep.ready[0], 1)
                run(pe, step)
                for t in range(BT):
                    for half in range(2):
                        second_product(Step((NBLOCK - 1) // 2, (NBLOCK - 1) % 2), t, half)


def keys(nc, x1, m, c, a):
    x_v = x1.rearrange("(n c t) d -> n t c d", c=HC, t=P)
    uT_v = m.uT.rearrange("(c b) i j -> b i c j", b=BATCH)
    with ExitStack() as ctx:
        def sb(what, shape, dt=F32):
            return ctx.enter_context(nc.sbuf_tensor(f"keys_{what}", shape, dt))

        def psum(what, shape, dt=F32):
            return ctx.enter_context(nc.psum_tensor(f"keys_{what}", shape, dt))

        def sem(what):
            return ctx.enter_context(nc.semaphore(f"keys_{what}"))

        w = sb("wk", [P, DC, H])
        bias = sb("bk", [P, H])
        x = [sb(f"x{s}", [P, HC, D]) for s in range(2)]
        bn = sb("bn", [P, HC, 6])
        gate, no_sum = sb("gate", [P, 1]), sb("no_sum", [P, 1])
        mv = sb("mean_var", [P, HC, 2])
        ve = sb("var_eps", [P, HC])
        rstd = sb("rstd", [P, HC])
        xn = sb("xn", [P, HC, D])
        aT = [sb(f"aT{s}", [P, HC, DC, P]) for s in range(2)]
        k = [sb(f"k{s}", [P, HC, H]) for s in range(2)]
        junk = sb("junk", [P, HC, H])
        ksq = sb("k_squared", [P, HC])
        norm = sb("k_norm", [P, HC])
        norm_eps = sb("k_norm_eps", [P, HC])
        rnorm = sb("k_norm_inverse", [P, HC])
        u = [sb(f"u{s}", [P, HC, H]) for s in range(2)]
        uT = [sb(f"uT{s}", [P, HC, P]) for s in range(2)]
        ps_a = psum("ps_a", [P, HC, DC, P])
        ps_k = [psum(f"ps_k{s}", [P, HC, H]) for s in range(2)]
        ps_u = psum("ps_u", [P, HC, P])
        ps_p = [psum(f"ps_p{s}", [P, HC, P]) for s in range(2)]

        w_in = sem("w_in")
        x_in = [sem(f"x_in{s}") for s in range(2)]
        kk_start = sem("kk_start")
        bn_done = sem("bn_done")
        stats_done = sem("stats_done")
        ve_done = sem("ve_done")
        rstd_done = sem("rstd_done")
        xn_done = sem("xn_done")
        ta_done = sem("ta_done")
        aT_done = sem("aT_done")
        product_done = sem("k_product")
        k_done = sem("k_done")
        ksq_done = sem("ksq_done")
        norm_done = sem("norm_done")
        norm_eps_done = sem("norm_eps_done")
        rnorm_done = sem("rnorm_done")
        u_done = sem("u_done")
        tu_done = sem("tu_done")
        uT_done = sem("uT_done")
        p_done = sem("p_done")
        kk_done = sem("kk_done")
        aT_stored = [sem(f"aT_stored{s}") for s in range(2)]
        uT_stored = [sem(f"uT_stored{s}") for s in range(2)]

        def stage(st, lag, what):
            at = st.later(lag)
            if not isinstance(at.n, int) or 0 <= at.n < NSTEP:
                what(at)

        def run(eng, step, tail=4):
            steps(eng, NSTEP + 3, step, head=5, tail=tail)

        with nc.Block() as block:
            @block.sync
            def _(sp):
                def load(st):
                    if not (isinstance(st.n, int) and st.n < 2):
                        wait(sp, xn_done, st.n - 1)
                    sp.dma_start(x[st.s][:], x_v[st.n]).then_inc(x_in[st.s], 16)

                def store_a(st):
                    sp.wait_ge(aT_done, 2 * (st.n + 1))
                    sp.dma_start(m.aT[st.n], aT[st.s][:]).then_inc(aT_stored[st.s], 16)

                def store_u(st):
                    sp.wait_ge(uT_done, st.n + 1)
                    sp.dma_start(uT_v[st.pair, :, HC * st.s:HC * st.s + HC], uT[st.s][:]
                                 ).then_inc(uT_stored[st.s], 16)

                def step(st):
                    stage(st, 2, load)
                    stage(st, -1, store_a)
                    stage(st, -3, store_u)

                load(Step(0, 0))
                sp.dma_start(w[:], a["WqkvT"].rearrange("(c p) n -> p c n", p=P)[:, :, H:2 * H]).then_inc(w_in, 16)
                sp.dma_start(bias[:], a["bqkv"][H:2 * H].partition_broadcast(P)).then_inc(w_in, 16)
                load(Step(0, 1))
                run(sp, step, tail=6)
                for s in range(2):
                    sp.wait_ge(aT_stored[s], 16 * NSTEP // 2)
                    sp.wait_ge(uT_stored[s], 16 * NSTEP // 2)

            @block.vector
            def _(v):
                def stats(st):
                    v.wait_ge(x_in[st.s], 16 * (st.pair + 1))
                    for t in range(HC):
                        i = nc.vector.bn_stats(bn[:, t], x[st.s][:, t])
                    i.then_inc(bn_done, 1)

                def aggregate(st):
                    v.wait_ge(bn_done, st.n + 1)
                    wait(v, rstd_done, st.n)
                    nc.vector.memset(gate[:], 0.0)
                    for t in range(HC):
                        i = nc.vector.bn_aggr(mv[:, t], bn[:, t])
                    i.then_inc(stats_done, 1)

                def normalise(st):
                    v.wait_ge(rstd_done, st.n + 1)
                    wait(v, ta_done, st.n)
                    for t in range(HC):
                        i = nc.vector.tensor_scalar(xn[:, t], x[st.s][:, t], mv[:, t, 0:1], rstd[:, t:t + 1],
                                                    ALU.subtract, ALU.mult)
                    i.then_inc(xn_done, 1)

                def add_bias(st):
                    v.wait_ge(product_done, st.n + 1)
                    if not is_first(st):
                        wait(v, u_done, st.n - 1)
                    nc.vector.tensor_tensor(k[st.s][:], ps_k[st.s][:],
                                            bias[:].unsqueeze(1).to_broadcast([P, HC, H]), ALU.add
                                            ).then_inc(k_done, 1)

                def add_eps(st):
                    v.wait_ge(norm_done, st.n + 1)
                    wait(v, rnorm_done, st.n)
                    nc.vector.tensor_scalar(norm_eps[:], norm[:], NORM_EPS, None, ALU.add)
                    nc.vector.tensor_scalar(m.knorm[:, bass.ds(st.n * HC, HC)], norm[:], NORM_EPS, None,
                                            ALU.add).then_inc(norm_eps_done, 1)

                def invert(st):
                    v.wait_ge(norm_eps_done, st.n + 1)
                    wait(v, u_done, st.n)
                    nc.vector.reciprocal(rnorm[:], norm_eps[:]).then_inc(rnorm_done, 1)

                def prefix(st, j):
                    if j == 0:
                        v.wait_ge(p_done, st.n + 1)
                        if is_first(st):
                            v.wait_ge(kk_start, 1)
                    chunk = HC * st.s + j
                    if chunk == CHUNKS - 1:
                        nc.vector.memset(no_sum[:], 0.0).then_inc(kk_done, 1)
                        return
                    wait(v, kk_done, HC * st.n + j)
                    nc.vector.tensor_tensor(m.KK[:, bass.ds(st.pair + (chunk + 1) * BATCH, 1), :],
                                            ps_p[st.s][:, j:j + 1], m.KK[:, bass.ds(st.pair + chunk * BATCH, 1), :],
                                            ALU.add).then_inc(kk_done, 1)

                def step(st):
                    def sums(j):
                        stage(st, -3, lambda x: prefix(x, j))

                    stage(st, 0, normalise)
                    stage(st, 1, stats)
                    stage(st, -2, add_eps)
                    sums(0)
                    stage(st, 1, aggregate)
                    stage(st, -2, invert)
                    sums(1)
                    sums(2)
                    stage(st, -1, add_bias)
                    sums(3)

                stats(Step(0, 0))
                aggregate(Step(0, 0))
                for b in range(BATCH):
                    i = nc.vector.tensor_copy(m.KK[:, b], c.ident[:])
                i.then_inc(kk_start, 1)
                v.wait_ge(w_in, 32)
                run(v, step)

            @block.gpsimd
            def _(pool):
                def rsqrt(st):
                    pool.wait_ge(stats_done, st.n + 1)
                    nc.gpsimd.tensor_tensor(ve[:], mv[:, :, 1], c.eps[:], ALU.add).then_inc(ve_done, 1)
                    pool.wait_ge(ve_done, st.n + 1)
                    wait(pool, xn_done, st.n)
                    nc.gpsimd.tensor_tensor(rstd[:], ve[:], c.minus_half[:], ALU.pow).then_inc(rstd_done, 1)

                def root(st):
                    pool.wait_ge(ksq_done, st.n + 1)
                    wait(pool, norm_eps_done, st.n)
                    nc.gpsimd.tensor_tensor(norm[:], ksq[:], c.plus_half[:], ALU.pow).then_inc(norm_done, 1)

                def step(st):
                    stage(st, 1, rsqrt)
                    stage(st, -1, root)

                rsqrt(Step(0, 0))
                run(pool, step)

            @block.scalar
            def _(act):
                def copy_aT(st):
                    act.wait_ge(ta_done, st.n + 1)
                    if not is_first(st):
                        wait(act, product_done, st.n - 1)
                    wait(act, aT_stored[st.s], 16 * st.pair)
                    for i in range(2):
                        nc.scalar.activation(aT[st.s][:, 2 * i:2 * i + 2], ps_a[:, 2 * i:2 * i + 2],
                                             ACT.Copy).then_inc(aT_done, 1)

                def squares(st):
                    act.wait_ge(k_done, st.n + 1)
                    wait(act, norm_done, st.n)
                    for j in range(HC):
                        i = nc.scalar.activation(junk[:, j], k[st.s][:, j], ACT.Square, accum_out=ksq[:, j:j + 1])
                    i.then_inc(ksq_done, 1)

                def scale_u(st):
                    act.wait_ge(rnorm_done, st.n + 1)
                    if not is_first(st):
                        wait(act, tu_done, st.n - 1)
                    for j in range(HC):
                        i = nc.scalar.activation(u[st.s][:, j], k[st.s][:, j], ACT.Copy, scale=rnorm[:, j:j + 1])
                    i.then_inc(u_done, 1)

                def copy_uT(st):
                    act.wait_ge(tu_done, st.n + 1)
                    wait(act, uT_stored[st.s], 16 * st.pair)
                    nc.scalar.activation(uT[st.s][:], ps_u[:], ACT.Copy).then_inc(uT_done, 1)

                def step(st):
                    stage(st, -3, copy_uT)
                    stage(st, 0, copy_aT)
                    stage(st, -2, scale_u)
                    stage(st, -1, squares)

                run(act, step)

            @block.tensor
            def _(pe):
                def turn_a(st):
                    pe.wait_ge(xn_done, st.n + 1)
                    wait(pe, aT_done, 2 * st.n)
                    for j in range(HC):
                        for d in range(DC):
                            i = nc.tensor.transpose(ps_a[:, j, d], xn[:, j, d * P:(d + 1) * P], c.ident[:])
                    i.then_inc(ta_done, 1)

                def product(st):
                    pe.wait_ge(aT_done, 2 * (st.n + 1))
                    if not is_first(st):
                        wait(pe, k_done, st.n - 1)
                    for j in range(HC):
                        for d in range(DC):
                            i = nc.tensor.matmul(ps_k[st.s][:, j], aT[st.s][:, j, d], w[:, d],
                                                 start=(d == 0), stop=(d == DC - 1))
                    i.then_inc(product_done, 1)

                def turn_u(st):
                    wait(pe, uT_done, st.n)
                    for j in range(HC):
                        i = nc.tensor.transpose(ps_u[:, j], u[st.s][:, j], c.ident[:])
                    i.then_inc(tu_done, 1)

                def squares(st):
                    pe.wait_ge(u_done, st.n + 1)
                    if not is_first(st):
                        wait(pe, kk_done, HC * (st.n - 1))
                    for j in range(HC):
                        i = nc.tensor.matmul(ps_p[st.s][:, j], u[st.s][:, j], u[st.s][:, j], start=True, stop=True)
                    i.then_inc(p_done, 1)

                def step(st):
                    stage(st, -3, squares)
                    stage(st, -3, turn_u)
                    stage(st, 0, turn_a)
                    stage(st, -1, product)

                pe.wait_ge(w_in, 32)
                run(pe, step)


LEAF_IN, LEAF_OUT, TURN_N, SCHUR, FIRST, ROWS, COLUMNS, QV, DOTS = (
    "leaf in", "leaf out", "turn n", "schur", "first", "rows", "columns", "qv", "dots")


def make_plan(end, with_qv):
    def qv(first, count):
        return [(QV, first, count), (DOTS, first, count)] if with_qv else []

    assert NSTEP == 16
    return [(LEAF_IN, 0, 32), *qv(0, 6), (LEAF_OUT, 0, 32), (SCHUR, 0, 32),
            (LEAF_IN, 32, 32), (TURN_N, 0, 32), (FIRST, 0, 32), *qv(6, 4), (LEAF_OUT, 32, 32),
            (COLUMNS, 0, 32), (SCHUR, 0, 64),
            (LEAF_IN, 64, 32), (TURN_N, 32, 32), (ROWS, 0, 32), (FIRST, 0, 64), *qv(10, 2), (LEAF_OUT, 64, 32),
            (SCHUR, 64, 32),
            (LEAF_IN, 96, 32), (TURN_N, 64, 32), (FIRST, 64, 32), *qv(12, 4), (LEAF_OUT, 96, 32),
            (COLUMNS, 64, 32), *{"rows": [(TURN_N, 96, 32), (ROWS, 64, 32), (ROWS, 0, 64)],
                                 "columns": [(COLUMNS, 0, 64)]}[end]]


QV_MAX = 6
BANKS = 4


def groups_of(w):
    n = 512 // w
    return n, NP // n


def bank_users(kind, w):
    if kind in (QV, DOTS):
        return ["act"] * (kind == DOTS)
    count = groups_of(w)[1]
    if kind == LEAF_OUT:
        return ["act"] * 4 + ["dve"]
    if kind == SCHUR:
        return ["act"] + ["act", "dve"] * (count - 1) + ["dve"]
    return ["act"] * {LEAF_IN: 1, TURN_N: 4}.get(kind, count)


class Fills:

    def __init__(self, plan):
        self.start, self.users = [], []
        for kind, _, w in plan:
            self.start.append(len(self.users))
            self.users += bank_users(kind, w)

    def emptied(self, n, engine):
        return self.users[:n].count(engine)


def y_fill(g):
    return max(2 * g - 1, 0)


def s_fill(g, count):
    return min(2 * g + 2, 2 * count - 1)


def factorise(nc, name, end, m, c, a=None):
    first_time = a is not None
    plan = make_plan(end, first_time)
    fills = Fills(plan)
    with ExitStack() as ctx:
        def sb(what, shape, dt=F32):
            return ctx.enter_context(nc.sbuf_tensor(f"{name}_{what}", shape, dt))

        def psum(what, shape, dt=F32):
            return ctx.enter_context(nc.psum_tensor(f"{name}_{what}", shape, dt))

        def sem(what):
            return ctx.enter_context(nc.semaphore(f"{name}_{what}"))

        KK, Tn, Tt, dinv, ndinv = m.KK, m.Tn, m.Tt, m.dinv, m.ndinv
        prod = sb("rank_one", [P, RW, W])
        mult = [sb(f"multipliers{i}", [P, W]) for i in range(2)]
        dl = sb("lane_dinv", [P, W])
        Y = [sb(f"Y{i}", [P, 512]) for i in range(2)]
        if first_time:
            wqv = sb("wqv", [P, DC, 2, H])
            bq = sb("bq_column", [P, 1])
            bv = sb("bv_rows", [P, H])
            ones = sb("ones", [P, 1])
            aT = [sb(f"aT{s}", [P, HC, DC, P]) for s in range(2)]
            uT = [sb(f"uT{s}", [P, HC, P]) for s in range(2)]
            qT = [sb(f"qT{s}", [P, HC, P]) for s in range(2)]
            v_raw = [sb(f"v_unbiased{s}", [P, HC, H]) for s in range(2)]
            v_out = [sb(f"v{s}", [P, HC, H]) for s in range(2)]
            uq = sb("u_times_q", [P, QV_MAX, HC, P])
            qT_v, uT_v, v_v = (y.rearrange("(c b) i j -> b i c j", b=BATCH) for y in (m.qT, m.uT, m.v))
        YV = {w: sb(f"Yd_and_V{w}", [P, NP, w]) for w in (32, 64)}
        ps_lane = psum("ps_lane", [P, 2, 512])
        M = ps_lane[:].rearrange("p a (b x) -> p (a b) x", x=2 * W)
        ps = [psum(f"ps{i}", [P, 512]) for i in range(BANKS)]
        ps_q = psum("ps_q", [P, HC, P])
        ps_v = psum("ps_v", [P, HC, H])

        lane_reset = sem("lane_reset")
        leaf_in = sem("leaf_in")
        row_done = sem("lane_row")
        chain = sem("lane_chain")
        leaf_done = sem("leaf_done")
        filled = sem("bank_filled")
        act_emptied = sem("act_emptied")
        dve_emptied = sem("dve_emptied")
        yd_done = sem("yd_done")

        if first_time:
            zeros = sem("zeros")
            w_in = sem("wqv_in")
            ones_done = sem("ones_done")
            a_in = [sem(f"aT_in{s}") for s in range(2)]
            u_in = [sem(f"uT_in{s}") for s in range(2)]
            q_made = sem("q_product")
            q_done = sem("q_done")
            v_made = sem("v_product")
            v_copied = sem("v_copied")
            v_done = sem("v_done")
            uq_done = sem("uq_done")
            q_stored = [sem(f"q_stored{s}") for s in range(2)]
            v_stored = [sem(f"v_stored{s}") for s in range(2)]

        def span(o, w):
            return slice(o, o + w)

        def leaf_number(o):
            return o // W

        def yds_before(index):
            return sum(groups_of(w)[1] for kind, _, w in plan[:index] if kind == SCHUR)

        with nc.Block() as block:
            @block.sync
            def _(sp):
                def load(n):
                    s = n % 2
                    if n > 1:
                        sp.wait_ge(v_made, n - 1)
                        sp.wait_ge(uq_done, n - 1)
                    sp.dma_start(aT[s][:], m.aT[n]).then_inc(a_in[s], 16)
                    sp.dma_start(uT[s][:], uT_v[n // 2, :, HC * s:HC * s + HC]).then_inc(u_in[s], 16)

                def store(n):
                    s = n % 2
                    sp.wait_ge(q_done, n + 1)
                    sp.dma_start(qT_v[n // 2, :, HC * s:HC * s + HC], qT[s][:]).then_inc(q_stored[s], 16)
                    sp.wait_ge(v_done, n + 1)
                    sp.dma_start(v_v[n // 2, :, HC * s:HC * s + HC], v_out[s][:]).then_inc(v_stored[s], 16)

                if first_time:
                    w_v = a["WqkvT"].rearrange("(c p) n -> p c n", p=P)
                    for i in range(2):
                        sp.dma_start(wqv[:, :, i], w_v[:, :, 2 * i * H:(2 * i + 1) * H]).then_inc(w_in, 16)
                    sp.dma_start(bq[:], a["bqkv"][0:H].rearrange("(p o) -> p o", o=1)).then_inc(w_in, 16)
                    sp.dma_start(bv[:], a["bqkv"][2 * H:].partition_broadcast(P)).then_inc(w_in, 16)
                    load(0)
                    load(1)
                    for n in range(NSTEP):
                        store(n)
                        if n + 2 < NSTEP:
                            load(n + 2)
                    for s in range(2):
                        sp.wait_ge(q_stored[s], 16 * NSTEP // 2)
                        sp.wait_ge(v_stored[s], 16 * NSTEP // 2)

            @block.gpsimd
            def _(pool):
                def clear():
                    for i in range(NW - 1):
                        rows, cols = span(i * W, W), slice((i + 1) * W, P)
                        nc.gpsimd.memset(Tn[rows, :, cols], 0.0).then_inc(zeros, 1)
                        pool.wait_ge(zeros, 2 * i + 1)
                        rows, cols = span((i + 1) * W, W), slice(0, (i + 1) * W)
                        nc.gpsimd.memset(Tt[rows, :, cols], 0.0).then_inc(zeros, 1)
                        pool.wait_ge(zeros, 2 * i + 2)

                def qv(index, n, slot):
                    s = n % 2
                    pool.wait_ge(v_copied, n + 1)
                    if n > 1:
                        pool.wait_ge(v_stored[s], 16 * (n // 2))
                    nc.gpsimd.tensor_tensor(v_out[s][:], v_raw[s][:], bv[:].unsqueeze(1).to_broadcast([P, HC, H]),
                                            ALU.add).then_inc(v_done, 1)
                    pool.wait_ge(q_done, n + 1)
                    pool.wait_ge(u_in[s], 16 * (n // 2 + 1))
                    if slot == 0 and n:
                        pool.wait_ge(filled, fills.start[index])
                    nc.gpsimd.tensor_tensor(uq[:, slot], uT[s][:], qT[s][:], ALU.mult).then_inc(uq_done, 1)

                if first_time:
                    nc.gpsimd.memset(ones[:], 1.0).then_inc(ones_done, 1)
                    pool.wait_ge(w_in, 64)
                    for index, (kind, o, w) in enumerate(plan):
                        if kind == QV:
                            for i in range(w):
                                qv(index, o + i, i)
                            if o == 0:
                                clear()

            @block.vector
            def _(v):
                links = [0]

                def note(ins):
                    links[0] += 1
                    ins.then_inc(chain, 1)
                    return links[0]

                def leaf(index, o):
                    r = leaf_number(o)
                    R = c.R[r % 2]

                    def multipliers(j):
                        for h in range(2):
                            lanes = slice(h * NP, (h + 1) * NP)
                            shape = [NP, W - 1 - j]
                            i = nc.vector.scalar_tensor_tensor(
                                out=mult[j % 2][lanes, j + 1 - h:W - h], in0=R[lanes, j, j + 1:W], scalar=-1.0,
                                in1=dl[lanes, j:j + 1].to_broadcast(shape), op0=ALU.mult, op1=ALU.mult)
                        return note(i)

                    v.wait_ge(leaf_in, r + 1)
                    v.wait_ge(act_emptied, fills.emptied(fills.start[index] + 1, "act"))
                    for h in range(2):
                        i = nc.vector.tensor_copy(R[h * NP:(h + 1) * NP, 0, :W + 1], M[0:NP, 0, :W + 1])
                    i.then_inc(row_done, 1)
                    v.wait_ge(row_done, W * r + 1)
                    inverse = note(nc.vector.reciprocal(dl[:, 0:1], R[:, 0, 0:1]))
                    v.wait_ge(chain, inverse)
                    scaled = multipliers(0)
                    for j in range(W - 1):
                        v.wait_ge(chain, scaled)
                        own = ((j + 1) % 2) * NP
                        window = slice(j + 1, W + j + 2)
                        for h in range(2):
                            lanes = slice(h * NP, (h + 1) * NP)
                            i = nc.vector.scalar_tensor_tensor(
                                out=R[lanes, j + 1, window], in0=R[lanes, j, window],
                                scalar=mult[j % 2][lanes, j + 1 - h:j + 2 - h],
                                in1=M[own:own + NP, (j + 1) // 2, window], op0=ALU.mult, op1=ALU.add)
                        i.then_inc(row_done, 1)
                        r0 = (j + 2) // 2
                        n = RW - r0
                        window = slice(j + 1, W + j + 1)
                        shape = [P, n, W]
                        if n:
                            v.wait_ge(chain, links[0])
                            i = nc.vector.tensor_tensor(prod[:, :n],
                                                        mult[j % 2][:, 2 * r0::2].unsqueeze(2).to_broadcast(shape),
                                                        R[:, j:j + 1, window].to_broadcast(shape), ALU.mult)
                            product = note(i)
                        v.wait_ge(row_done, W * r + j + 2)
                        i = nc.vector.reciprocal(dl[:, j + 1:j + 2], R[:, j + 1, j + 1:j + 2])
                        if j == W - 2:
                            i.then_inc(leaf_done, 1)
                            break
                        inverse = note(i)
                        if n:
                            v.wait_ge(chain, product)
                            note(nc.vector.tensor_tensor(M[:, r0:r0 + 1, window], M[:, r0:r0 + 1, window],
                                                         prod[:, :1], ALU.add))
                        v.wait_ge(chain, inverse)
                        scaled = multipliers(j + 1)
                        if n > 1:
                            note(nc.vector.tensor_tensor(M[:, r0 + 1:, window], M[:, r0 + 1:, window],
                                                         prod[:, 1:n], ALU.add))

                def leaf_out(index, o):
                    n = fills.start[index] + 4
                    v.wait_ge(filled, n + 1)
                    nc.vector.tensor_copy(dinv[span(o, W)], ps[n % BANKS][0:W, 0:NP])
                    nc.vector.tensor_scalar(ndinv[span(o, W)], ps[n % BANKS][0:W, 0:NP], -1.0, None,
                                            ALU.mult).then_inc(dve_emptied, 1)

                def schur(index, o, w):
                    n, count = groups_of(w)
                    b1, b2 = span(o, w), span(o + w, w)

                    def scale(g):
                        pr = slice(g * n, g * n + n)
                        v.wait_ge(act_emptied, fills.emptied(fills.start[index] + y_fill(g) + 1, "act"))
                        nc.vector.tensor_tensor(YV[w][b1, pr], Y[g % 2][b1].rearrange("i (p j) -> i p j", p=n),
                                                ndinv[b1, pr].unsqueeze(2).to_broadcast([w, n, w]),
                                                ALU.mult).then_inc(yd_done, 1)

                    def update(g):
                        pr = slice(g * n, g * n + n)
                        fill = fills.start[index] + s_fill(g, count)
                        v.wait_ge(filled, fill + 1)
                        nc.vector.tensor_tensor(KK[b2, pr, b2],
                                                ps[fill % BANKS][b2].rearrange("i (p j) -> i p j", p=n),
                                                KK[b2, pr, b2], ALU.add).then_inc(dve_emptied, 1)

                    v.wait_ge(dve_emptied, fills.emptied(fills.start[index], "dve"))
                    scale(0)
                    for g in range(count):
                        if g + 1 < count:
                            scale(g + 1)
                        update(g)

                for index, (kind, o, w) in enumerate(plan):
                    if kind == LEAF_IN:
                        leaf(index, o)
                    elif kind == LEAF_OUT:
                        leaf_out(index, o)
                    elif kind == SCHUR:
                        schur(index, o, w)

            @block.scalar
            def _(act):
                def empty(fill, dst, src):
                    act.wait_ge(filled, fill + 1)
                    nc.scalar.activation(dst, src, ACT.Copy).then_inc(act_emptied, 1)

                def reset_lanes():
                    nc.scalar.activation(M[:, :, W:], c.lane_ident[:], ACT.Copy).then_inc(lane_reset, 1)

                def leaf_in_(fill):
                    empty(fill, M[NP:, :, 0:W], ps[fill % BANKS][0:NP].rearrange("p (r x) -> p r x", x=W))

                def leaf_out(first, o):
                    for q in range(4):
                        fill, at = first + q, o + 8 * q
                        empty(fill, Tt[span(o, W), :, at:at + 8],
                              ps[fill % BANKS][0:W].rearrange("j (i p) -> j p i", i=8))
                    if leaf_number(o) + 1 < NW:
                        act.wait_ge(leaf_done, leaf_number(o) + 1)
                        reset_lanes()

                def turn_n(first, o):
                    for q in range(4):
                        fill, at = first + q, o + 8 * q
                        empty(fill, Tn[span(o, W), :, at:at + 8],
                              ps[fill % BANKS][0:W].rearrange("i (j p) -> i p j", j=8))

                def schur(first, o, w):
                    for g in range(groups_of(w)[1]):
                        fill = first + y_fill(g)
                        empty(fill, Y[g % 2][span(o, w)], ps[fill % BANKS][span(o, w)])

                def qv(n):
                    s = n % 2
                    act.wait_ge(q_made, n + 1)
                    if n > 1:
                        act.wait_ge(q_stored[s], 16 * (n // 2))
                        act.wait_ge(uq_done, n - 1)
                    nc.scalar.activation(qT[s][:], ps_q[:], ACT.Identity, bias=bq[:, 0:1]).then_inc(q_done, 1)
                    act.wait_ge(v_made, n + 1)
                    if n > 1:
                        act.wait_ge(v_done, n - 1)
                    nc.scalar.activation(v_raw[s][:], ps_v[:], ACT.Copy).then_inc(v_copied, 1)

                def block_out(first, w, at, dst):
                    n, count = groups_of(w)
                    for g in range(count):
                        fill = first + g
                        empty(fill, dst(slice(g * n, g * n + n)),
                              ps[fill % BANKS][at].rearrange("i (p j) -> i p j", p=n))

                reset_lanes()
                if first_time:
                    act.wait_ge(w_in, 64)
                for index, (kind, o, w) in enumerate(plan):
                    first, b1, b2 = fills.start[index], span(o, w), span(o + w, w)
                    if kind == LEAF_IN:
                        leaf_in_(first)
                    elif kind == QV:
                        for i in range(w):
                            qv(o + i)
                    elif kind == DOTS:
                        empty(first, m.uq[:, o * HC:(o + w) * HC], ps[first % BANKS][:, :w * HC])
                    elif kind == LEAF_OUT:
                        leaf_out(first, o)
                    elif kind == TURN_N:
                        turn_n(first, o)
                    elif kind == SCHUR:
                        schur(first, o, w)
                    elif kind == FIRST:
                        block_out(first, w, b2, lambda pr: YV[w][b2, pr])
                    elif kind == ROWS:
                        block_out(first, w, b2, lambda pr: Tn[b2, pr, b1])
                    else:
                        block_out(first, w, b1, lambda pr: Tt[b1, pr, b2])

            @block.tensor
            def _(pe):
                def free(fill):
                    last = fill - BANKS
                    if last >= 0:
                        user = fills.users[last]
                        pe.wait_ge(act_emptied if user == "act" else dve_emptied,
                                   fills.emptied(last + 1, user))
                    return ps[fill % BANKS]

                def all_emptied(first):
                    wait(pe, act_emptied, fills.emptied(first, "act"))
                    wait(pe, dve_emptied, fills.emptied(first, "dve"))

                def leaf_in_(first, o):
                    b = span(o, W)
                    pe.wait_ge(lane_reset, leaf_number(o) + 1)
                    to = free(first)
                    for j in range(RW):
                        i = nc.tensor.transpose(to[0:NP, j * W:(j + 1) * W], KK[b, :, o + 2 * j + 1], c.ident[b, b])
                    i.then_inc(filled, 1)
                    for j in range(RW):
                        i = nc.tensor.transpose(M[0:NP, j, 0:W], KK[b, :, o + 2 * j], c.ident[b, b])
                    i.then_inc(leaf_in, 1)

                def turn(fill, source, final=None):
                    to = free(fill)
                    for k in range(8):
                        if final:
                            pe.wait_ge(row_done, final(k))
                        i = nc.tensor.transpose(to[0:W, k * NP:(k + 1) * NP], source(k), c.ident[0:NP, 0:NP])
                    i.then_inc(filled, 1)

                def leaf_out(first, o):
                    r = leaf_number(o)
                    for q in range(4):
                        turn(first + q, lambda k: c.R[r % 2][0:NP, 8 * q + k, W:],
                             final=lambda k: W * r + 8 * q + k + 1)
                    to = free(first + 4)
                    pe.wait_ge(leaf_done, r + 1)
                    nc.tensor.transpose(to[0:W, 0:NP], dl[0:NP], c.ident[0:NP, 0:NP]).then_inc(filled, 1)

                def turn_n(first, o):
                    for q in range(4):
                        turn(first + q, lambda k: c.R[leaf_number(o) % 2][0:NP, :, W + 8 * q + k])

                def schur(index, first, o, w):
                    n, count = groups_of(w)
                    b1, b2 = span(o, w), span(o + w, w)

                    def reduce_right(g):
                        fill = first + y_fill(g)
                        to = free(fill)
                        for k in range(n):
                            p = g * n + k
                            i = nc.tensor.matmul(to[b1, k * w:(k + 1) * w], Tt[b1, p, b1], KK[b1, p, b2],
                                                 start=True, stop=True)
                        i.then_inc(filled, 1)

                    all_emptied(first)
                    reduce_right(0)
                    for g in range(count):
                        if g + 1 < count:
                            reduce_right(g + 1)
                        pe.wait_ge(act_emptied, fills.emptied(first + y_fill(g) + 1, "act"))
                        pe.wait_ge(yd_done, yds_before(index) + g + 1)
                        fill = first + s_fill(g, count)
                        to = free(fill)
                        for k in range(n):
                            i = nc.tensor.matmul(to[b2, k * w:(k + 1) * w], Y[g % 2][b1, k * w:(k + 1) * w],
                                                 YV[w][b1, g * n + k], start=True, stop=True)
                        i.then_inc(filled, 1)

                def qv(n):
                    s = n % 2
                    pe.wait_ge(a_in[s], 16 * (n // 2 + 1))
                    if n:
                        pe.wait_ge(q_done, n)
                    for d in range(DC):
                        i = nc.tensor.matmul(ps_q[:], wqv[:, d, 0], aT[s][:, :, d], start=(d == 0), stop=(d == DC - 1))
                    i.then_inc(q_made, 1)
                    if n:
                        pe.wait_ge(v_copied, n)
                    for j in range(HC):
                        for d in range(DC):
                            i = nc.tensor.matmul(ps_v[:, j], aT[s][:, j, d], wqv[:, d, 1],
                                                 start=(d == 0), stop=(d == DC - 1))
                    i.then_inc(v_made, 1)

                def dots(first, o, w):
                    to = free(first)
                    pe.wait_ge(uq_done, o + w)
                    for k in range(w):
                        for j in range(HC):
                            at = k * HC + j
                            i = nc.tensor.matmul(to[:, at:at + 1], uq[:, k, j], ones[:], start=True, stop=True)
                    i.then_inc(filled, 1)

                def products(first, w, at, left, right):
                    n, count = groups_of(w)
                    all_emptied(first)
                    for g in range(count):
                        to = free(first + g)
                        for k in range(n):
                            p = g * n + k
                            i = nc.tensor.matmul(to[at, k * w:(k + 1) * w], left(p), right(p), start=True, stop=True)
                        i.then_inc(filled, 1)

                if first_time:
                    pe.wait_ge(w_in, 64)
                    pe.wait_ge(ones_done, 1)
                for index, (kind, o, w) in enumerate(plan):
                    first, b1, b2 = fills.start[index], span(o, w), span(o + w, w)
                    if first_time and (kind, w) == (SCHUR, 2 * W):
                        pe.wait_ge(zeros, 2 * (NW - 1))
                    if kind == LEAF_IN:
                        all_emptied(first)
                        leaf_in_(first, o)
                    elif kind == QV:
                        for i in range(w):
                            qv(o + i)
                    elif kind == DOTS:
                        dots(first, o, w)
                    elif kind == LEAF_OUT:
                        leaf_out(first, o)
                    elif kind == TURN_N:
                        turn_n(first, o)
                    elif kind == SCHUR:
                        schur(index, first, o, w)
                    elif kind == FIRST:
                        products(first, w, b2, lambda p: YV[w][b1, p], lambda p: Tn[b1, p, b1])
                    elif kind == ROWS:
                        products(first, w, b2, lambda p: Tt[b2, p, b2], lambda p: YV[w][b2, p])
                    else:
                        products(first, w, b1, lambda p: YV[w][b2, p], lambda p: Tt[b2, p, b2])


def gram(nc, m, c):
    uT_v, UA_v = (y.rearrange("(g k) i j -> g i k j", k=GROUP) for y in (m.uT, m.UA))
    with ExitStack() as ctx:
        def sb(what, shape, dt=F32):
            return ctx.enter_context(nc.sbuf_tensor(f"gram_{what}", shape, dt))

        def psum(what):
            return [ctx.enter_context(nc.psum_tensor(f"gram_{what}{i}", [P, GROUP, P], F32)) for i in range(2)]

        def sem(what):
            return ctx.enter_context(nc.semaphore(f"gram_{what}"))

        group = [P, GROUP, P]
        uTa, uTb, Td, A, WW, UA = ([sb(f"{x}{s}", group) for s in range(2)]
                                   for x in ("uT_for_w", "uT_for_g", "Td", "A", "W", "UA"))
        ps_a, ps_w, ps_g, ps_u = (psum(x) for x in ("ps_a", "ps_w", "ps_g", "ps_u"))
        ua_in = [sem(f"uT_for_w_in{s}") for s in range(2)]
        ub_in = [sem(f"uT_for_g_in{s}") for s in range(2)]
        td_done, a_done, A_done, w_done, W_done, g_done, kk_done, u_done, UA_done = (
            sem(x) for x in ("td_done", "a_product", "A_done", "w_product", "W_done", "g_product", "kk_done",
                             "u_turned", "UA_done"))
        stored = [sem(f"stored{s}") for s in range(2)]

        with nc.Block() as block:
            @block.sync
            def _(sp):
                def load_a(st):
                    if not (isinstance(st.n, int) and st.n < 2):
                        wait(sp, w_done, st.n - 1)
                    sp.dma_start(uTa[st.s][:], uT_v[st.n]).then_inc(ua_in[st.s], 16)

                def load_b(st):
                    if not (isinstance(st.n, int) and st.n < 2):
                        wait(sp, g_done, st.n - 1)
                    sp.dma_start(uTb[st.s][:], uT_v[st.n]).then_inc(ub_in[st.s], 16)

                def step(st):
                    if not is_last(st, NG):
                        load_a(st.later(1))
                        load_b(st.later(1))

                load_a(Step(0, 0))
                load_b(Step(0, 0))
                steps(sp, NG, step)

            @block.vector
            def _(v):
                def scale(st):
                    if not is_first(st):
                        wait(v, a_done, st.n - 1)
                    nc.vector.tensor_tensor(Td[st.s][:], m.Tn[:, bass.ds(st.n * GROUP, GROUP), :],
                                            m.dinv[:, bass.ds(st.n * GROUP, GROUP)].unsqueeze(2).to_broadcast(group),
                                            ALU.mult).then_inc(td_done, 1)

                def copy_w(st):
                    v.wait_ge(w_done, st.n + 1)
                    if not is_first(st):
                        wait(v, g_done, st.n - 1)
                        wait(v, u_done, st.n - 1)
                    nc.vector.tensor_copy(WW[st.s][:], ps_w[st.s][:]).then_inc(W_done, 1)

                def add_identity(st):
                    v.wait_ge(g_done, st.n + 1)
                    nc.vector.tensor_tensor(m.KK[:, bass.ds(st.n * GROUP, GROUP), :], ps_g[st.s][:],
                                            c.ident[:].unsqueeze(1).to_broadcast(group),
                                            ALU.add).then_inc(kk_done, 1)

                def step(st):
                    if not isinstance(st.n, int) or st.n + 2 < NG:
                        scale(st.later(2))
                    copy_w(st)
                    if not is_first(st):
                        add_identity(st.later(-1))

                scale(Step(0, 0))
                scale(Step(0, 1))
                steps(v, NG, step, tail=3)
                add_identity(Step(NG // 2 - 1, 1))

            @block.scalar
            def _(act):
                def copy_a(st):
                    act.wait_ge(a_done, st.n + 1)
                    if not is_first(st):
                        wait(act, w_done, st.n - 1)
                    nc.scalar.activation(A[st.s][:], ps_a[st.s][:], ACT.Copy).then_inc(A_done, 1)

                def copy_ua(st):
                    act.wait_ge(u_done, st.n + 1)
                    wait(act, stored[st.s], 16 * st.pair)
                    nc.scalar.activation(UA[st.s][:], ps_u[st.s][:], ACT.Copy).then_inc(UA_done, 1)

                def store(st):
                    act.wait_ge(UA_done, st.n + 1)
                    act.dma_start(UA_v[st.n], UA[st.s][:]).then_inc(stored[st.s], 16)

                def step(st):
                    if not is_last(st, NG):
                        copy_a(st.later(1))
                    if not is_first(st):
                        copy_ua(st.later(-1))
                        store(st.later(-1))

                copy_a(Step(0, 0))
                steps(act, NG, step)
                copy_ua(Step(NG // 2 - 1, 1))
                store(Step(NG // 2 - 1, 1))
                for s in range(2):
                    act.wait_ge(stored[s], 16 * NG // 2)

            @block.tensor
            def _(pe):
                def inverse(st):
                    pe.wait_ge(td_done, st.n + 1)
                    if not is_first(st):
                        wait(pe, A_done, st.n - 1)
                    for k in range(GROUP):
                        i = nc.tensor.matmul(ps_a[st.s][:, k], Td[st.s][:, k], m.Tn[:, bass.ds(st.n * GROUP + k, 1), :],
                                             start=True, stop=True)
                    i.then_inc(a_done, 1)

                def times_u(st):
                    pe.wait_ge(ua_in[st.s], 16 * (st.pair + 1))
                    pe.wait_ge(A_done, st.n + 1)
                    if not is_first(st):
                        wait(pe, W_done, st.n - 1)
                    for k in range(GROUP):
                        i = nc.tensor.matmul(ps_w[st.s][:, k], A[st.s][:, k], uTa[st.s][:, k], start=True, stop=True)
                    i.then_inc(w_done, 1)

                def products(st):
                    pe.wait_ge(ub_in[st.s], 16 * (st.pair + 1))
                    pe.wait_ge(W_done, st.n + 1)
                    if not is_first(st):
                        wait(pe, kk_done, st.n - 1)
                        wait(pe, UA_done, st.n - 1)
                    for k in range(GROUP):
                        i = nc.tensor.matmul(ps_g[st.s][:, k], uTb[st.s][:, k], WW[st.s][:, k], start=True, stop=True)
                    i.then_inc(g_done, 1)
                    for k in range(GROUP):
                        i = nc.tensor.transpose(ps_u[st.s][:, k], WW[st.s][:, k], c.ident[:])
                    i.then_inc(u_done, 1)

                def step(st):
                    if not is_last(st, NG):
                        inverse(st.later(1))
                    times_u(st)
                    if not is_first(st):
                        products(st.later(-1))

                inverse(Step(0, 0))
                steps(pe, NG, step)
                products(Step(NG // 2 - 1, 1))


def outputs(nc, x1, x2, m, c, a):
    x_v, o_v = (y.rearrange("(b c t) d -> c t b d", b=BATCH, t=P) for y in (x1, x2))
    UA_v, qT_v, v_v = (y.rearrange("(g k) i j -> g i k j", k=GROUP) for y in (m.UA, m.qT, m.v))
    with ExitStack() as ctx:
        def sb(what, shape, dt=F32):
            return ctx.enter_context(nc.sbuf_tensor(f"out_{what}", shape, dt))

        def psum(what, shape):
            return ctx.enter_context(nc.psum_tensor(f"out_{what}", shape, F32))

        def sem(what):
            return ctx.enter_context(nc.semaphore(f"out_{what}"))

        group = [P, GROUP, P]
        wide = [P, GROUP, D]
        UA, qT, v0, vd, zT, zn, sc, oT, M = ([sb(f"{x}{s}", group) for s in range(2)]
                                             for x in ("UA", "qT", "v", "v_over_d", "zT", "z", "scores", "oT", "M"))
        x, xb, xo = ([sb(f"{y}{s}", wide) for s in range(2)] for y in ("x", "x_plus_bias", "x_out"))
        s_all, s_over_d = sb("s", [P, NP]), sb("s_over_d", [P, NP])
        dcol = [sb(f"dcol{s}", [P, GROUP]) for s in range(2)]
        wo = sb("wo", [P, D])
        bo = sb("bo", [P, D])
        ps_z, ps_s, ps_n, ps_o, ps_m = (psum(y, group) for y in ("ps_z", "ps_s", "ps_n", "ps_o", "ps_m"))
        ps_r = psum("ps_r", wide)
        w_in = sem("w_in")
        UA_in, q_in, v_in, x_in, stored = ([sem(f"{y}{s}") for s in range(2)]
                                           for y in ("UA_in", "q_in", "v_in", "x_in", "stored"))
        s_done_all = sem("s_done")
        (M_zero, dcol_done, vd_done, xb_done, z_done, zT_done, s_done, sc_done, n_done, zn_done, o_done, oT_done,
         m_done, M_done, r_done, xo_done) = (
            sem(y) for y in ("M_zero", "dcol_done", "vd_done", "xb_done", "z_product", "zT_done", "s_product",
                             "sc_done", "z_turned", "zn_done", "o_product", "oT_done", "m_product", "M_done",
                             "r_product", "xo_done"))

        with nc.Block() as block:
            @block.sync
            def _(sp):
                def load(st, tiles, src, landed, used):
                    if not (isinstance(st.n, int) and st.n < 2):
                        wait(sp, used, st.n - 1)
                    sp.dma_start(tiles[st.s][:], src).then_inc(landed[st.s], 16)

                def load_ua(st):
                    load(st, UA, UA_v[st.n], UA_in, z_done)

                def load_rest(st):
                    load(st, qT, qT_v[st.n], q_in, o_done)
                    load(st, v0, v_v[st.n], v_in, vd_done)
                    load(st, x, x_v[st.pair, :, GROUP * st.s:GROUP * st.s + GROUP], x_in, xb_done)

                def step(st):
                    if not is_last(st, NG):
                        load_rest(st.later(1))
                    if not isinstance(st.n, int) or st.n + 2 < NG:
                        load_ua(st.later(2))

                load_ua(Step(0, 0))
                load_ua(Step(0, 1))
                load_rest(Step(0, 0))
                sp.dma_start(bo[:], a["bo"].partition_broadcast(P)).then_inc(w_in, 16)
                sp.dma_start(wo[:], a["WoT"]).then_inc(w_in, 16)
                steps(sp, NG, step, tail=3)

            @block.gpsimd
            def _(pool):
                def scale_v(st):
                    pool.wait_ge(v_in[st.s], 16 * (st.pair + 1))
                    pool.wait_ge(dcol_done, st.n + 1)
                    if not is_first(st):
                        wait(pool, m_done, st.n - 1)
                    nc.gpsimd.tensor_tensor(vd[st.s][:], v0[st.s][:], dcol[st.s][:].unsqueeze(2).to_broadcast(group),
                                            ALU.mult).then_inc(vd_done, 1)

                def add_bias(st):
                    pool.wait_ge(x_in[st.s], 16 * (st.pair + 1))
                    if not is_first(st):
                        wait(pool, xo_done, st.n - 1)
                    nc.gpsimd.tensor_tensor(xb[st.s][:], x[st.s][:], bo[:].unsqueeze(1).to_broadcast(wide),
                                            ALU.add).then_inc(xb_done, 1)

                def step(st):
                    if not is_last(st, NG):
                        scale_v(st.later(1))
                    add_bias(st)

                scale_v(Step(0, 0))
                pool.wait_ge(w_in, 32)
                steps(pool, NG, step)

            @block.vector
            def _(v):
                def pick_d(st):
                    if not is_first(st):
                        wait(v, vd_done, st.n - 1)
                    nc.vector.tensor_copy(dcol[st.s][:], s_over_d[:, bass.ds(st.n * GROUP, GROUP)]
                                          ).then_inc(dcol_done, 1)

                def mask(st):
                    v.wait_ge(s_done, st.n + 1)
                    if not is_first(st):
                        wait(v, o_done, st.n - 1)
                    nc.vector.tensor_tensor(sc[st.s][:], ps_s[:], c.causal[:].unsqueeze(1).to_broadcast(group),
                                            ALU.mult).then_inc(sc_done, 1)

                def update(st):
                    v.wait_ge(m_done, st.n + 1)
                    nc.vector.tensor_tensor(M[st.s][:], ps_m[:], M[st.s][:], ALU.add).then_inc(M_done, 1)

                def residual(st):
                    v.wait_ge(r_done, st.n + 1)
                    v.wait_ge(xb_done, st.n + 1)
                    wait(v, stored[st.s], 16 * st.pair)
                    nc.vector.tensor_tensor(xo[st.s][:], ps_r[:], xb[st.s][:], ALU.add).then_inc(xo_done, 1)

                def step(st):
                    if not is_last(st, NG):
                        pick_d(st.later(1))
                    mask(st)
                    if not is_first(st):
                        residual(st.later(-1))
                    update(st)

                nc.vector.tensor_tensor(s_all[:], m.knorm[:], m.uq[:], ALU.mult).then_inc(s_done_all, 1)
                v.wait_ge(s_done_all, 1)
                nc.vector.tensor_tensor(s_over_d[:].rearrange("p (c b) -> p b c", b=BATCH),
                                        s_all[:].rearrange("p (b c) -> p b c", b=BATCH),
                                        m.dinv[:].rearrange("p (c b) -> p b c", b=BATCH),
                                        ALU.mult).then_inc(s_done_all, 1)
                v.wait_ge(s_done_all, 2)
                for s in range(2):
                    nc.vector.memset(M[s][:], 0.0).then_inc(M_zero, 1)
                v.wait_ge(M_zero, 2)
                pick_d(Step(0, 0))
                steps(v, NG, step)
                residual(Step(NG // 2 - 1, 1))

            @block.scalar
            def _(act):
                def copy(st, dst, src, made, used, done):
                    act.wait_ge(made, st.n + 1)
                    if not is_first(st):
                        wait(act, used, st.n - 1)
                    nc.scalar.activation(dst[st.s][:], src[:], ACT.Copy).then_inc(done, 1)

                def store(st):
                    act.wait_ge(xo_done, st.n + 1)
                    act.dma_start(o_v[st.pair, :, GROUP * st.s:GROUP * st.s + GROUP], xo[st.s][:]
                                  ).then_inc(stored[st.s], 16)

                def step(st):
                    if not is_last(st, NG):
                        copy(st.later(1), zT, ps_z, z_done, n_done, zT_done)
                    copy(st, zn, ps_n, n_done, m_done, zn_done)
                    if not is_first(st):
                        store(st.later(-1))
                    copy(st, oT, ps_o, o_done, r_done, oT_done)

                copy(Step(0, 0), zT, ps_z, z_done, n_done, zT_done)
                steps(act, NG, step)
                store(Step(NG // 2 - 1, 1))
                for s in range(2):
                    act.wait_ge(stored[s], 16 * NG // 2)

            @block.tensor
            def _(pe):
                def z_product(st):
                    pe.wait_ge(UA_in[st.s], 16 * (st.pair + 1))
                    wait(pe, zT_done, st.n)
                    for k in range(GROUP):
                        i = nc.tensor.matmul(ps_z[:, k], UA[st.s][:, k], m.Tt[:, bass.ds(st.n * GROUP + k, 1), :],
                                             start=True, stop=True)
                    i.then_inc(z_done, 1)

                def scores(st):
                    pe.wait_ge(zT_done, st.n + 1)
                    pe.wait_ge(q_in[st.s], 16 * (st.pair + 1))
                    wait(pe, sc_done, st.n)
                    for k in range(GROUP):
                        i = nc.tensor.matmul(ps_s[:, k], zT[st.s][:, k], qT[st.s][:, k], start=True, stop=True)
                    i.then_inc(s_done, 1)
                    wait(pe, zn_done, st.n)
                    for k in range(GROUP):
                        i = nc.tensor.transpose(ps_n[:, k], zT[st.s][:, k], c.ident[:])
                    i.then_inc(n_done, 1)

                def attend(st):
                    pe.wait_ge(sc_done, st.n + 1)
                    pe.wait_ge(vd_done, st.n + 1)
                    wait(pe, oT_done, st.n)
                    if is_first(st):
                        pe.wait_ge(M_zero, 2)
                    else:
                        wait(pe, M_done, st.n - 1)
                    for k in range(GROUP):
                        nc.tensor.matmul(ps_o[:, k], vd[st.s][:, k], sc[st.s][:, k], start=True, stop=False)
                        i = nc.tensor.matmul(ps_o[:, k], M[st.s][:, k], qT[st.s][:, k], start=False, stop=True)
                    i.then_inc(o_done, 1)
                    pe.wait_ge(zn_done, st.n + 1)
                    wait(pe, M_done, st.n)
                    for k in range(GROUP):
                        i = nc.tensor.matmul(ps_m[:, k], zn[st.s][:, k], vd[st.s][:, k], start=True, stop=True)
                    i.then_inc(m_done, 1)

                def project_out(st):
                    if is_first(st):
                        pe.wait_ge(w_in, 32)
                    pe.wait_ge(oT_done, st.n + 1)
                    wait(pe, xo_done, st.n)
                    for k in range(GROUP):
                        i = nc.tensor.matmul(ps_r[:, k], oT[st.s][:, k], wo[:], start=True, stop=True)
                    i.then_inc(r_done, 1)

                def step(st):
                    if not is_last(st, NG):
                        z_product(st.later(1))
                    scores(st)
                    if not is_first(st):
                        project_out(st.later(-1))
                    attend(st)

                z_product(Step(0, 0))
                steps(pe, NG, step)
                project_out(Step(NG // 2 - 1, 1))


class Names:
    pass


def macaron(nc, a, out):
    def dram(name, shape):
        return nc.dram_tensor(name, shape, F32, kind="Internal").ap()

    x1, x2 = dram("x1_scratch", (TOKENS, D)), dram("x2_scratch", (TOKENS, D))
    m = Names()
    m.qT, m.uT, m.v, m.UA = (dram(f"{n}_scratch", (NP, P, P)) for n in ("qT", "uT", "v", "UA"))
    m.aT = dram("aT_scratch", (NSTEP, P, HC, DC, P))
    with ExitStack() as ctx:
        c = Names()
        constants(nc, ctx, c)
        feed_forward(nc, "ffn1", a["x"], x1, c, a)
        with ExitStack() as own:
            m.KK, m.Tn, m.Tt = (own.enter_context(nc.sbuf_tensor(n, [P, NP, P], F32)) for n in ("KK", "Tn", "Tt"))
            m.dinv, m.ndinv = (own.enter_context(nc.sbuf_tensor(n, [P, NP], F32)) for n in ("dinv", "minus_dinv"))
            m.knorm, m.uq = (own.enter_context(nc.sbuf_tensor(n, [P, NP], F32)) for n in ("k_norms", "u_dot_q"))
            keys(nc, x1, m, c, a)
            factorise(nc, "inv", "rows", m, c, a)
            gram(nc, m, c)
            factorise(nc, "ldl", "columns", m, c)
            outputs(nc, x1, x2, m, c, a)
        feed_forward(nc, "ffn2", x2, out, c)


def kernel(**inputs):
    import numpy as np
    import concourse.bacc as bacc
    from concourse import mybir as _mybir
    from concourse.bass_utils import run_bass_kernel_spmd

    g = {k.replace("L0_", ""): np.asarray(v) for k, v in inputs.items()}
    laid = {
        "x": g["attn_x"].reshape(TOKENS, D),
        "W1T": g["ffn_W1"].T,
        "W2T": g["ffn_W2"].T,
        "b1": g["ffn_b1"].reshape(FC, P).T,
        "b2": g["ffn_b2"],
        "WqkvT": np.concatenate([g["attn_Wq"].T, g["attn_Wk"].T, g["attn_Wv"].T], axis=1),
        "bqkv": np.concatenate([g["attn_bq"], g["attn_bk"], g["attn_bv"]]),
        "WoT": g["attn_Wo"].T,
        "bo": g["attn_bo"],
    }
    nc = bacc.Bacc("TRN2", target_bir_lowering=False, num_devices=1)
    arrays, aps = {}, {}
    for k, v in laid.items():
        arrays[f"in_{k}"] = np.ascontiguousarray(v)
        aps[k] = nc.dram_tensor(f"in_{k}", v.shape, _mybir.dt.from_np(v.dtype), kind="ExternalInput").ap()
    out = nc.dram_tensor("out_x", (TOKENS, D), F32, kind="ExternalOutput").ap()
    macaron(nc, aps, out)
    r = run_bass_kernel_spmd(nc, [arrays], core_ids=[0])
    return r.results[0]["out_x"].reshape(BATCH, T, D)
```
